# Optimizing a Trainium2 kernel written in Bass

```python
import numpy as np
import jax
import jax.numpy as jnp

def _softmax(x, axis=-1):
    return jax.nn.softmax(x, axis=axis)

def _gelu(x):
    return jax.nn.gelu(x, approximate=True)

def _silu(x):
    return jax.nn.silu(x)

def _sigmoid(x):
    return jax.nn.sigmoid(x)

def _layernorm(x, axis=-1, eps=1e-05):
    m = jnp.mean(x, axis=axis, keepdims=True)
    v = jnp.var(x, axis=axis, keepdims=True)
    return (x - m) / jnp.sqrt(v + eps)

def _scatter_add(tgt, idx, src, axis=0):
    return tgt.at[idx].add(src)

def _segment_sum(src, seg, n):
    return jax.ops.segment_sum(src, seg, n)
kernel_name = 'mk_flamingo_gated_d2_seqx_r4_39e561'

def setup_inputs(seed: int=0):
    np.random.seed(seed)
    _w = jnp.asarray

    def _rec_inputs():
        import jax
        import jax.numpy as jnp
        _rk = jax.random.key(seed)
        x = 7.22e-05 + 1 * jax.random.normal(jax.random.fold_in(_rk, 1), (16, 112, 512), jnp.float32)
        _lenS = 112 - jax.random.randint(jax.random.fold_in(_rk, 7), (16,), 0, max(1, 112 // 4) + 1, jnp.int32)
        _lenS2 = 375 - jax.random.randint(jax.random.fold_in(_rk, 8), (16,), 0, max(1, 375 // 4) + 1, jnp.int32)
        _ctx_2048P = jax.random.normal(jax.random.fold_in(_rk, 11), (16, 16, 512), jnp.float32)
        _ctx_2048c = jax.random.dirichlet(jax.random.fold_in(_rk, 511), 0.3 * jnp.ones((16,), jnp.float32), (16, 375))
        _ctx_2048t = jnp.einsum('bsk,bkd->bsd', _ctx_2048c, _ctx_2048P)
        _ctx_2048t = _ctx_2048t * jax.lax.rsqrt(jnp.mean(jnp.square(_ctx_2048t)) + 1e-12) * 0.953939
        ctx_2048 = 4.13588e-05 + 0.999923 * (_ctx_2048t + 0.3 * jax.random.normal(jax.random.fold_in(_rk, 611), (16, 375, 512), jnp.float32))
        _g = jax.random.normal(jax.random.fold_in(_rk, 9001), (2, 2), jnp.float32)
        _g = jnp.sign(_g) * jnp.maximum(jnp.abs(_g), 1.0) + (_g == 0) * 1.0
        g_xattn = _g[0]
        g_ffn = _g[1]
        return (x, ctx_2048, g_xattn, g_ffn)
    x, ctx_2048, g_xattn, g_ffn = _rec_inputs()

    def _L0_xattn_setup():
        import math
        import jax, jax.numpy as jnp
        import numpy as np
        HEADS = 16
        MASKED_BIAS = -10000.0

        def _mha(q, k, v):
            B, Sq, D = q.shape
            Sk = k.shape[-2]
            hd = D // HEADS
            qh = q.reshape(B, Sq, HEADS, hd).transpose(0, 2, 1, 3)
            kh = k.reshape(B, Sk, HEADS, hd).transpose(0, 2, 1, 3)
            vh = v.reshape(B, Sk, HEADS, hd).transpose(0, 2, 1, 3)
            scores = jnp.einsum('bhqd,bhkd->bhqk', qh, kh) / math.sqrt(hd)
            qi = jnp.arange(Sq)[:, None] + (Sk - Sq)
            ki = jnp.arange(Sk)[None, :]
            causal = ki <= qi
            scores = jnp.where(causal[None, None], scores, jnp.asarray(MASKED_BIAS, scores.dtype))
            attn = jax.nn.softmax(scores, axis=-1)
            out = jnp.einsum('bhqk,bhkd->bhqd', attn, vh)
            return out.transpose(0, 2, 1, 3).reshape(B, Sq, D)
        key = jax.random.key(seed)
        kq, kk, kv = jax.random.split(key, 3)
        B, S, D = (4, 256, 512)
        q = jax.random.normal(kq, (B, S, D), dtype=jnp.float32)
        k = jax.random.normal(kk, (B, S, D), dtype=jnp.float32)
        v = jax.random.normal(kv, (B, S, D), dtype=jnp.float32)
        return {'q': q, 'k': k, 'v': v}
    _L0_xattn_all = _L0_xattn_setup()
    _L0_xattn_in = {k: v for k, v in _L0_xattn_all.items() if k in ()}
    del _L0_xattn_all

    def _L0_ffn_setup():
        import jax, jax.numpy as jnp
        import numpy as np
        HIDDEN = 512
        INTER = 2048
        SCALE = 64.0

        def fwht(x):
            orig_shape = x.shape
            n = orig_shape[-1]
            x = x.reshape(-1, n)
            h = 1
            while h < n:
                x = x.reshape(-1, n // (2 * h), 2, h)
                a, b = (x[:, :, 0, :], x[:, :, 1, :])
                x = jnp.stack([a + b, a - b], axis=2).reshape(-1, n)
                h *= 2
            return (x / jnp.sqrt(jnp.asarray(n, x.dtype))).reshape(orig_shape)
        key = jax.random.key(seed)
        ks = jax.random.split(key, 8)
        inp = jax.random.normal(ks[0], (4, 512, HIDDEN), dtype=jnp.float32)
        SU_ug = jnp.where(jax.random.bernoulli(ks[1], 0.5, (HIDDEN,)), 1.0, -1.0).astype(jnp.float32)
        SU_dp = jnp.where(jax.random.bernoulli(ks[2], 0.5, (INTER,)), 1.0, -1.0).astype(jnp.float32)
        Wscale_ug = jax.random.uniform(ks[3], (2 * INTER,), jnp.float32, 0.5, 1.5)
        Wscale_dp = jax.random.uniform(ks[4], (HIDDEN,), jnp.float32, 0.5, 1.5)
        W_up = jax.random.normal(ks[5], (INTER, HIDDEN), dtype=jnp.float32) * 0.02
        W_gate = jax.random.normal(ks[6], (INTER, HIDDEN), dtype=jnp.float32) * 0.02
        W_down = jax.random.normal(ks[7], (HIDDEN, INTER), dtype=jnp.float32) * 0.02
        return {'input': inp, 'SU_ug': SU_ug, 'SU_dp': SU_dp, 'Wscale_ug': Wscale_ug, 'Wscale_dp': Wscale_dp, 'W_up': W_up, 'W_gate': W_gate, 'W_down': W_down}
    _L0_ffn_all = _L0_ffn_setup()
    _L0_ffn_in = {k: v for k, v in _L0_ffn_all.items() if k in ('SU_ug', 'SU_dp', 'Wscale_ug', 'Wscale_dp', 'W_up', 'W_gate', 'W_down')}
    del _L0_ffn_all

    def _L1_xattn_setup():
        import jax, jax.numpy as jnp
        import numpy as np
        HIDDEN = 512
        N_HEADS = 16
        N_KV_HEADS = 4
        HEAD_DIM = 128
        EPS = 1e-06

        def rms_norm(x, w, eps=EPS):
            xf = x.astype(jnp.float32)
            var = jnp.mean(xf * xf, axis=-1, keepdims=True)
            return w * (xf * jax.lax.rsqrt(var + eps)).astype(x.dtype)
        key = jax.random.key(seed)
        ks = jax.random.split(key, 8)
        B, S, S_ENC = (4, 512, 256)
        inner = N_HEADS * HEAD_DIM
        kv_dim = N_KV_HEADS * HEAD_DIM
        s = 0.02
        return {'hidden_states': jax.random.normal(ks[0], (B, S, HIDDEN), jnp.float32), 'encoder_hidden_states': jax.random.normal(ks[1], (B, S_ENC, HIDDEN), jnp.float32), 'Wq': jax.random.normal(ks[2], (HIDDEN, inner), jnp.float32) * s, 'Wk': jax.random.normal(ks[3], (HIDDEN, kv_dim), jnp.float32) * s, 'Wv': jax.random.normal(ks[4], (HIDDEN, kv_dim), jnp.float32) * s, 'Wo': jax.random.normal(ks[5], (inner, HIDDEN), jnp.float32) * s, 'q_norm_w': jnp.ones((HEAD_DIM,), jnp.float32), 'k_norm_w': jnp.ones((HEAD_DIM,), jnp.float32)}
    _L1_xattn_all = _L1_xattn_setup()
    _L1_xattn_in = {k: v for k, v in _L1_xattn_all.items() if k in ('Wq', 'Wk', 'Wv', 'Wo', 'q_norm_w', 'k_norm_w')}
    del _L1_xattn_all

    def _L1_ffn_setup():
        import jax, jax.numpy as jnp
        import numpy as np
        N_HEAD = 16
        N_EMBD = 512
        R = 8
        HEAD_DIM = N_EMBD // N_HEAD
        D_STD = HEAD_DIM - R
        THRESHOLD = 0.1
        B, T = (4, 256)
        key = jax.random.key(seed)
        k1, k2, k3, k4, k5 = jax.random.split(key, 5)
        fused_dim = 2 * N_HEAD * D_STD + N_EMBD + 2 * N_HEAD * R
        x = jax.random.normal(k1, (B, T, N_EMBD), dtype=jnp.float32)
        Wa = jax.random.normal(k2, (N_EMBD, fused_dim), dtype=jnp.float32) * 0.02
        Wp = jax.random.normal(k3, (N_EMBD, N_EMBD), dtype=jnp.float32) * 0.02
        w_std = jax.random.uniform(k4, (N_HEAD,), dtype=jnp.float32, minval=0.3, maxval=0.7)
        w_rec = jax.random.uniform(k5, (N_HEAD,), dtype=jnp.float32)
        return {'x': x, 'Wa': Wa, 'Wp': Wp, 'w_std': w_std, 'w_rec': w_rec}
    _L1_ffn_all = _L1_ffn_setup()
    _L1_ffn_in = {k: v for k, v in _L1_ffn_all.items() if k in ('Wa', 'Wp', 'w_std', 'w_rec')}
    del _L1_ffn_all
    return {'x': x, 'ctx_2048': ctx_2048, 'g_xattn': g_xattn, 'g_ffn': g_ffn, 'L0_ffn_SU_ug': _L0_ffn_in['SU_ug'], 'L0_ffn_SU_dp': _L0_ffn_in['SU_dp'], 'L0_ffn_Wscale_ug': _L0_ffn_in['Wscale_ug'], 'L0_ffn_Wscale_dp': _L0_ffn_in['Wscale_dp'], 'L0_ffn_W_up': _L0_ffn_in['W_up'], 'L0_ffn_W_gate': _L0_ffn_in['W_gate'], 'L0_ffn_W_down': _L0_ffn_in['W_down'], 'L1_xattn_Wq': _L1_xattn_in['Wq'], 'L1_xattn_Wk': _L1_xattn_in['Wk'], 'L1_xattn_Wv': _L1_xattn_in['Wv'], 'L1_xattn_Wo': _L1_xattn_in['Wo'], 'L1_xattn_q_norm_w': _L1_xattn_in['q_norm_w'], 'L1_xattn_k_norm_w': _L1_xattn_in['k_norm_w'], 'L1_ffn_Wa': _L1_ffn_in['Wa'], 'L1_ffn_Wp': _L1_ffn_in['Wp'], 'L1_ffn_w_std': _L1_ffn_in['w_std'], 'L1_ffn_w_rec': _L1_ffn_in['w_rec']}

def reference(x, ctx_2048, g_xattn, g_ffn, L0_ffn_SU_ug, L0_ffn_SU_dp, L0_ffn_Wscale_ug, L0_ffn_Wscale_dp, L0_ffn_W_up, L0_ffn_W_gate, L0_ffn_W_down, L1_xattn_Wq, L1_xattn_Wk, L1_xattn_Wv, L1_xattn_Wo, L1_xattn_q_norm_w, L1_xattn_k_norm_w, L1_ffn_Wa, L1_ffn_Wp, L1_ffn_w_std, L1_ffn_w_rec):
    import jax
    import jax.numpy as jnp

    def _L0_xattn_ref(q, k, v):
        import math
        import jax, jax.numpy as jnp
        import numpy as np
        HEADS = 16
        MASKED_BIAS = -10000.0

        def _mha(q, k, v):
            B, Sq, D = q.shape
            Sk = k.shape[-2]
            hd = D // HEADS
            qh = q.reshape(B, Sq, HEADS, hd).transpose(0, 2, 1, 3)
            kh = k.reshape(B, Sk, HEADS, hd).transpose(0, 2, 1, 3)
            vh = v.reshape(B, Sk, HEADS, hd).transpose(0, 2, 1, 3)
            scores = jnp.einsum('bhqd,bhkd->bhqk', qh, kh) / math.sqrt(hd)
            qi = jnp.arange(Sq)[:, None] + (Sk - Sq)
            ki = jnp.arange(Sk)[None, :]
            causal = ki <= qi
            scores = jnp.where(causal[None, None], scores, jnp.asarray(MASKED_BIAS, scores.dtype))
            attn = jax.nn.softmax(scores, axis=-1)
            out = jnp.einsum('bhqk,bhkd->bhqd', attn, vh)
            return out.transpose(0, 2, 1, 3).reshape(B, Sq, D)
        return _mha(q, k, v)

    def _L0_ffn_ref(input, SU_ug, SU_dp, Wscale_ug, Wscale_dp, W_up, W_gate, W_down):
        import jax, jax.numpy as jnp
        import numpy as np
        HIDDEN = 512
        INTER = 2048
        SCALE = 64.0

        def fwht(x):
            orig_shape = x.shape
            n = orig_shape[-1]
            x = x.reshape(-1, n)
            h = 1
            while h < n:
                x = x.reshape(-1, n // (2 * h), 2, h)
                a, b = (x[:, :, 0, :], x[:, :, 1, :])
                x = jnp.stack([a + b, a - b], axis=2).reshape(-1, n)
                h *= 2
            return (x / jnp.sqrt(jnp.asarray(n, x.dtype))).reshape(orig_shape)
        n = SU_ug.shape[0]
        x = input.reshape(-1, n)
        x = fwht(x * SU_ug) / SCALE
        x_up = x @ W_up.T * (Wscale_ug[:INTER] * SCALE)
        x_gate = x @ W_gate.T * (Wscale_ug[INTER:] * SCALE)
        x = jax.nn.silu(x_gate) * x_up
        x = fwht(x * SU_dp) / SCALE
        x = x @ W_down.T * (Wscale_dp * SCALE)
        return x.reshape(input.shape)

    def _L1_xattn_ref(hidden_states, encoder_hidden_states, Wq, Wk, Wv, Wo, q_norm_w, k_norm_w):
        import jax, jax.numpy as jnp
        import numpy as np
        HIDDEN = 512
        N_HEADS = 16
        N_KV_HEADS = 4
        HEAD_DIM = 128
        EPS = 1e-06

        def rms_norm(x, w, eps=EPS):
            xf = x.astype(jnp.float32)
            var = jnp.mean(xf * xf, axis=-1, keepdims=True)
            return w * (xf * jax.lax.rsqrt(var + eps)).astype(x.dtype)
        B, S, _ = hidden_states.shape
        S_enc = encoder_hidden_states.shape[1]
        groups = N_HEADS // N_KV_HEADS
        scale = 1.0 / HEAD_DIM ** 0.5
        q = (hidden_states @ Wq).reshape(B, S, N_HEADS, HEAD_DIM)
        k = (encoder_hidden_states @ Wk).reshape(B, S_enc, N_KV_HEADS, HEAD_DIM)
        v = (encoder_hidden_states @ Wv).reshape(B, S_enc, N_KV_HEADS, HEAD_DIM)
        q = rms_norm(q, q_norm_w)
        k = rms_norm(k, k_norm_w)
        k = jnp.repeat(k, groups, axis=2)
        v = jnp.repeat(v, groups, axis=2)
        scores = jnp.einsum('bqhd,bkhd->bhqk', q, k) * scale
        probs = jax.nn.softmax(scores, axis=-1)
        out = jnp.einsum('bhqk,bkhd->bqhd', probs, v)
        out = out.reshape(B, S, N_HEADS * HEAD_DIM)
        return out @ Wo

    def _L1_ffn_ref(x, Wa, Wp, w_std, w_rec):
        import jax, jax.numpy as jnp
        import numpy as np
        N_HEAD = 16
        N_EMBD = 512
        R = 8
        HEAD_DIM = N_EMBD // N_HEAD
        D_STD = HEAD_DIM - R
        THRESHOLD = 0.1
        B, T = (4, 256)
        Bx, Tx, C = x.shape
        H, D, Ds, r = (N_HEAD, HEAD_DIM, D_STD, R)
        s_std = jnp.sqrt(jnp.clip(w_std, 1e-08, None))
        s_rec = jnp.sqrt(jnp.clip(w_rec, 1e-08, None))
        col_scale = jnp.concatenate([jnp.repeat(s_std, Ds), jnp.repeat(s_std, Ds), jnp.ones((C,), dtype=x.dtype), jnp.repeat(s_rec, r), jnp.repeat(s_rec, r)])
        Wb = Wa * col_scale[None, :]
        fused = x @ Wb
        q_std_end = H * Ds
        k_std_end = q_std_end + H * Ds
        v_end = k_std_end + C
        q_low_end = v_end + H * r

        def heads(t, d):
            return t.reshape(Bx, Tx, H, d).transpose(0, 2, 1, 3)
        Q_std = heads(fused[..., :q_std_end], Ds)
        K_std = heads(fused[..., q_std_end:k_std_end], Ds)
        V = heads(fused[..., k_std_end:v_end], D)
        Q_low = heads(fused[..., v_end:q_low_end], r)
        K_low = heads(fused[..., q_low_end:], r)
        use_ra = (w_rec > THRESHOLD)[None, :, None, None]
        q_tail = jnp.where(use_ra, K_low, Q_low)
        k_tail = jnp.where(use_ra, Q_low, K_low)
        Qf = jnp.concatenate([Q_std, q_tail], axis=-1)
        Kf = jnp.concatenate([K_std, k_tail], axis=-1)
        scale = 1.0 / jnp.sqrt(jnp.asarray(D, dtype=x.dtype))
        scores = jnp.einsum('bhtd,bhsd->bhts', Qf, Kf) * scale
        causal = jnp.tril(jnp.ones((Tx, Tx), dtype=bool))
        scores = jnp.where(causal[None, None], scores, jnp.finfo(scores.dtype).min)
        attn = jax.nn.softmax(scores, axis=-1)
        out = jnp.einsum('bhts,bhsd->bhtd', attn, V)
        y = out.transpose(0, 2, 1, 3).reshape(Bx, Tx, C)
        return y @ Wp
    x = x + jnp.tanh(g_xattn[0]) * _L0_xattn_ref(_layernorm(x, axis=-1), ctx_2048, ctx_2048)
    x = x + jnp.tanh(g_ffn[0]) * _L0_ffn_ref(_layernorm(x, axis=-1), L0_ffn_SU_ug, L0_ffn_SU_dp, L0_ffn_Wscale_ug, L0_ffn_Wscale_dp, L0_ffn_W_up, L0_ffn_W_gate, L0_ffn_W_down)
    x = x + jnp.tanh(g_xattn[1]) * _L1_xattn_ref(_layernorm(x, axis=-1), ctx_2048, L1_xattn_Wq, L1_xattn_Wk, L1_xattn_Wv, L1_xattn_Wo, L1_xattn_q_norm_w, L1_xattn_k_norm_w)
    x = x + jnp.tanh(g_ffn[1]) * _L1_ffn_ref(_layernorm(x, axis=-1), L1_ffn_Wa, L1_ffn_Wp, L1_ffn_w_std, L1_ffn_w_rec)
    return x

_drawn_inputs = setup_inputs


def setup_inputs(seed=0):
    import zlib

    import numpy as np

    out = dict(_drawn_inputs(seed))
    spreads = {'g_ffn': (-1.0, 0.6), 'L1_xattn_q_norm_w': (1.0, 0.6), 'L1_xattn_k_norm_w': (1.0, 0.6)}
    factors = {'L0_ffn_Wscale_dp': 2.948, 'L1_ffn_w_std': 64.0, 'L1_ffn_w_rec': 58.397}
    for name, (base, spread) in spreads.items():
        noise = np.random.default_rng([zlib.crc32(name.encode()), seed]).standard_normal(out[name].shape)
        drawn = base * np.exp(spread * noise) if base else spread * noise
        out[name] = jnp.asarray(drawn.astype(out[name].dtype))
    for name, factor in factors.items():
        out[name] = (out[name] * factor).astype(out[name].dtype)
    return out
```

```python
from contextlib import ExitStack

import concourse.bass as bass
from concourse import mybir

F32 = mybir.dt.float32
F32R = mybir.dt.float32r
U8 = mybir.dt.uint8
ALU = mybir.AluOpType
ACT = mybir.ActivationFunctionType
AX = mybir.AxisListType

B, S, T, D = 16, 112, 375, 512
P = 128
DC = D // P
H = 16
HD = D // H
G = 4
HPG = H // G
KC, KP = 3, T // 3
TE = T + 1
XHD = 128
INTER = 2048
R = 8
DS = HD - R
LN_EPS = 1e-5
RMS_EPS = 1e-6
PASSES = ((0, 0), (0, 1), (1, 0))


def f32(ap):
    return ap.bitcast(F32)


class Memory:

    def __init__(self, nc, phase):
        self.nc, self.phase, self.stack = nc, phase, ExitStack()

    def __enter__(self):
        self.semaphores = []
        self.stack.__enter__()
        return self

    def __exit__(self, *what):
        done = self.stack.__exit__(*what)
        if self.semaphores:
            self.nc.clear_and_free_semaphores(self.semaphores)
            self.nc.all_engine_barrier()
        return done

    def sb(self, name, shape, dt=F32):
        return self.stack.enter_context(self.nc.sbuf_tensor(f"{self.phase}_{name}", shape, dt))

    def ps(self, name, shape, dt=F32):
        return self.stack.enter_context(self.nc.psum_tensor(f"{self.phase}_{name}", shape, dt))

    def sem(self, name):
        self.semaphores.append(self.nc.alloc_semaphore(f"{self.phase}_{name}"))
        return self.semaphores[-1]

    def block(self):
        return self.stack.enter_context(self.nc.Block())


def batches(eng, head, body):
    head((0, 0, 0))
    body(None, (0, 0, 0), (1, 1, 0))
    with eng.Fori(0, B // 2 - 1) as i:
        body((2 * i, 0, i), (2 * i + 1, 1, i), (2 * i + 2, 0, i + 1))
        body((2 * i + 1, 1, i), (2 * i + 2, 0, i + 1), (2 * i + 3, 1, i + 1))
    last = B // 2 - 1
    body((B - 2, 0, last), (B - 1, 1, last), None)
    body((B - 1, 1, last), None, None)


def constants(m):
    return {
        "ident": m.sb("ident", [P, P]),
        "hadamard": m.sb("hadamard", [P, P]),
        "neghalf": m.sb("neghalf", [P, H]),
        "rms_eps": m.sb("rms_eps", [P, G]),
        "later": m.sb("later", [S, S], U8),
        "masked_score": m.sb("masked_score", [S, S]),
        "gates": m.sb("gates", [P, 4]),
        "qk_w": m.sb("qk_w", [P, 1]),
        "bn": m.sb("bn", [S, B, 6]),
        "mv": m.sb("mv", [S, B, 2]),
        "ve": m.sb("ve", [S, B]),
        "rstd": m.sb("rstd", [S, B, 1]),
    }


def setup_phase(nc, keep, io):
    with Memory(nc, "s") as m:
        xin = m.sb("xin", [S, B, D])
        qw = m.sb("qw", [P, 2])
        gate_raw = m.sb("gate_raw", [P, 4])
        had_tmp = m.sb("had_tmp", [P, P])
        ones, later = m.sb("ones", [P, P]), m.sb("later", [S, S])
        zeroed, made, x_loaded, w_loaded = m.sem("zeroed"), m.sem("made"), m.sem("x_loaded"), m.sem("w_loaded")
        norm = norm_semaphores(m)
        block = m.block()

        @block.sync
        def _(sp):
            sp.dma_start(xin[:, :, :], io["x"].rearrange("b s d -> s b d")).then_inc(x_loaded, 16)
            with nc.allow_non_contiguous_dma(reason="a few words"):
                sp.dma_start(qw[:, 0:1], io["q_norm_w"].rearrange("(p a) -> p a", a=1)).then_inc(w_loaded, 16)
                sp.dma_start(qw[:, 1:2], io["k_norm_w"].rearrange("(p a) -> p a", a=1)).then_inc(w_loaded, 16)
                for n, name in enumerate(("g_xattn", "g_ffn")):
                    row = io[name].rearrange("(a n) -> a n", a=1)
                    sp.dma_start(gate_raw[:, 2 * n:2 * n + 2], row.broadcast_to([P, 2])).then_inc(w_loaded, 16)

        @block.gpsimd
        def _(pool):
            pool.memset(keep["ident"][:, :], 0.0).then_inc(zeroed, 1)
            pool.memset(ones[:, :], 1.0).then_inc(zeroed, 1)
            pool.memset(keep["neghalf"][:, :], -0.5).then_inc(zeroed, 1)
            pool.memset(keep["rms_eps"][:, :], RMS_EPS).then_inc(zeroed, 1)
            pool.wait_ge(zeroed, 4)
            pool.affine_select(out=keep["ident"][:, :], in_=keep["ident"][:, :], compare_op=ALU.not_equal, fill=1.0,
                               base=0, pattern=[[-1, P]], channel_multiplier=1).then_inc(made, 1)
            pool.affine_select(out=later[:, :], in_=ones[0:S, 0:S], compare_op=ALU.is_gt, fill=0.0,
                               base=0, pattern=[[1, S]], channel_multiplier=-1).then_inc(made, 1)
            norm_rstd(pool, keep, norm)

        @block.scalar
        def _(act):
            act.wait_ge(w_loaded, 64)
            act.activation(keep["gates"][:, :], gate_raw[:, :], ACT.Tanh)

        @block.vector
        def _(dve):
            dve.wait_ge(w_loaded, 64)
            dve.scalar_tensor_tensor(out=keep["qk_w"][:, :], in0=qw[:, 0:1], scalar=float(XHD) ** -0.5, in1=qw[:, 1:2],
                                     op0=ALU.mult, op1=ALU.mult)
            dve.memset(keep["masked_score"][:, :], -10000.0)
            dve.wait_ge(made, 2)
            dve.tensor_copy(keep["later"][:, :], later[:, :])
            stages = P.bit_length() - 1
            src = keep["ident"]
            for stage in range(stages):
                dst = had_tmp if (stages - stage) % 2 == 0 else keep["hadamard"]
                dve.wait_ge(made, 2 + 2 * stage)
                pair, out = (t[:, :].rearrange("p (a two n) -> p a two n", two=2, n=1 << stage) for t in (src, dst))
                dve.tensor_tensor(out[:, :, 0, :], pair[:, :, 0, :], pair[:, :, 1, :], ALU.add).then_inc(made, 1)
                dve.tensor_tensor(out[:, :, 1, :], pair[:, :, 0, :], pair[:, :, 1, :], ALU.subtract).then_inc(made, 1)
                src = dst
            dve.wait_ge(x_loaded, 16)
            for b in range(B):
                dve.bn_stats(keep["bn"][:, b, :], xin[:, b, :]).then_inc(norm["counted"], 1)
            norm_moments(dve, keep, norm)


def norm_semaphores(m):
    return {name: m.sem(name) for name in ("counted", "moments", "shifted")}


def norm_moments(dve, keep, norm):
    dve.wait_ge(norm["counted"], B)
    for b in range(B):
        dve.bn_aggr(keep["mv"][:, b, :], keep["bn"][:, b, :]).then_inc(norm["moments"], 1)
    dve.wait_ge(norm["moments"], B)
    dve.tensor_scalar(keep["ve"][:, :], keep["mv"][:, :, 1], LN_EPS, None, ALU.add).then_inc(norm["shifted"], 1)


def norm_rstd(pool, keep, norm):
    pool.wait_ge(norm["shifted"], 1)
    pool.tensor_tensor(keep["rstd"][:, :, 0], keep["ve"][:, :], keep["neghalf"][0:S, 0:B], ALU.pow)


def phase_a(nc, keep, io):
    FILL = ((0, ("k", 0), 0), (1, ("v", 0), 1), (3, ("ctx", 0), 2), (4, ("back", 0), 1), (4, ("k", 1), 0), (5, ("kt", 0), 2),
            (6, ("ctx", 1), 1), (7, ("v", 1), 2), (8, ("k", 2), 0), (9, ("ctx", 2), 1), (10, ("q", 0), 2), (11, ("kt", 1), 1),
            (12, ("v", 2), 2), (13, ("kt", 2), 0))
    ITEMS = [what for _, what, _ in FILL]
    BANK = {what: n for _, what, n in FILL}
    NEXT, BEFORE = ("ctx", "q"), ("back",)
    SUM_K = {1: 0, 5: 1, 9: 2}
    SCALE_K = {2: 0, 7: 1, 11: 2}
    WEIGH = {2: -1, 6: 0, 10: 1, 14: 2}
    COPY = {3: -1, 7: 0, 11: 1, 15: 2}
    FINISH = 5
    AHEAD = 2
    with Memory(nc, "a") as m:
        w_raw = m.sb("w_raw", [P, DC, 2 * D])
        w = [m.sb(f"w_{n}", [P, DC, 2 * D], F32R) for n in ("hi", "lo")]
        xin = m.sb("xin", [S, 2, D])
        xn = m.sb("xn", [S, D])
        ctx = m.sb("ctx", [KP, 2, KC, D])
        v = [m.sb(f"v_{n}", [KP, 2, KC, D], F32R) for n in ("hi", "lo")]
        kT = [m.sb(f"kT_{n}", [P, 2, DC, TE], F32R) for n in ("hi", "lo")]
        q = [m.sb(f"q_{n}", [P, 2, G, HPG, S], F32R) for n in ("hi", "lo")]
        probs = m.sb("probs", [S, AHEAD, T])
        pT = [m.sb(f"pT_{n}", [KP, 2, KC, HPG, S], F32R) for n in ("hi", "lo")]
        oT = m.sb("oT", [P, G, S])
        xout = m.sb("xout", [S, 2, D])
        kn = m.sb("kn", [KP, 2, D])
        vout = m.sb("vout", [KP, KC, D])
        kout = m.sb("kout", [P, DC, TE])
        squares = m.sb("squares", [KP, D])
        ssq = m.sb("ssq", [KP, 2, G])
        ssq_eps = m.sb("ssq_eps", [KP, 2, G])
        rk = m.sb("rk", [KP, 2, G])
        nmax = m.sb("nmax", [S, 2, H])
        sums = m.sb("sums", [S, 2, H])
        rsum = m.sb("rsum", [S, H])
        tmp = m.sb("tmp", [S, D])

        score = [m.ps(f"score{n}", [P, 512]) for n in range(AHEAD)]
        turned = [m.ps(f"turned{n}", [P, 512]) for n in range(2)]
        outp = m.ps("outp", [P, 512])
        shared = [m.ps(f"shared{n}", [P, 512]) for n in range(3)]

        w_loaded, w_hi, w_split, cleared = m.sem("w_loaded"), m.sem("w_hi"), m.sem("w_split"), m.sem("cleared")
        x_loaded = [m.sem(f"x_loaded{n}") for n in range(2)]
        ctx_loaded = [m.sem(f"ctx_loaded{n}") for n in range(2)]
        x_stored = [m.sem(f"x_stored{n}") for n in range(2)]
        k_stored, v_stored = m.sem("k_stored"), m.sem("v_stored")
        xn_done = m.sem("xn_done")
        shared_ready = m.sem("shared_ready")
        kT_hi, v_hi, q_hi = m.sem("kT_hi"), m.sem("v_hi"), m.sem("q_hi")
        kT_split, v_split, q_split = m.sem("kT_split"), m.sem("v_split"), m.sem("q_split")
        scores_ready, masked, max_done = m.sem("scores_ready"), m.sem("masked"), m.sem("max_done")
        probs_ready, turned_ready = m.sem("probs_ready"), m.sem("turned_ready")
        pT_hi, pT_split = m.sem("pT_hi"), m.sem("pT_split")
        out_ready, out_copied, out_copied_too = m.sem("out_ready"), m.sem("out_copied"), m.sem("out_copied_too")
        squared, ssq_done, eps_done, rk_done, kn_done = m.sem("squared"), m.sem("ssq_done"), m.sem("eps_done"), m.sem("rk_done"), m.sem("kn_done")
        k_out, v_out = m.sem("k_out"), m.sem("v_out")
        rsum_done, tmp_done, x_done = m.sem("rsum_done"), m.sem("tmp_done"), m.sem("x_done")
        norm = norm_semaphores(m)
        block = m.block()

        def bank(what):
            return shared[BANK[what]]

        def missing(e, what):
            if not isinstance(e, int):
                return False
            return (e <= 0 and what[0] in BEFORE or e < 0 and what[0] not in NEXT
                    or e >= B - 1 and what[0] in NEXT or e >= B and what[0] not in BEFORE)

        def written(e, what):
            if isinstance(e, int) and e in (-1, 0, B - 1, B):
                ahead = [n for n in ITEMS if n[0] in NEXT]
                if e == -1:
                    return ahead.index(what) + 1
                order = [n for n in ITEMS if not missing(e, n)] if e < B else [("back", 0)]
                first = len(ahead) + (len(ITEMS) * e - len(BEFORE) if e else 0) - (len(ahead) if e == B else 0)
                return first + order.index(what) + 1
            return 4 - len(BEFORE) + len(ITEMS) * e + ITEMS.index(what) + 1

        def read(e, what):
            name, c = what
            if name == "k":
                return kn_done, KC * e + c + 1
            if name == "v":
                return v_out, KC * e + c + 1
            if name == "kt":
                return k_out, KC * e + c + 1
            if name == "ctx":
                return kT_split, KC * (e + 1) + c + 1
            if name == "q":
                return q_split, e + 2
            return tmp_done, e

        def earlier(e, what):
            own = [n for n in ITEMS if BANK[n] == BANK[what]]
            at = own.index(what)
            while True:
                at, e = (at - 1, e) if at else (len(own) - 1, e - 1)
                if isinstance(e, int) and e < -1:
                    return None
                if not missing(e, own[at]):
                    return e, own[at]

        @block.sync
        def _(sp):
            for n, name in enumerate(("Wk", "Wv")):
                sp.dma_start(w_raw[:, :, n * D:(n + 1) * D], io[name].rearrange("(c p) n -> p c n", p=P)).then_inc(w_loaded, 16)

            def load_ctx(b, p, half):
                sp.dma_start(ctx[:, p, :, :], io["ctx"][b, :, :].rearrange("(c p) d -> p c d", p=KP)).then_inc(ctx_loaded[p], 16)

            def load_x(b, p, half):
                sp.dma_start(xin[:, p, :], io["x"][b, :, :]).then_inc(x_loaded[p], 16)

            def head(cur):
                load_ctx(*cur)
                load_x(*cur)

            def body(before, cur, after):
                if after:
                    if before:
                        sp.wait_ge(v_split, before[0] + 1)
                        sp.wait_ge(kT_split, KC * before[0] + KC)
                    load_ctx(*after)
                if before:
                    b, p, half = before
                    sp.wait_ge(x_done, b + 1)
                    sp.dma_start(io["x1"][b, :, :], xout[:, p, :]).then_inc(x_stored[p], 16)
                if after:
                    load_x(*after)
                if cur:
                    sp.wait_ge(v_out, KC * cur[0] + KC)
                    sp.dma_start(io["v1"][cur[0], :, :, :], vout[:, :, :]).then_inc(v_stored, 16)
                    sp.wait_ge(k_out, KC * cur[0] + KC)
                    sp.dma_start(io["k1"][cur[0], :, :, :], kout[:, :, :]).then_inc(k_stored, 16)

            batches(sp, head, body)
            for p in range(2):
                sp.wait_ge(x_stored[p], 16 * (B // 2) + 16)
            sp.wait_ge(k_stored, 16 * B + 16)
            sp.wait_ge(v_stored, 16 * B + 16)

        @block.gpsimd
        def _(pool):
            for part in q:
                pool.memset(f32(part[:, :, :, :, :]), 0.0).then_inc(cleared, 1)
            for part in kT:
                pool.memset(f32(part[:, :, :, T:TE]), 0.0).then_inc(cleared, 1)
            pool.memset(kout[:, :, T:TE], 0.0).then_inc(cleared, 1)

            def head(cur):
                b, p, half = cur
                pool.wait_ge(v_hi, b + 1)
                pool.tensor_tensor(v[1][:, p, :, :], ctx[:, p, :, :], f32(v[0][:, p, :, :]), ALU.subtract).then_inc(v_split, 1)

            def body(before, cur, after):
                for c in range(KC if cur else 0):
                    n = KC * cur[0] + c + 1
                    pool.wait_ge(ssq_done, n)
                    pool.tensor_tensor(ssq_eps[:, c % 2, :], ssq[:, c % 2, :], keep["rms_eps"][0:KP, :], ALU.add).then_inc(eps_done, 1)
                    pool.wait_ge(eps_done, n)
                    pool.tensor_tensor(rk[:, c % 2, :], ssq_eps[:, c % 2, :], keep["neghalf"][0:KP, 0:G], ALU.pow).then_inc(rk_done, 1)
                if after:
                    head(after)

            batches(pool, head, body)
            norm_rstd(pool, keep, norm)

        @block.scalar
        def _(act):
            for signal, credit in ((probs_ready, AHEAD), (out_copied, 1)):
                act.sem_inc(signal, credit)
            act.wait_ge(w_loaded, 32)
            act.activation(w[0][:, :, :], w_raw[:, :, :], ACT.Copy).then_inc(w_hi, 1)
            act.wait_ge(cleared, 5)

            def ctx_hi(b, p, c):
                act.wait_ge(shared_ready, written(b - 1, ("ctx", c)))
                src = bank(("ctx", c))[:, 0:DC * KP].rearrange("p (c k) -> p c k", c=DC)
                act.activation(kT[0][:, p, :, c * KP:(c + 1) * KP], src, ACT.Copy).then_inc(kT_hi, 1)
                if c == KC - 1:
                    act.activation(v[0][:, p, :, :], ctx[:, p, :, :], ACT.Copy).then_inc(v_hi, 1)

            def query_hi(b, p):
                act.wait_ge(shared_ready, written(b - 1, ("q", 0)))
                for j in range(HPG):
                    r = slice(HD * j, HD * j + HD)
                    src = bank(("q", 0))[r, 0:DC * S].rearrange("p (g s) -> p g s", g=G)
                    act.activation(q[0][r, p, :, j, :], src, ACT.Copy, scale=float(HD) ** -0.5).then_inc(q_hi, 1)

            def head(cur):
                for c in range(KC):
                    ctx_hi(cur[0], cur[1], c)
                query_hi(cur[0], cur[1])

            def exps(b, p, h):
                act.wait_ge(max_done, H * b + h + 1)
                act.wait_ge(turned_ready, H * b + h + 1)
                act.activation(probs[:, h % AHEAD, :], score[h % AHEAD][0:S, 0:T], ACT.Exp, bias=nmax[:, p, h:h + 1],
                               accum_out=sums[:, p, h:h + 1]).then_inc(probs_ready, 1)

            def key_squares(b, c):
                act.wait_ge(shared_ready, written(b, ("k", c)))
                act.activation(squares[:, :], bank(("k", c))[0:KP, :], ACT.Square, scale=float(XHD) ** -0.5).then_inc(squared, 1)

            def values_out(b, c):
                act.wait_ge(shared_ready, written(b, ("v", c)))
                act.wait_ge(v_stored, 16 * b + 16)
                act.activation(vout[:, c, :], bank(("v", c))[0:KP, :], ACT.Copy).then_inc(v_out, 1)

            def keys_out(b, c):
                act.wait_ge(shared_ready, written(b, ("kt", c)))
                act.wait_ge(k_stored, 16 * b + 16)
                src = bank(("kt", c))[:, 0:DC * KP].rearrange("p (c k) -> p c k", c=DC)
                act.activation(kout[:, :, c * KP:(c + 1) * KP], src, ACT.Copy, scale=keep["qk_w"][:, 0:1]).then_inc(k_out, 1)

            def probs_hi(b, h):
                g, j = divmod(h, HPG)
                act.wait_ge(turned_ready, H * b + h + 1 + AHEAD)
                src = turned[h % 2][0:KP, 0:KC * S].rearrange("p (c s) -> p c s", c=KC)
                act.activation(pT[0][:, g % 2, :, j, :], src, ACT.Copy).then_inc(pT_hi, 1)

            def copy_out(b, g):
                act.wait_ge(out_ready, G * b + g + 1)
                for j in range(HPG // 2):
                    r = slice(HD * j, HD * j + HD)
                    last = act.activation(oT[r, g, :], outp[r, j * S:(j + 1) * S], ACT.Copy)
                last.then_inc(out_copied, 1)

            def body(before, cur, after):
                if cur and not before:
                    for h in range(AHEAD):
                        exps(cur[0], cur[1], h)
                for h in range(H):
                    if cur:
                        probs_hi(cur[0], h)
                        if h + AHEAD < H:
                            exps(cur[0], cur[1], h + AHEAD)
                        elif after:
                            exps(after[0], after[1], h + AHEAD - H)
                    if h in COPY:
                        if COPY[h] < 0 and before:
                            copy_out(before[0], G - 1)
                        elif COPY[h] >= 0 and cur:
                            copy_out(cur[0], COPY[h])
                    for _, (what, c), _ in (f for f in FILL if f[0] == h):
                        if what == "k" and cur:
                            key_squares(cur[0], c)
                        elif what == "v" and cur:
                            values_out(cur[0], c)
                        elif what == "kt" and cur:
                            keys_out(cur[0], c)
                        elif what == "ctx" and after:
                            ctx_hi(after[0], after[1], c)
                        elif what == "q" and after:
                            query_hi(after[0], after[1])

            batches(act, head, body)

        @block.vector
        def _(dve):
            dve.sem_inc(out_copied_too, 1)
            dve.sem_inc(pT_split, 2)
            dve.sem_inc(v_stored, 16)
            dve.sem_inc(k_stored, 16)
            for n in range(2):
                dve.sem_inc(x_stored[n], 16)
            dve.wait_ge(w_hi, 1)
            dve.tensor_tensor(w[1][:, :, :], w_raw[:, :, :], f32(w[0][:, :, :]), ALU.subtract).then_inc(w_split, 1)

            def normalize(b, p, half):
                dve.wait_ge(x_loaded[p], 16 * half + 16)
                dve.tensor_scalar(xn[:, :], xin[:, p, :], keep["mv"][:, b, 0:1], keep["rstd"][:, b, :],
                                  ALU.subtract, ALU.mult).then_inc(xn_done, 1)

            def ctx_lo(b, p, c):
                dve.wait_ge(kT_hi, KC * b + c + 1)
                src = bank(("ctx", c))[:, 0:DC * KP].rearrange("p (c k) -> p c k", c=DC)
                cols = slice(c * KP, (c + 1) * KP)
                dve.tensor_tensor(kT[1][:, p, :, cols], src, f32(kT[0][:, p, :, cols]), ALU.subtract).then_inc(kT_split, 1)

            def query_lo(b, p):
                dve.wait_ge(q_hi, HPG * b + HPG)
                for j in range(HPG):
                    r = slice(HD * j, HD * j + HD)
                    src = bank(("q", 0))[r, 0:DC * S].rearrange("p (g s) -> p g s", g=G)
                    last = dve.scalar_tensor_tensor(out=q[1][r, p, :, j, :], in0=src, scalar=float(HD) ** -0.5,
                                                    in1=f32(q[0][r, p, :, j, :]), op0=ALU.mult, op1=ALU.subtract)
                last.then_inc(q_split, 1)

            def head(cur):
                normalize(*cur)
                for c in range(KC):
                    ctx_lo(cur[0], cur[1], c)
                query_lo(cur[0], cur[1])

            def maximum(b, p, h):
                head = H * b + h + 1
                head = head if isinstance(head, int) else dve.to_reg(head)
                dve.wait_ge(cleared, 5)
                dve.wait_ge(scores_ready, head)
                dve.copy_predicated(score[h % AHEAD][0:S, T - S:T], keep["later"][:, :], keep["masked_score"][:, :]).then_inc(masked, 1)
                dve.wait_ge(masked, H * b + h + 1)
                dve.tensor_reduce(nmax[:, p, h:h + 1], score[h % AHEAD][0:S, 0:T], axis=AX.X, op=ALU.max, negate=True).then_inc(max_done, 1)

            def sum_keys(b, c):
                dve.wait_ge(squared, KC * b + c + 1)
                dve.tensor_reduce(ssq[:, c % 2, :], squares[:, :].rearrange("p (g d) -> p g d", g=G), axis=AX.X, op=ALU.add).then_inc(ssq_done, 1)

            def scale_keys(b, c):
                dve.wait_ge(rk_done, KC * b + c + 1)
                src = bank(("k", c))[0:KP, :].rearrange("p (g d) -> p g d", g=G)
                dve.tensor_tensor(kn[:, c % 2, :].rearrange("p (g d) -> p g d", g=G), src,
                                  rk[:, c % 2, :].unsqueeze(2).broadcast_to([KP, G, P]), ALU.mult).then_inc(kn_done, 1)

            def probs_lo(b, h):
                g, j = divmod(h, HPG)
                dve.wait_ge(pT_hi, H * b + h + 1)
                src = turned[h % 2][0:KP, 0:KC * S].rearrange("p (c s) -> p c s", c=KC)
                dve.tensor_tensor(pT[1][:, g % 2, :, j, :], src, f32(pT[0][:, g % 2, :, j, :]), ALU.subtract).then_inc(pT_split, 1)

            def copy_out(b, g):
                dve.wait_ge(out_ready, G * b + g + 1)
                for j in range(HPG // 2, HPG):
                    r = slice(HD * j, HD * j + HD)
                    last = dve.tensor_copy(oT[r, g, :], outp[r, j * S:(j + 1) * S])
                last.then_inc(out_copied_too, 1)

            def finish(b, p, half):
                dve.wait_ge(probs_ready, H * b + H + AHEAD)
                dve.reciprocal(rsum[:, :], sums[:, p, :]).then_inc(rsum_done, 1)
                dve.wait_ge(shared_ready, written(b + 1, ("back", 0)))
                dve.wait_ge(rsum_done, b + 1)
                dve.tensor_tensor(tmp[:, :].rearrange("p (h d) -> p h d", h=H), bank(("back", 0))[0:S, :].rearrange("p (h d) -> p h d", h=H),
                                  rsum[:, :].unsqueeze(2).broadcast_to([S, H, HD]), ALU.mult).then_inc(tmp_done, 1)
                dve.wait_ge(tmp_done, b + 1)
                dve.wait_ge(x_stored[p], 16 * half + 16)
                dve.scalar_tensor_tensor(out=xout[:, p, :], in0=tmp[:, :], scalar=keep["gates"][0:S, 0:1], in1=xin[:, p, :],
                                         op0=ALU.mult, op1=ALU.add).then_inc(x_done, 1)
                dve.wait_ge(x_done, b + 1)
                dve.bn_stats(keep["bn"][:, b, :], xout[:, p, :]).then_inc(norm["counted"], 1)

            def body(before, cur, after):
                if cur and not before:
                    for h in range(AHEAD):
                        maximum(cur[0], cur[1], h)
                for h in range(H):
                    if cur:
                        if h + AHEAD < H:
                            maximum(cur[0], cur[1], h + AHEAD)
                        elif after:
                            maximum(after[0], after[1], h + AHEAD - H)
                        probs_lo(cur[0], h)
                        if h in SUM_K:
                            sum_keys(cur[0], SUM_K[h])
                        if h in SCALE_K:
                            scale_keys(cur[0], SCALE_K[h])
                    if h in COPY:
                        if COPY[h] < 0 and before:
                            copy_out(before[0], G - 1)
                        elif COPY[h] >= 0 and cur:
                            copy_out(cur[0], COPY[h])
                    if h == FINISH and before:
                        finish(*before)
                    for _, (what, c), _ in (f for f in FILL if f[0] == h and after):
                        if what == "ctx":
                            if c == KC - 1:
                                normalize(*after)
                            ctx_lo(after[0], after[1], c)
                        elif what == "q":
                            query_lo(after[0], after[1])

            batches(dve, head, body)
            norm_moments(dve, keep, norm)

        @block.tensor
        def _(pe):
            pe.sem_inc(turned_ready, AHEAD)
            ident = keep["ident"]

            def bank_free(e, what):
                before = earlier(e, what)
                if before:
                    pe.wait_ge(*read(*before))

            def turn_ctx(b, p, half, c):
                if c == 0:
                    pe.wait_ge(ctx_loaded[p], 16 * half + 16)
                bank_free(b - 1, ("ctx", c))
                for n in range(DC):
                    last = pe.transpose(bank(("ctx", c))[:, n * KP:(n + 1) * KP], ctx[:, p, c, n * P:(n + 1) * P], ident[0:KP, 0:KP])
                last.then_inc(shared_ready, 1)

            def turn_queries(b):
                pe.wait_ge(xn_done, b + 1)
                bank_free(b - 1, ("q", 0))
                for n in range(DC):
                    last = pe.transpose(bank(("q", 0))[:, n * S:(n + 1) * S], xn[:, n * P:(n + 1) * P], ident[0:S, 0:S])
                last.then_inc(shared_ready, 1)

            def head(cur):
                for c in range(KC):
                    turn_ctx(*cur, c)
                turn_queries(cur[0])

            def scores(b, p, h):
                g, j = divmod(h, HPG)
                if h == 0:
                    pe.wait_ge(q_split, b + 1)
                    pe.wait_ge(kT_split, KC * b + KC)
                pe.wait_ge(probs_ready, H * b + h + 1)
                for n, (s, r) in enumerate(PASSES):
                    last = pe.matmul(score[h % AHEAD][0:S, 0:TE], q[s][:, p, g, j, :], kT[r][:, p, g, :],
                                     start=n == 0, stop=n == len(PASSES) - 1)
                last.then_inc(scores_ready, 1)

            def project(b, p, what):
                name, c = what
                bank_free(b, what)
                cols = slice(0, D) if name == "k" else slice(D, 2 * D)
                for n, (s, r) in enumerate(PASSES):
                    for k in range(DC):
                        last = pe.matmul(bank(what)[0:KP, :], kT[s][:, p, k, c * KP:(c + 1) * KP], w[r][:, k, cols],
                                         start=n == 0 and k == 0, stop=n == len(PASSES) - 1 and k == DC - 1)
                last.then_inc(shared_ready, 1)

            def turn_keys(b, c):
                pe.wait_ge(kn_done, KC * b + c + 1)
                bank_free(b, ("kt", c))
                for n in range(DC):
                    last = pe.transpose(bank(("kt", c))[:, n * KP:(n + 1) * KP], kn[:, c % 2, n * P:(n + 1) * P], ident[0:KP, 0:KP])
                last.then_inc(shared_ready, 1)

            def turn_probs(b, h):
                pe.wait_ge(probs_ready, H * b + h + 1 + AHEAD)
                pe.wait_ge(pT_split, H * b + h + 1)
                for c in range(KC):
                    last = pe.transpose(turned[h % 2][0:KP, c * S:(c + 1) * S], probs[:, h % AHEAD, c * KP:(c + 1) * KP], ident[0:S, 0:S])
                last.then_inc(turned_ready, 1)

            def weigh(b, p, g):
                pe.wait_ge(pT_split, H * b + HPG * (g + 1) + 2)
                pe.wait_ge(out_copied, G * b + g + 1)
                pe.wait_ge(out_copied_too, G * b + g + 1)
                if g == 0:
                    pe.wait_ge(v_split, b + 1)
                for n, (s, r) in enumerate(PASSES):
                    for c in range(KC):
                        last = pe.matmul(outp[:, 0:HPG * S], v[s][:, p, c, g * P:(g + 1) * P],
                                         pT[r][:, g % 2, c, :, :].rearrange("p j s -> p (j s)"),
                                         start=n == 0 and c == 0, stop=n == len(PASSES) - 1 and c == KC - 1)
                last.then_inc(out_ready, 1)

            def turn_back(b):
                pe.wait_ge(out_copied, G * b + G + 1)
                pe.wait_ge(out_copied_too, G * b + G + 1)
                bank_free(b + 1, ("back", 0))
                for g in range(G):
                    last = pe.transpose(bank(("back", 0))[0:S, g * P:(g + 1) * P], oT[:, g, :], ident[:, :])
                last.then_inc(shared_ready, 1)

            def body(before, cur, after):
                if cur and not before:
                    pe.wait_ge(w_split, 1)
                    for h in range(AHEAD):
                        scores(cur[0], cur[1], h)
                for h in range(H):
                    if cur:
                        turn_probs(cur[0], h)
                        if h + AHEAD < H:
                            scores(cur[0], cur[1], h + AHEAD)
                        elif after:
                            scores(after[0], after[1], h + AHEAD - H)
                    if h in WEIGH:
                        if WEIGH[h] < 0 and before:
                            weigh(before[0], before[1], G - 1)
                        elif WEIGH[h] >= 0 and cur:
                            weigh(cur[0], cur[1], WEIGH[h])
                    for _, (what, c), _ in (f for f in FILL if f[0] == h):
                        if what in ("k", "v") and cur:
                            project(cur[0], cur[1], (what, c))
                        elif what == "kt" and cur:
                            turn_keys(cur[0], c)
                        elif what == "ctx" and after:
                            turn_ctx(*after, c)
                        elif what == "q" and after:
                            turn_queries(after[0])
                        elif what == "back" and before:
                            turn_back(before[0])

            batches(pe, head, body)


IC = INTER // P
NG = 4
BPG = B // NG
GS = BPG * S


def phase_b_prepare(nc, keep, io, big):
    wug, wdn, xT = big["wug"], big["wdn"], big["xT"]
    BLOCKS = IC // NG
    STAGES = 4
    with Memory(nc, "p") as m:
        ug_raw = m.sb("ug_raw", [P, 4, D])
        down_raw = m.sb("down_raw", [P, INTER])
        down = [m.sb(f"down{n}", [P, INTER]) for n in range(2)]
        signs = m.sb("signs", [S, D])
        down_scale = m.sb("down_scale", [P, NG])
        xin = m.sb("xin", [S, 2, D])
        xn = m.sb("xn", [S, D])
        z = [m.sb(f"z{n}", [S, D]) for n in range(3)]
        zT = m.sb("zT", [P, DC, GS])
        z_bank = [m.ps(f"z_bank{n}", [P, 512]) for n in range(2)]
        h_bank = [m.ps(f"h_bank{n}", [P, 512]) for n in range(2)]
        u_bank = [m.ps(f"u_bank{n}", [P, 512]) for n in range(2)]
        d_bank = [m.ps(f"d_bank{n}", [P, 512]) for n in range(2)]
        small_loaded, d_loaded = m.sem("small_loaded"), m.sem("d_loaded")
        u_loaded = [m.sem(f"u_loaded{n}") for n in range(4)]
        x_loaded = [m.sem(f"x_loaded{n}") for n in range(2)]
        xn_done, signed, z_sums, z_done, z_turned, z_copied = (m.sem(n) for n in ("xn_done", "signed", "z_sums", "z_done", "z_turned", "z_copied"))
        rotated, x_hi, x_split = m.sem("rotated"), m.sem("x_hi"), m.sem("x_split")
        u_turned, u_copied = m.sem("u_turned"), m.sem("u_copied")
        d_scaled, d_sums, d_done, d_turned, d_copied = (m.sem(n) for n in ("d_scaled", "d_sums", "d_done", "d_turned", "d_copied"))
        d_rotated, d_signed, scales_made = m.sem("d_rotated"), m.sem("d_signed"), m.sem("scales_made")
        block = m.block()

        @block.sync
        def _(sp):
            with nc.allow_non_contiguous_dma(reason="scales by partition"):
                sp.dma_start(signs[:, :], io["SU_ug"].rearrange("(a n) -> a n", a=1).broadcast_to([S, D])).then_inc(small_loaded, 16)
                sp.dma_start(down_scale[:, :], io["Wscale_dp"].rearrange("(q p) -> p q", p=P)).then_inc(small_loaded, 16)
                sp.dma_start(big["down_signs"][:, :], io["SU_dp"].rearrange("(c p) -> p c", p=P)).then_inc(small_loaded, 16)
                sp.dma_start(big["ug_scale"][:, :], io["Wscale_ug"].rearrange("(c p) -> p c", p=P)).then_inc(small_loaded, 16)
            with sp.Fori(0, NG) as i:
                sp.wait_ge(d_scaled, i + 1)
                sp.dma_start(down_raw[:, :], io["W_down"].rearrange("(q p) n -> q p n", p=P)[i, :, :]).then_inc(d_loaded, 16)
                for k in range(BPG):
                    j = BPG * i + k
                    sp.wait_ge(xn_done, j + 1)
                    sp.dma_start(xin[:, k % 2, :], io["x1"][j, :, :]).then_inc(x_loaded[k % 2], 16)
                    for n, name in enumerate(("W_up", "W_gate")):
                        u = 2 * k + n
                        sp.wait_ge(u_turned, 2 * BLOCKS * i + u + 1)
                        sp.dma_start(ug_raw[:, u % 4, :], io[name].rearrange("(c p) n -> c p n", p=P)[j, :, :]).then_inc(u_loaded[u % 4], 16)

        @block.gpsimd
        def _(pool):
            pool.wait_ge(small_loaded, 64)
            with pool.Fori(0, NG) as i:
                for k in range(BPG):
                    j = BPG * i + k
                    pool.wait_ge(xn_done, j + 1 + 2)
                    pool.wait_ge(z_sums, 4 * j + 2)
                    pool.tensor_tensor(z[0][:, :], xn[:, :], signs[:, :], ALU.mult).then_inc(signed, 1)

        @block.scalar
        def _(act):
            for signal, credit in ((d_scaled, 1), (z_copied, 2), (u_copied, 2), (d_copied, 2), (d_signed, 2)):
                act.sem_inc(signal, credit)
            act.wait_ge(scales_made, 1)
            with act.Fori(0, NG) as i:
                act.wait_ge(d_loaded, 16 * i + 16)
                act.wait_ge(d_turned, 4 * i + 4)
                act.activation(down[0][:, :], down_raw[:, :], ACT.Copy, scale=down_scale[:, bass.ds(i, 1)]).then_inc(d_scaled, 1)
                for k in range(BPG):
                    j = BPG * i + k
                    for n in range(2):
                        u = 2 * k + n
                        act.wait_ge(u_turned, 2 * BLOCKS * i + u + 1 + 4)
                        act.activation(wug[:, :, n, bass.ds(j * P, P)], u_bank[n][:, :].rearrange("p (c n) -> p c n", c=DC),
                                       ACT.Copy).then_inc(u_copied, 1)
                    act.wait_ge(z_turned, j + 1 + 1)
                    if k == 0:
                        act.wait_ge(rotated, DC * i + 1)
                    act.activation(zT[:, :, k * S:(k + 1) * S], z_bank[k % 2][:, 0:DC * S].rearrange("p (c s) -> p c s", c=DC),
                                   ACT.Copy).then_inc(z_copied, 1)
                for c in range(DC):
                    act.wait_ge(d_turned, DC * i + c + 1 + 4)
                    act.activation(wdn[:, 4 * c:4 * c + 4, bass.ds(i * P, P)], d_bank[c % 2][:, :].rearrange("p (c n) -> p c n", c=4),
                                   ACT.Copy).then_inc(d_copied, 1)
                    act.wait_ge(rotated, DC * i + c + 1 + 1)
                    act.activation(xT[0][:, c, bass.ds(i * GS, GS)], h_bank[c % 2][:, 0:GS], ACT.Copy, scale=float(D) ** -0.5).then_inc(x_hi, 1)
            with act.Fori(0, IC // 2) as i:
                for n in range(2):
                    act.wait_ge(d_rotated, 2 * i + n + 1)
                    act.activation(wdn[:, 2 * i + n, :], d_bank[n][:, :], ACT.Copy,
                                   scale=big["down_signs"][:, bass.ds(2 * i + n, 1)]).then_inc(d_signed, 1)

        @block.vector
        def _(dve):
            for signal, credit in ((xn_done, 2), (z_sums, 4), (x_split, 2)):
                dve.sem_inc(signal, credit)
            dve.wait_ge(small_loaded, 64)
            dve.tensor_scalar(down_scale[:, :], down_scale[:, :], float(INTER) ** -0.5, None, ALU.mult).then_inc(scales_made, 1)

            def normalize(i, k):
                j = BPG * i + k
                dve.wait_ge(x_loaded[k % 2], 32 * i + 16 * (k // 2) + 16)
                dve.wait_ge(signed, j + 1)
                dve.tensor_scalar(xn[:, :], xin[:, k % 2, :], keep["mv"][:, j, 0:1], keep["rstd"][:, j, :],
                                  ALU.subtract, ALU.mult).then_inc(xn_done, 1)

            def pairs(buffer, h):
                halves = buffer.rearrange("p (a two n) -> p a two n", two=2, n=h)
                return halves[:, :, 0, :], halves[:, :, 1, :]

            def rotate_batch(i, k):
                j = BPG * i + k
                dve.wait_ge(signed, j + 1 + 1)
                for stage in range(2):
                    (a, b), (s, d) = pairs(z[stage][:, :], P << stage), pairs(z[stage + 1][:, :], P << stage)
                    if stage:
                        dve.wait_ge(z_sums, 4 * j + 2 + 4)
                        dve.wait_ge(z_turned, j + 1)
                    dve.tensor_tensor(s, a, b, ALU.add).then_inc(z_sums, 1)
                    dve.tensor_tensor(d, a, b, ALU.subtract).then_inc(z_sums, 1)

            def rotate_down(i, stage):
                if stage:
                    dve.wait_ge(d_sums, 2 * STAGES * i + 2 * stage)
                else:
                    dve.wait_ge(d_scaled, i + 1 + 1)
                (a, b), (s, d) = pairs(down[stage % 2][:, :], P << stage), pairs(down[1 - stage % 2][:, :], P << stage)
                dve.tensor_tensor(s, a, b, ALU.add).then_inc(d_sums, 1)
                dve.tensor_tensor(d, a, b, ALU.subtract).then_inc(d_sums, 1)

            dve.sem_inc(signed, 1)
            with dve.Fori(0, NG) as i:
                for k in range(BPG):
                    normalize(i, k)
                    rotate_down(i, k)
                    rotate_batch(i, k)
                for c in range(DC):
                    dve.wait_ge(x_hi, DC * i + c + 1)
                    cols = bass.ds(i * GS, GS)
                    dve.scalar_tensor_tensor(out=xT[1][:, c, cols], in0=h_bank[c % 2][:, 0:GS], scalar=float(D) ** -0.5,
                                             in1=f32(xT[0][:, c, cols]), op0=ALU.mult, op1=ALU.subtract).then_inc(x_split, 1)

        @block.tensor
        def _(pe):
            for signal, credit in ((z_turned, 1), (rotated, 1), (u_turned, 4), (d_turned, 4)):
                pe.sem_inc(signal, credit)
            ident, had = keep["ident"], keep["hadamard"]
            with pe.Fori(0, NG) as i:
                for k in range(BPG):
                    j = BPG * i + k
                    for n in range(2):
                        u = 2 * k + n
                        pe.wait_ge(u_loaded[u % 4], 32 * i + 16 * (u // 4) + 16)
                        pe.wait_ge(u_copied, 2 * BLOCKS * i + u + 1)
                        for c in range(DC):
                            last = pe.transpose(u_bank[n][:, c * P:(c + 1) * P], ug_raw[:, u % 4, c * P:(c + 1) * P], ident[:, :])
                        last.then_inc(u_turned, 1)
                    pe.wait_ge(z_sums, 4 * j + 4 + 4)
                    pe.wait_ge(z_copied, j + 1)
                    for c in range(DC):
                        last = pe.transpose(z_bank[k % 2][:, c * S:(c + 1) * S], z[2][:, c * P:(c + 1) * P], ident[0:S, 0:S])
                    last.then_inc(z_turned, 1)
                for c in range(NG):
                    pe.wait_ge(d_sums, 2 * STAGES * i + 2 * STAGES)
                    pe.wait_ge(d_copied, NG * i + c + 1)
                    for n in range(4):
                        r = slice((4 * c + n) * P, (4 * c + n + 1) * P)
                        last = pe.transpose(d_bank[c % 2][:, n * P:(n + 1) * P], down[0][:, r], ident[:, :])
                    last.then_inc(d_turned, 1)
                    if c == 0:
                        pe.wait_ge(z_copied, BPG * i + BPG + 2)
                    pe.wait_ge(x_split, DC * i + c + 1)
                    pe.matmul(h_bank[c % 2][:, 0:GS], had[:, :], zT[:, c, :], start=True, stop=True).then_inc(rotated, 1)
            pe.wait_ge(d_copied, NG * NG + 2)
            with pe.Fori(0, IC // 2) as i:
                for n in range(2):
                    pe.wait_ge(d_signed, 2 * i + n + 1)
                    pe.matmul(d_bank[n][:, :], had[:, :], wdn[:, 2 * i + n, :], start=True, stop=True).then_inc(d_rotated, 1)


def phase_b(nc, keep, io):
    with Memory(nc, "f") as outer:
        big = {
            "wug": outer.sb("wug", [P, DC, 2, INTER]),
            "wdn": outer.sb("wdn", [P, IC, D]),
            "xT": [outer.sb(f"xT_{n}", [P, DC, B * S], F32R) for n in ("hi", "lo")],
            "down_signs": outer.sb("down_signs", [P, IC]),
            "ug_scale": outer.sb("ug_scale", [P, 2 * IC]),
        }
        phase_b_prepare(nc, keep, io, big)
        phase_b_run(nc, keep, io, big)


def phase_b_run(nc, keep, io, big):
    wug, wdn, xT, ug_scale = big["wug"], big["wdn"], big["xT"], big["ug_scale"]
    with Memory(nc, "b") as m:
        wu = [m.sb(f"wu_{n}", [P, 2, DC, 2, P], F32R) for n in ("hi", "lo")]
        wd = [m.sb(f"wd_{n}", [P, 2, D], F32R) for n in ("hi", "lo")]
        silu = m.sb("silu", [P, 2, GS])
        hidden = m.sb("hidden", [P, 2, GS])
        hT = [m.sb(f"hT_{n}", [P, 2, GS], F32R) for n in ("hi", "lo")]
        xio = m.sb("xio", [S, BPG, D])
        up = [m.ps(f"up{n}", [P, 512]) for n in range(2)]
        gate = [m.ps(f"gate{n}", [P, 512]) for n in range(2)]
        y = [m.ps(f"y{n}", [P, 512]) for n in range(BPG)]
        x_loaded, x_stored, x_done, y_ready = m.sem("x_loaded"), m.sem("x_stored"), m.sem("x_done"), m.sem("y_ready")
        wu_hi, wu_split, wd_hi, wd_split = m.sem("wu_hi"), m.sem("wu_split"), m.sem("wd_hi"), m.sem("wd_split")
        gu_ready, silu_done, h_done, h_hi, h_split = (m.sem(n) for n in ("gu_ready", "silu_done", "h_done", "h_hi", "h_split"))
        norm = norm_semaphores(m)
        block = m.block()

        @block.sync
        def _(sp):
            with sp.Fori(0, NG) as g:
                sp.wait_ge(x_stored, 16 * g + 16)
                sp.dma_start(xio[:, :, :], io["x1"][bass.ds(BPG * g, BPG), :, :].rearrange("b s d -> s b d")).then_inc(x_loaded, 16)
                sp.wait_ge(x_done, BPG * g + BPG)
                sp.wait_ge(norm["counted"], BPG * g + BPG)
                sp.dma_start(io["x2"][bass.ds(BPG * g, BPG), :, :].rearrange("b s d -> s b d"), xio[:, :, :]).then_inc(x_stored, 16)
            sp.wait_ge(x_stored, 16 * NG + 16)

        @block.gpsimd
        def _(pool):
            pool.sem_inc(x_stored, 16)
            norm_rstd(pool, keep, norm)

        @block.scalar
        def _(act):
            for p in range(2):
                act.activation(wu[0][:, p, :, :, :], wug[:, :, :, p * P:(p + 1) * P], ACT.Copy).then_inc(wu_hi, 1)
            with act.Fori(0, NG) as g:
                with act.Fori(0, IC // 2) as i:
                    for p in range(2):
                        c, t = 2 * i + p, IC * g + 2 * i + p
                        act.wait_ge(gu_ready, t + 1 + 1)
                        act.activation(silu[:, p, :], gate[p][:, 0:GS], ACT.Silu, scale=ug_scale[:, bass.ds(IC + c, 1)]).then_inc(silu_done, 1)
                        act.activation(wd[0][:, p, :], wdn[:, c, :], ACT.Copy).then_inc(wd_hi, 1)
                        act.wait_ge(h_done, t + 1 + 2)
                        act.activation(hT[0][:, p, :], hidden[:, p, :], ACT.Copy).then_inc(h_hi, 1)
                        act.activation(wu[0][:, p, :, :, :], wug[:, :, :, bass.ds(((c + 2) % IC) * P, P)], ACT.Copy).then_inc(wu_hi, 1)

        @block.vector
        def _(dve):
            dve.sem_inc(h_done, 2)
            dve.sem_inc(x_done, 1)
            for p in range(2):
                dve.wait_ge(wu_hi, p + 1)
                dve.tensor_tensor(wu[1][:, p, :, :, :], wug[:, :, :, p * P:(p + 1) * P], f32(wu[0][:, p, :, :, :]),
                                  ALU.subtract).then_inc(wu_split, 1)
            with dve.Fori(0, NG) as g:
                with dve.Fori(0, IC // 2) as i:
                    for p in range(2):
                        c, t = 2 * i + p, IC * g + 2 * i + p
                        dve.wait_ge(silu_done, t + 1)
                        dve.scalar_tensor_tensor(out=hidden[:, p, :], in0=up[p][:, 0:GS], scalar=ug_scale[:, bass.ds(c, 1)], in1=silu[:, p, :],
                                                 op0=ALU.mult, op1=ALU.mult).then_inc(h_done, 1)
                        dve.wait_ge(wd_hi, t + 1)
                        dve.tensor_tensor(wd[1][:, p, :], wdn[:, c, :], f32(wd[0][:, p, :]), ALU.subtract).then_inc(wd_split, 1)
                        dve.wait_ge(h_hi, t + 1)
                        dve.tensor_tensor(hT[1][:, p, :], hidden[:, p, :], f32(hT[0][:, p, :]), ALU.subtract).then_inc(h_split, 1)
                        dve.wait_ge(wu_hi, t + 3)
                        dve.tensor_tensor(wu[1][:, p, :, :, :], wug[:, :, :, bass.ds(((c + 2) % IC) * P, P)],
                                          f32(wu[0][:, p, :, :, :]), ALU.subtract).then_inc(wu_split, 1)
                dve.wait_ge(x_loaded, 16 * g + 16)
                dve.wait_ge(y_ready, g + 1)
                for k in range(BPG):
                    dve.scalar_tensor_tensor(out=xio[:, k, :], in0=y[k][0:S, :], scalar=keep["gates"][0:S, 2:3], in1=xio[:, k, :],
                                             op0=ALU.mult, op1=ALU.add).then_inc(x_done, 1)
                for k in range(BPG):
                    dve.wait_ge(x_done, BPG * g + k + 1 + 1)
                    dve.bn_stats(keep["bn"][:, BPG * g + k, :], xio[:, k, :]).then_inc(norm["counted"], 1)
            norm_moments(dve, keep, norm)

        @block.tensor
        def _(pe):
            pe.sem_inc(gu_ready, 1)

            def project(g, c, t, p):
                pe.wait_ge(wu_split, t + 1)
                pe.wait_ge(h_done, t + 1)
                for n, out in ((1, gate[p]), (0, up[p])):
                    for k, (s, r) in enumerate(PASSES):
                        for d in range(DC):
                            last = pe.matmul(out[:, 0:GS], wu[s][:, p, d, n, :], xT[r][:, d, bass.ds(g * GS, GS)],
                                             start=k == 0 and d == 0, stop=k == len(PASSES) - 1 and d == DC - 1)
                last.then_inc(gu_ready, 1)

            def reduce(t, p, first, final):
                pe.wait_ge(h_split, t + 1)
                pe.wait_ge(wd_split, t + 1)
                for b in range(BPG):
                    for k, (s, r) in enumerate(PASSES):
                        last = pe.matmul(y[b][0:S, :], hT[s][:, p, b * S:(b + 1) * S], wd[r][:, p, :],
                                         start=first and k == 0, stop=final and k == len(PASSES) - 1)
                if final:
                    last.then_inc(y_ready, 1)

            with pe.Fori(0, NG) as g:
                project(g, 0, IC * g, 0)
                project(g, 1, IC * g + 1, 1)
                pe.wait_ge(x_done, BPG * g + 1)
                reduce(IC * g, 0, True, False)
                with pe.Fori(1, IC // 2) as i:
                    for p in range(2):
                        t = IC * g + 2 * i + p
                        project(g, 2 * i + p, t, p)
                        reduce(t - 1, 1 - p, False, False)
                reduce(IC * g + IC - 1, 1, False, True)


def phase_c(nc, keep, io):
    with Memory(nc, "o") as outer:
        wo = [outer.sb(f"wo_{n}", [P, H, D], F32R) for n in ("hi", "lo")]
        phase_c_queries(nc, keep, io, wo)
        phase_c_attention(nc, keep, io, wo)


def phase_c_queries(nc, keep, io, wo):
    LAG = 2
    QW = G * D
    TURN_X = 1
    with Memory(nc, "q") as m:
        w_raw = m.sb("w_raw", [P, DC, QW])
        w = [m.sb(f"w_{n}", [P, DC, QW], F32R) for n in ("hi", "lo")]
        xin = m.sb("xin", [S, 2, D])
        xn = m.sb("xn", [S, D])
        xT = [m.sb(f"xT_{n}", [P, 2, DC, S], F32R) for n in ("hi", "lo")]
        squares = m.sb("squares", [S, D])
        ssq = m.sb("ssq", [S, 2, G])
        ssq_eps = m.sb("ssq_eps", [S, 2, G])
        rq = m.sb("rq", [S, 2, G])
        qn = m.sb("qn", [S, 2, D])
        qT = m.sb("qT", [P, 2, H, S])
        x_bank = m.ps("x_bank", [P, 512])
        q_bank = [m.ps(f"q_bank{n}", [P, 512]) for n in range(G)]
        t_bank = [m.ps(f"t_bank{n}", [P, 512]) for n in range(2)]
        w_loaded = [m.sem(f"w_loaded{n}") for n in range(DC)]
        w_hi, w_split, wo_loaded, wo_hi, wo_split = (m.sem(n) for n in ("w_hi", "w_split", "wo_loaded", "wo_hi", "wo_split"))
        x_loaded = [m.sem(f"x_loaded{n}") for n in range(2)]
        q_stored = [m.sem(f"q_stored{n}") for n in range(2)]
        xn_done, x_turned, x_hi, x_split = (m.sem(n) for n in ("xn_done", "x_turned", "x_hi", "x_split"))
        q_ready, squared, ssq_done, eps_done, rq_done = (m.sem(n) for n in ("q_ready", "squared", "ssq_done", "eps_done", "rq_done"))
        qn_done, q_turned, q_copied = m.sem("qn_done"), m.sem("q_turned"), m.sem("q_copied")
        block = m.block()

        def lagging(before, cur, n):
            which = cur if n >= LAG else before
            return which and (which[0], which[1], (n - LAG) % G)

        @block.sync
        def _(sp):
            def load_x(b, p, half):
                sp.dma_start(xin[:, p, :], io["x2"][b, :, :]).then_inc(x_loaded[p], 16)

            def head(cur):
                load_x(*cur)
                wq = io["Wq"].rearrange("(c p) n -> p c n", p=P)
                for c in range(DC):
                    sp.dma_start(w_raw[:, c, :], wq[:, c, :]).then_inc(w_loaded[c], 16)

            def body(before, cur, after):
                if after:
                    if before:
                        sp.wait_ge(xn_done, before[0] + 1)
                    load_x(*after)
                if cur and not before:
                    sp.wait_ge(w_split, DC)
                    sp.dma_start(w_raw[:, :, :].rearrange("p c n -> p (c n)"),
                                 io["Wo"].rearrange("(h p) n -> p h n", p=P)).then_inc(wo_loaded, 16)
                if before:
                    b, p, half = before
                    sp.wait_ge(q_copied, G * b + G + 2)
                    sp.dma_start(io["q1"][b, :, :, :], qT[:, p, :, :]).then_inc(q_stored[p], 16)

            batches(sp, head, body)
            for p in range(2):
                sp.wait_ge(q_stored[p], 16 * (B // 2) + 16)

        @block.gpsimd
        def _(pool):
            def body(before, cur, after):
                for n in range(G if cur else 0):
                    t = G * cur[0] + n + 1
                    pool.wait_ge(ssq_done, t + 1)
                    pool.tensor_tensor(ssq_eps[:, n % 2, :], ssq[:, n % 2, :], keep["rms_eps"][0:S, :], ALU.add).then_inc(eps_done, 1)
                    pool.wait_ge(eps_done, t)
                    pool.tensor_tensor(rq[:, n % 2, :], ssq_eps[:, n % 2, :], keep["neghalf"][0:S, 0:G], ALU.pow).then_inc(rq_done, 1)

            batches(pool, lambda cur: None, body)

        @block.scalar
        def _(act):
            act.sem_inc(q_copied, 2)
            for c in range(DC):
                act.wait_ge(w_loaded[c], 16)
                act.activation(w[0][:, c, :], w_raw[:, c, :], ACT.Copy).then_inc(w_hi, 1)

            def head(cur):
                b, p, half = cur
                act.wait_ge(x_turned, b + 1)
                act.activation(xT[0][:, p, :, :], x_bank[:, 0:DC * S].rearrange("p (c s) -> p c s", c=DC), ACT.Copy).then_inc(x_hi, 1)

            def copy_queries(b, p, half, n):
                t = G * b + n + 1
                act.wait_ge(q_turned, t + 2)
                act.wait_ge(q_stored[p], 16 * half + 16)
                act.activation(qT[:, p, G * n:G * n + G, :], t_bank[n % 2][:, 0:G * S].rearrange("p (h s) -> p h s", h=G),
                               ACT.Copy).then_inc(q_copied, 1)

            def body(before, cur, after):
                for n in range(G):
                    if cur:
                        act.wait_ge(q_ready, G * cur[0] + n + 1)
                        act.wait_ge(ssq_done, G * cur[0] + n + 1)
                        act.activation(squares[:, :], q_bank[n][0:S, :], ACT.Square, scale=float(XHD) ** -0.5).then_inc(squared, 1)
                    late = cur if n >= LAG else before
                    if late:
                        copy_queries(*late, (n - LAG) % G)
                    if n == TURN_X and after:
                        head(after)
                if cur and not before:
                    act.wait_ge(wo_loaded, 16)
                    for n in range(G):
                        act.activation(wo[0][:, n * G:n * G + G, :].rearrange("p h n -> p (h n)"), w_raw[:, n, :], ACT.Copy).then_inc(wo_hi, 1)

            batches(act, head, body)

        @block.vector
        def _(dve):
            for signal, credit in ((qn_done, G), (x_split, 1), (ssq_done, 1)):
                dve.sem_inc(signal, credit)
            for n in range(2):
                dve.sem_inc(q_stored[n], 16)

            def normalize(b, p, half):
                dve.wait_ge(x_loaded[p], 16 * half + 16)
                dve.tensor_scalar(xn[:, :], xin[:, p, :], keep["mv"][:, b, 0:1], keep["rstd"][:, b, :],
                                  ALU.subtract, ALU.mult).then_inc(xn_done, 1)

            def x_lo(b, p, half):
                dve.wait_ge(x_hi, b + 1)
                dve.tensor_tensor(xT[1][:, p, :, :], x_bank[:, 0:DC * S].rearrange("p (c s) -> p c s", c=DC),
                                  f32(xT[0][:, p, :, :]), ALU.subtract).then_inc(x_split, 1)

            def head(cur):
                normalize(*cur)
                x_lo(*cur)
                for c in range(DC):
                    dve.wait_ge(w_hi, c + 1)
                    dve.tensor_tensor(w[1][:, c, :], w_raw[:, c, :], f32(w[0][:, c, :]), ALU.subtract).then_inc(w_split, 1)

            def scale(b, n):
                t = G * b + n + 1
                dve.wait_ge(squared, t)
                dve.tensor_reduce(ssq[:, n % 2, :], squares[:, :].rearrange("p (h d) -> p h d", h=G), axis=AX.X, op=ALU.add).then_inc(ssq_done, 1)
                dve.wait_ge(rq_done, t)
                dve.wait_ge(q_turned, t)
                dve.tensor_tensor(qn[:, n % 2, :].rearrange("p (h d) -> p h d", h=G), q_bank[n][0:S, :].rearrange("p (h d) -> p h d", h=G),
                                  rq[:, n % 2, :].unsqueeze(2).broadcast_to([S, G, XHD]), ALU.mult).then_inc(qn_done, 1)

            def body(before, cur, after):
                for n in range(G):
                    if n == 0 and after:
                        normalize(*after)
                    if cur:
                        scale(cur[0], n)
                    if n == TURN_X and after:
                        x_lo(*after)
                if cur and not before:
                    for n in range(G):
                        dve.wait_ge(wo_hi, n + 1)
                        dve.tensor_tensor(wo[1][:, n * G:n * G + G, :].rearrange("p h n -> p (h n)"), w_raw[:, n, :],
                                          f32(wo[0][:, n * G:n * G + G, :]).rearrange("p h n -> p (h n)"), ALU.subtract).then_inc(wo_split, 1)

            batches(dve, head, body)

        @block.tensor
        def _(pe):
            pe.sem_inc(q_turned, 2)
            ident = keep["ident"]

            def head(cur):
                b = cur[0]
                pe.wait_ge(xn_done, b + 1)
                pe.wait_ge(x_split, b + 1)
                for c in range(DC):
                    last = pe.transpose(x_bank[:, c * S:(c + 1) * S], xn[:, c * P:(c + 1) * P], ident[0:S, 0:S])
                last.then_inc(x_turned, 1)

            def project(b, p, n):
                if n == 0:
                    pe.wait_ge(x_split, b + 1 + 1)
                pe.wait_ge(qn_done, G * b + n + 1)
                for k, (s, r) in enumerate(PASSES):
                    for c in range(DC):
                        last = pe.matmul(q_bank[n][0:S, :], xT[s][:, p, c, :], w[r][:, c, n * D:(n + 1) * D],
                                         start=k == 0 and c == 0, stop=k == len(PASSES) - 1 and c == DC - 1)
                last.then_inc(q_ready, 1)

            def turn(b, n):
                t = G * b + n + 1
                pe.wait_ge(qn_done, t + G)
                pe.wait_ge(q_copied, t)
                for h in range(G):
                    last = pe.transpose(t_bank[n % 2][:, h * S:(h + 1) * S], qn[:, n % 2, h * P:(h + 1) * P], ident[0:S, 0:S])
                last.then_inc(q_turned, 1)

            def body(before, cur, after):
                if cur and not before:
                    pe.wait_ge(w_split, DC)
                for n in range(G):
                    if cur:
                        project(cur[0], cur[1], n)
                    late = cur if n >= LAG else before
                    if late:
                        turn(late[0], (n - LAG) % G)
                    if n == TURN_X and after:
                        head(after)

            batches(pe, head, body)


def phase_c_attention(nc, keep, io, wo):
    AHEAD = 4
    EXPS = 3
    RECIPROCAL = 2
    WEIGH = {2: -1, 6: 0, 10: 1, 14: 2}
    SPLIT_OUT = {3: -1, 7: 0, 11: 1, 15: 2}
    PROJECT = {0: -2, 4: -1, 8: 0, 12: 1}
    FINISH = 5
    SPLIT_V = 3
    SPLIT_K = {4: 0, 6: 1, 8: 2, 10: 3}
    SPLIT_Q = {5: 0, 7: 1, 9: 2, 11: 3}
    with Memory(nc, "c") as m:
        q_raw = m.sb("q_raw", [P, H, S])
        k_raw = m.sb("k_raw", [P, G, TE])
        v_raw = m.sb("v_raw", [KP, KC, D])
        q = [m.sb(f"q_{n}", [P, 2, H, S], F32R) for n in ("hi", "lo")]
        k = [m.sb(f"k_{n}", [P, 2, G, TE], F32R) for n in ("hi", "lo")]
        v = [m.sb(f"v_{n}", [KP, KC, D], F32R) for n in ("hi", "lo")]
        xin = m.sb("xin", [S, 2, D])
        xout = m.sb("xout", [S, 2, D])
        probs = m.sb("probs", [S, AHEAD, T])
        pT = [m.sb(f"pT_{n}", [KP, 2, KC, HPG, S], F32R) for n in ("hi", "lo")]
        oT = [m.sb(f"oT_{n}", [P, 2, HPG, S], F32R) for n in ("hi", "lo")]
        nmax = m.sb("nmax", [S, 2, H])
        sums = m.sb("sums", [S, 2, H])
        rsum = m.sb("rsum", [S, 2, H])
        score = [m.ps(f"score{n}", [P, 512]) for n in range(AHEAD)]
        turned = [m.ps(f"turned{n}", [P, 512]) for n in range(2)]
        outp = m.ps("outp", [P, 512])
        y = m.ps("y", [P, 512])
        q_loaded, k_loaded, v_loaded = m.sem("q_loaded"), m.sem("k_loaded"), m.sem("v_loaded")
        x_loaded = [m.sem(f"x_loaded{n}") for n in range(2)]
        x_stored = [m.sem(f"x_stored{n}") for n in range(2)]
        q_hi, q_split, k_hi, k_split, v_hi, v_split = (m.sem(n) for n in ("q_hi", "q_split", "k_hi", "k_split", "v_hi", "v_split"))
        scores_ready, max_done, probs_ready, rsum_done, scaled = (m.sem(n) for n in ("scores_ready", "max_done", "probs_ready", "rsum_done", "scaled"))
        turned_ready, pT_hi, pT_split = m.sem("turned_ready"), m.sem("pT_hi"), m.sem("pT_split")
        out_ready, o_hi, o_split, y_ready, x_done = (m.sem(n) for n in ("out_ready", "o_hi", "o_split", "y_ready", "x_done"))
        norm = norm_semaphores(m)
        block = m.block()

        def group(slots, h, before, cur):
            if h not in slots:
                return None
            which = before if slots[h] < 0 else cur
            return which and (*which, slots[h] % G)

        @block.sync
        def _(sp):
            def load(b, p, half):
                sp.dma_start(q_raw[:, :, :], io["q1"][b, :, :, :]).then_inc(q_loaded, 16)
                sp.dma_start(k_raw[:, :, :], io["k1"][b, :, :, :]).then_inc(k_loaded, 16)

            def load_rest(b, p, half):
                sp.dma_start(v_raw[:, :, :], io["v1"][b, :, :, :]).then_inc(v_loaded, 16)
                sp.dma_start(xin[:, p, :], io["x2"][b, :, :]).then_inc(x_loaded[p], 16)

            def head(cur):
                load(*cur)
                load_rest(*cur)

            def body(before, cur, after):
                if after:
                    sp.wait_ge(q_split, G * cur[0] + G)
                    sp.wait_ge(k_split, G * cur[0] + G)
                    load(*after)
                if before:
                    b, p, half = before
                    sp.wait_ge(x_done, b + 1 + 1)
                    sp.dma_start(io["x3"][b, :, :], xout[:, p, :]).then_inc(x_stored[p], 16)
                if after:
                    sp.wait_ge(v_split, cur[0] + 1)
                    load_rest(*after)

            batches(sp, head, body)
            for p in range(2):
                sp.wait_ge(x_stored[p], 16 * (B // 2) + 16)

        @block.gpsimd
        def _(pool):
            def scale(b, p, h):
                pool.wait_ge(rsum_done, H * b + h + 1)
                pool.tensor_tensor(probs[:, h % AHEAD, :], probs[:, h % AHEAD, :], rsum[:, p, h:h + 1].broadcast_to([S, T]),
                                   ALU.mult).then_inc(scaled, 1)

            def body(before, cur, after):
                for h in range(H if cur else 0):
                    scale(cur[0], cur[1], h)

            batches(pool, lambda cur: None, body)
            norm_rstd(pool, keep, norm)

        @block.scalar
        def _(act):
            act.sem_inc(probs_ready, AHEAD)

            def queries_hi(b, p, g):
                act.wait_ge(q_loaded, 16 * b + 16)
                act.activation(q[0][:, p, HPG * g:HPG * g + HPG, :], q_raw[:, HPG * g:HPG * g + HPG, :], ACT.Copy).then_inc(q_hi, 1)

            def keys_hi(b, p, g):
                act.wait_ge(k_loaded, 16 * b + 16)
                act.activation(k[0][:, p, g, :], k_raw[:, g, :], ACT.Copy).then_inc(k_hi, 1)

            def head(cur):
                for g in range(G):
                    keys_hi(cur[0], cur[1], g)
                    queries_hi(cur[0], cur[1], g)

            def exps(b, p, h):
                act.wait_ge(max_done, H * b + h + 1)
                act.wait_ge(turned_ready, H * b + h + 1)
                act.activation(probs[:, h % AHEAD, :], score[h % AHEAD][0:S, 0:T], ACT.Exp, bias=nmax[:, p, h:h + 1],
                               accum_out=sums[:, p, h:h + 1]).then_inc(probs_ready, 1)

            def probs_hi(b, h):
                g, j = divmod(h, HPG)
                act.wait_ge(turned_ready, H * b + h + 1 + AHEAD)
                src = turned[h % 2][0:KP, 0:KC * S].rearrange("p (c s) -> p c s", c=KC)
                act.activation(pT[0][:, g % 2, :, j, :], src, ACT.Copy).then_inc(pT_hi, 1)

            def values_hi(b):
                act.wait_ge(v_loaded, 16 * b + 16)
                act.activation(v[0][:, :, :], v_raw[:, :, :], ACT.Copy).then_inc(v_hi, 1)

            def out_hi(b, p, half, g):
                act.wait_ge(out_ready, G * b + g + 1)
                act.activation(oT[0][:, g % 2, :, :], outp[:, 0:HPG * S].rearrange("p (j s) -> p j s", j=HPG), ACT.Copy).then_inc(o_hi, 1)

            def body(before, cur, after):
                if cur and not before:
                    for h in range(EXPS):
                        exps(cur[0], cur[1], h)
                for h in range(H):
                    if cur:
                        probs_hi(cur[0], h)
                        if h + EXPS < H:
                            exps(cur[0], cur[1], h + EXPS)
                        elif after:
                            exps(after[0], after[1], h + EXPS - H)
                    done = group(SPLIT_OUT, h, before, cur)
                    if done:
                        out_hi(*done)
                    if h == SPLIT_V and cur:
                        values_hi(cur[0])
                    if h in SPLIT_K and after:
                        keys_hi(after[0], after[1], SPLIT_K[h])
                    if h in SPLIT_Q and after:
                        queries_hi(after[0], after[1], SPLIT_Q[h])

            batches(act, head, body)

        @block.vector
        def _(dve):
            for signal, credit in ((pT_split, 2), (o_split, 1), (x_done, 1)):
                dve.sem_inc(signal, credit)
            for n in range(2):
                dve.sem_inc(x_stored[n], 16)

            def queries_lo(b, p, g):
                dve.wait_ge(q_hi, G * b + g + 1)
                heads = slice(HPG * g, HPG * g + HPG)
                dve.tensor_tensor(q[1][:, p, heads, :], q_raw[:, heads, :], f32(q[0][:, p, heads, :]), ALU.subtract).then_inc(q_split, 1)

            def keys_lo(b, p, g):
                dve.wait_ge(k_hi, G * b + g + 1)
                dve.tensor_tensor(k[1][:, p, g, :], k_raw[:, g, :], f32(k[0][:, p, g, :]), ALU.subtract).then_inc(k_split, 1)

            def head(cur):
                for g in range(G):
                    keys_lo(cur[0], cur[1], g)
                    queries_lo(cur[0], cur[1], g)

            def maximum(b, p, h):
                dve.wait_ge(scores_ready, H * b + h + 1)
                dve.tensor_reduce(nmax[:, p, h:h + 1], score[h % AHEAD][0:S, 0:T], axis=AX.X, op=ALU.max, negate=True).then_inc(max_done, 1)

            def reciprocal(b, p, h):
                dve.wait_ge(probs_ready, H * b + h + 1 + AHEAD)
                dve.reciprocal(rsum[:, p, h:h + 1], sums[:, p, h:h + 1]).then_inc(rsum_done, 1)

            def probs_lo(b, h):
                g, j = divmod(h, HPG)
                dve.wait_ge(pT_hi, H * b + h + 1)
                src = turned[h % 2][0:KP, 0:KC * S].rearrange("p (c s) -> p c s", c=KC)
                dve.tensor_tensor(pT[1][:, g % 2, :, j, :], src, f32(pT[0][:, g % 2, :, j, :]), ALU.subtract).then_inc(pT_split, 1)

            def values_lo(b):
                dve.wait_ge(v_hi, b + 1)
                dve.tensor_tensor(v[1][:, :, :], v_raw[:, :, :], f32(v[0][:, :, :]), ALU.subtract).then_inc(v_split, 1)

            def out_lo(b, p, half, g):
                dve.wait_ge(o_hi, G * b + g + 1)
                dve.tensor_tensor(oT[1][:, g % 2, :, :], outp[:, 0:HPG * S].rearrange("p (j s) -> p j s", j=HPG),
                                  f32(oT[0][:, g % 2, :, :]), ALU.subtract).then_inc(o_split, 1)

            def finish(b, p, half):
                dve.wait_ge(y_ready, b + 1)
                dve.wait_ge(x_loaded[p], 16 * half + 16)
                dve.wait_ge(x_stored[p], 16 * half + 16)
                dve.scalar_tensor_tensor(out=xout[:, p, :], in0=y[0:S, :], scalar=keep["gates"][0:S, 1:2], in1=xin[:, p, :],
                                         op0=ALU.mult, op1=ALU.add).then_inc(x_done, 1)
                dve.wait_ge(x_done, b + 1 + 1)
                dve.bn_stats(keep["bn"][:, b, :], xout[:, p, :]).then_inc(norm["counted"], 1)

            def body(before, cur, after):
                def ahead(what, n):
                    if n < H:
                        what(cur[0], cur[1], n)
                    elif after:
                        what(after[0], after[1], n - H)

                if cur and not before:
                    for h in range(AHEAD):
                        maximum(cur[0], cur[1], h)
                    for h in range(RECIPROCAL):
                        reciprocal(cur[0], cur[1], h)
                for h in range(H):
                    if cur:
                        ahead(maximum, h + AHEAD)
                        probs_lo(cur[0], h)
                        ahead(reciprocal, h + RECIPROCAL)
                    done = group(SPLIT_OUT, h, before, cur)
                    if done:
                        out_lo(*done)
                    if h == SPLIT_V and cur:
                        values_lo(cur[0])
                    if h == FINISH and before:
                        finish(*before)
                    if h in SPLIT_K and after:
                        keys_lo(after[0], after[1], SPLIT_K[h])
                    if h in SPLIT_Q and after:
                        queries_lo(after[0], after[1], SPLIT_Q[h])

            batches(dve, head, body)
            norm_moments(dve, keep, norm)

        @block.tensor
        def _(pe):
            pe.sem_inc(turned_ready, AHEAD)
            ident = keep["ident"]

            def scores(b, p, h):
                if h == 0:
                    pe.wait_ge(q_split, G * b + G)
                    pe.wait_ge(k_split, G * b + G)
                pe.wait_ge(probs_ready, H * b + h + 1)
                for n, (s, r) in enumerate(PASSES):
                    last = pe.matmul(score[h % AHEAD][0:S, 0:TE], q[s][:, p, h, :], k[r][:, p, h // HPG, :],
                                     start=n == 0, stop=n == len(PASSES) - 1)
                last.then_inc(scores_ready, 1)

            def turn(b, h):
                pe.wait_ge(scaled, H * b + h + 1)
                pe.wait_ge(pT_split, H * b + h + 1)
                for c in range(KC):
                    last = pe.transpose(turned[h % 2][0:KP, c * S:(c + 1) * S], probs[:, h % AHEAD, c * KP:(c + 1) * KP], ident[0:S, 0:S])
                last.then_inc(turned_ready, 1)

            def weigh(b, p, half, g):
                pe.wait_ge(pT_split, H * b + HPG * (g + 1) + 2)
                pe.wait_ge(o_split, G * b + g + 1)
                pe.wait_ge(v_split, b + 1)
                for n, (s, r) in enumerate(PASSES):
                    for c in range(KC):
                        last = pe.matmul(outp[:, 0:HPG * S], v[s][:, c, g * P:(g + 1) * P],
                                         pT[r][:, g % 2, c, :, :].rearrange("p j s -> p (j s)"),
                                         start=n == 0 and c == 0, stop=n == len(PASSES) - 1 and c == KC - 1)
                last.then_inc(out_ready, 1)

            def project(b, p, half, g):
                pe.wait_ge(o_split, G * b + g + 1 + 1)
                if g == 0:
                    pe.wait_ge(x_done, b + 1)
                for n, (s, r) in enumerate(PASSES):
                    for j in range(HPG):
                        last = pe.matmul(y[0:S, :], oT[s][:, g % 2, j, :], wo[r][:, HPG * g + j, :],
                                         start=g == 0 and n == 0 and j == 0, stop=g == G - 1 and n == len(PASSES) - 1 and j == HPG - 1)
                if g == G - 1:
                    last.then_inc(y_ready, 1)

            def body(before, cur, after):
                if cur and not before:
                    for h in range(AHEAD):
                        scores(cur[0], cur[1], h)
                for h in range(H):
                    if cur:
                        turn(cur[0], h)
                        if h + AHEAD < H:
                            scores(cur[0], cur[1], h + AHEAD)
                        elif after:
                            scores(after[0], after[1], h + AHEAD - H)
                    done = group(WEIGH, h, before, cur)
                    if done:
                        weigh(*done)
                    done = group(PROJECT, h, before, cur)
                    if done:
                        project(*done)

            batches(pe, lambda cur: None, body)


def phase_d(nc, keep, io):
    with Memory(nc, "e") as outer:
        qkv = {
            "q": outer.sb("q", [P, G, B * S]),
            "k": outer.sb("k", [P, G, B * S]),
            "v": outer.sb("v", [S, B, D]),
        }
        phase_d_project(nc, keep, io, qkv)
        phase_d_attention(nc, keep, io, qkv)


def phase_d_project(nc, keep, io, qkv):
    THRESHOLD = 0.1
    CLIP = 1e-8
    QS, KS, V0, QL, KL = 0, H * DS, 2 * H * DS, 2 * H * DS + D, 2 * H * DS + D + H * R
    WIDTH = KL + H * R
    BLOCKS = 2 * G + BPG
    NEXT = 2
    with Memory(nc, "g") as m:
        raw = m.sb("raw", [P, WIDTH])
        wf = m.sb("wf", [P, 3 * D])
        low = m.sb("low", [P, 2, H, R])
        w = [m.sb(f"w_{n}", [P, DC, 3 * D], F32R) for n in ("hi", "lo")]
        head_raw = m.sb("head_raw", [P, 2, H])
        head_clip = m.sb("head_clip", [P, 2, H])
        head_scale = m.sb("head_scale", [P, 2, H])
        half = m.sb("half", [P, 2, H])
        swap = m.sb("swap", [P, H, R], U8)
        xin = m.sb("xin", [S, BPG, D])
        xn = m.sb("xn", [S, BPG, D])
        xT = [m.sb(f"xT_{n}", [P, 2, DC, GS], F32R) for n in ("hi", "lo")]
        x_bank = [m.ps(f"x_bank{n}", [P, 512]) for n in range(2)]
        out_bank = [m.ps(f"out_bank{n}", [P, 512]) for n in range(4)]
        head_loaded, clipped, scaled, swapped, w_loaded = (m.sem(n) for n in ("head_loaded", "clipped", "scaled", "swapped", "w_loaded"))
        low_done, w_done, w_chosen, w_hi, w_split = (m.sem(n) for n in ("low_done", "w_done", "w_chosen", "w_hi", "w_split"))
        x_loaded, xn_done, x_turned, x_hi, x_split = (m.sem(n) for n in ("x_loaded", "xn_done", "x_turned", "x_hi", "x_split"))
        ready, copied = m.sem("ready"), [m.sem(f"copied{n}") for n in range(2)]
        block = m.block()

        def groups(eng, head, body):
            head((0, 0))
            body((0, 0), (1, 1))
            with eng.Fori(0, NG // 2 - 1) as i:
                body((2 * i + 1, 1), (2 * i + 2, 0))
                body((2 * i + 2, 0), (2 * i + 3, 1))
            body((NG - 1, 1), None)

        @block.sync
        def _(sp):
            for n, name in enumerate(("w_std", "w_rec")):
                with nc.allow_non_contiguous_dma(reason="a few words"):
                    sp.dma_start(head_raw[:, n, :], io[name].rearrange("(a n) -> a n", a=1).broadcast_to([P, H])).then_inc(head_loaded, 16)

            def head(cur):
                if not isinstance(cur[0], int) or cur[0] > 0:
                    sp.wait_ge(xn_done, cur[0])
                first = BPG * cur[0]
                sp.dma_start(xin[:, :, :], io["x3"][bass.ds(first, BPG), :, :].rearrange("b s d -> s b d")).then_inc(x_loaded, 16)
                if isinstance(cur[0], int) and cur[0] == 0:
                    for c in range(DC):
                        if c:
                            sp.wait_ge(w_split, c)
                        sp.dma_start(raw[:, :], io["Wa"].rearrange("(c p) n -> c p n", p=P)[c, :, :]).then_inc(w_loaded, 16)

            groups(sp, head, lambda cur, after: after and head(after))

        @block.gpsimd
        def _(pool):
            pool.memset(half[:, :, :], 0.5).then_inc(clipped, 1)
            pool.wait_ge(clipped, 2)
            pool.tensor_tensor(head_scale[:, :, :], head_clip[:, :, :], half[:, :, :], ALU.pow).then_inc(scaled, 1)

        def columns(first, width):
            return wf[:, first:first + D].rearrange("p (h d) -> p h d", h=H)[:, :, width]

        @block.scalar
        def _(act):
            act.sem_inc(copied[0], 2)
            for c in range(DC):
                act.wait_ge(w_chosen, 2 * c + 2)
                act.activation(w[0][:, c, 0:2 * D], wf[:, 0:2 * D], ACT.Copy).then_inc(w_hi, 1)
                act.activation(w[0][:, c, 2 * D:], raw[:, V0:V0 + D], ACT.Copy).then_inc(w_hi, 1)

            def head(cur):
                for c in range(DC):
                    act.wait_ge(x_turned, DC * cur[0] + c + 1)
                    act.activation(xT[0][:, cur[1], c, :], x_bank[c % 2][:, 0:GS], ACT.Copy).then_inc(x_hi, 1)

            def body(cur, after):
                g = cur[0]
                for n in range(0, BLOCKS, 2):
                    act.wait_ge(ready, BLOCKS * g + n + 1)
                    if n < G:
                        act.activation(qkv["q"][:, n, bass.ds(g * GS, GS)], out_bank[n % 4][:, 0:GS], ACT.Copy,
                                       scale=float(HD) ** -0.5).then_inc(copied[0], 1)
                    elif n < 2 * G:
                        act.activation(qkv["k"][:, n - G, bass.ds(g * GS, GS)], out_bank[n % 4][:, 0:GS], ACT.Copy).then_inc(copied[0], 1)
                    else:
                        act.activation(qkv["v"][:, BPG * g + n - 2 * G, :], out_bank[n % 4][0:S, :], ACT.Copy).then_inc(copied[0], 1)
                    if n == NEXT and after:
                        head(after)

            groups(act, head, body)

        @block.vector
        def _(dve):
            dve.sem_inc(copied[1], 2)
            dve.sem_inc(x_split, 2)
            dve.wait_ge(head_loaded, 32)
            dve.tensor_scalar(head_clip[:, :, :], head_raw[:, :, :], CLIP, None, ALU.max).then_inc(clipped, 1)
            dve.tensor_scalar(swap[:, :, :], head_raw[:, 1, :].unsqueeze(2).broadcast_to([P, H, R]), THRESHOLD, None, ALU.is_gt).then_inc(swapped, 1)

            def head(cur):
                g = cur[0]
                dve.wait_ge(x_loaded, 16 * g + 16)
                for n in range(BPG):
                    b = BPG * g + n
                    last = dve.tensor_scalar(xn[:, n, :], xin[:, n, :], keep["mv"][:, b, 0:1], keep["rstd"][:, b, :],
                                             ALU.subtract, ALU.mult)
                last.then_inc(xn_done, 1)
                for c in range(DC):
                    dve.wait_ge(x_hi, DC * g + c + 1)
                    dve.tensor_tensor(xT[1][:, cur[1], c, :], x_bank[c % 2][:, 0:GS], f32(xT[0][:, cur[1], c, :]), ALU.subtract).then_inc(x_split, 1)

            def weights():
                for c in range(DC):
                    dve.wait_ge(scaled, 1)
                    dve.wait_ge(w_loaded, 16 * c + 16)
                    for n, first in enumerate((QL, KL)):
                        dve.tensor_tensor(low[:, n, :, :], raw[:, first:first + H * R].rearrange("p (h r) -> p h r", h=H),
                                          head_scale[:, 1, :].unsqueeze(2).broadcast_to([P, H, R]), ALU.mult).then_inc(low_done, 1)
                    for n, first in enumerate((QS, KS)):
                        dve.tensor_tensor(columns(n * D, slice(0, DS)), raw[:, first:first + H * DS].rearrange("p (h d) -> p h d", h=H),
                                          head_scale[:, 0, :].unsqueeze(2).broadcast_to([P, H, DS]), ALU.mult)
                    dve.wait_ge(low_done, 2 * c + 2)
                    for n in range(2):
                        dve.tensor_copy(columns(n * D, slice(DS, HD)), low[:, n, :, :]).then_inc(w_done, 1)
                    dve.wait_ge(w_done, 2 * c + 2)
                    dve.wait_ge(swapped, 1)
                    for n in range(2):
                        dve.copy_predicated(columns(n * D, slice(DS, HD)), swap[:, :, :], low[:, 1 - n, :, :]).then_inc(w_chosen, 1)
                    dve.wait_ge(w_hi, 2 * c + 2)
                    dve.tensor_tensor(w[1][:, c, 0:2 * D], wf[:, 0:2 * D], f32(w[0][:, c, 0:2 * D]), ALU.subtract)
                    dve.tensor_tensor(w[1][:, c, 2 * D:], raw[:, V0:V0 + D], f32(w[0][:, c, 2 * D:]), ALU.subtract).then_inc(w_split, 1)

            def body(cur, after):
                g = cur[0]
                for n in range(1, BLOCKS, 2):
                    dve.wait_ge(ready, BLOCKS * g + n + 1)
                    if n < G:
                        dve.tensor_scalar(qkv["q"][:, n, bass.ds(g * GS, GS)], out_bank[n % 4][:, 0:GS], float(HD) ** -0.5, None,
                                          ALU.mult).then_inc(copied[1], 1)
                    elif n < 2 * G:
                        dve.tensor_copy(qkv["k"][:, n - G, bass.ds(g * GS, GS)], out_bank[n % 4][:, 0:GS]).then_inc(copied[1], 1)
                    else:
                        dve.tensor_copy(qkv["v"][:, BPG * g + n - 2 * G, :], out_bank[n % 4][0:S, :]).then_inc(copied[1], 1)
                    if n == NEXT - 1 and after:
                        head(after)

            weights()
            groups(dve, head, body)

        @block.tensor
        def _(pe):
            ident = keep["ident"]

            def head(cur):
                g = cur[0]
                pe.wait_ge(xn_done, g + 1)
                for c in range(DC):
                    pe.wait_ge(x_split, DC * g + c + 1)
                    for n in range(BPG):
                        last = pe.transpose(x_bank[c % 2][:, n * S:(n + 1) * S], xn[:, n, c * P:(c + 1) * P], ident[0:S, 0:S])
                    last.then_inc(x_turned, 1)

            def body(cur, after):
                g, p = cur
                if isinstance(g, int) and g == 0:
                    pe.wait_ge(w_split, DC)
                pe.wait_ge(x_split, DC * g + DC + 2)
                for n in range(BLOCKS):
                    pe.wait_ge(copied[n % 2], BLOCKS // 2 * g + n // 2 + 1)
                    for k, (s, r) in enumerate(PASSES):
                        for c in range(DC):
                            flags = dict(start=k == 0 and c == 0, stop=k == len(PASSES) - 1 and c == DC - 1)
                            if n < 2 * G:
                                last = pe.matmul(out_bank[n % 4][:, 0:GS], w[s][:, c, n * P:(n + 1) * P], xT[r][:, p, c, :], **flags)
                            else:
                                b = n - 2 * G
                                last = pe.matmul(out_bank[n % 4][0:S, :], xT[s][:, p, c, b * S:(b + 1) * S], w[r][:, c, 2 * D:], **flags)
                    last.then_inc(ready, 1)
                    if n == NEXT and after:
                        head(after)

            groups(pe, head, body)


def phase_d_attention(nc, keep, io, qkv):
    AHEAD = 2
    LOWEST = -3.4028234663852886e38
    SPLIT_K = {0: (0, 1), 1: (2, 3)}
    with Memory(nc, "d") as m:
        wp_raw = m.sb("wp_raw", [P, DC, D])
        wp = [m.sb(f"wp_{n}", [P, DC, D], F32R) for n in ("hi", "lo")]
        lowest = m.sb("lowest", [S, S])
        q = [m.sb(f"q_{n}", [P, 2, G, S], F32R) for n in ("hi", "lo")]
        k = [m.sb(f"k_{n}", [P, 2, G, HPG, S], F32R) for n in ("hi", "lo")]
        probs = m.sb("probs", [S, 2, HPG, S])
        pT = m.sb("pT", [S, 2, HPG, S])
        nmax = m.sb("nmax", [S, 2, H])
        sums = m.sb("sums", [S, 2, H])
        rsum = m.sb("rsum", [S, H])
        on = m.sb("on", [S, D])
        oT = [m.sb(f"oT_{n}", [P, DC, S], F32R) for n in ("hi", "lo")]
        xin = m.sb("xin", [S, 2, D])
        xout = m.sb("xout", [S, 2, D])
        score = [m.ps(f"score{n}", [P, 512]) for n in range(G)]
        turned = [m.ps(f"turned{n}", [P, 512]) for n in range(2)]
        outp = m.ps("outp", [P, 512])
        tail = m.ps("tail", [P, 512])
        wp_loaded, wp_hi, wp_split, cleared = m.sem("wp_loaded"), m.sem("wp_hi"), m.sem("wp_split"), m.sem("cleared")
        x_loaded = [m.sem(f"x_loaded{n}") for n in range(2)]
        x_stored = [m.sem(f"x_stored{n}") for n in range(2)]
        q_hi, q_split, k_hi, k_split = m.sem("q_hi"), m.sem("q_split"), m.sem("k_hi"), m.sem("k_split")
        scores_ready, masked, max_done, probs_ready = (m.sem(n) for n in ("scores_ready", "masked", "max_done", "probs_ready"))
        turned_ready, pT_copied, out_ready, rsum_done, on_done = (m.sem(n) for n in ("turned_ready", "pT_copied", "out_ready", "rsum_done", "on_done"))
        o_turned, o_hi, o_split, y_ready, x_done = (m.sem(n) for n in ("o_turned", "o_hi", "o_split", "y_ready", "x_done"))
        block = m.block()

        @block.sync
        def _(sp):
            sp.dma_start(wp_raw[:, :, :], io["Wp"].rearrange("(c p) n -> p c n", p=P)).then_inc(wp_loaded, 16)

            def load(b, p, half):
                sp.dma_start(xin[:, p, :], io["x3"][b, :, :]).then_inc(x_loaded[p], 16)

            def body(before, cur, after):
                if before:
                    b, p, half = before
                    sp.wait_ge(x_done, b + 1 + 1)
                    sp.dma_start(io["out"][b, :, :], xout[:, p, :]).then_inc(x_stored[p], 16)
                if after:
                    load(*after)

            batches(sp, lambda cur: load(*cur), body)
            for p in range(2):
                sp.wait_ge(x_stored[p], 16 * (B // 2) + 16)

        @block.gpsimd
        def _(pool):
            for part in k:
                pool.memset(f32(part[:, :, :, :, :]), 0.0).then_inc(cleared, 1)
            pool.memset(lowest[:, :], LOWEST).then_inc(cleared, 1)
            pool.wait_ge(cleared, 3)

            def keys_lo(b, p, j):
                pool.wait_ge(k_hi, HPG * b + j + 1)
                r = slice(HD * j, HD * j + HD)
                pool.tensor_tensor(k[1][r, p, :, j, :], qkv["k"][r, :, bass.ds(b * S, S)], f32(k[0][r, p, :, j, :]), ALU.subtract).then_inc(k_split, 1)

            def head(cur):
                for j in range(HPG):
                    keys_lo(cur[0], cur[1], j)

            batches(pool, head, lambda before, cur, after: after and head(after))

        @block.scalar
        def _(act):
            act.sem_inc(probs_ready, G)
            act.wait_ge(cleared, 3)

            def keys_hi(b, p, j):
                r = slice(HD * j, HD * j + HD)
                act.activation(k[0][r, p, :, j, :], qkv["k"][r, :, bass.ds(b * S, S)], ACT.Copy).then_inc(k_hi, 1)

            def queries_hi(b, p):
                act.activation(q[0][:, p, :, :], qkv["q"][:, :, bass.ds(b * S, S)], ACT.Copy).then_inc(q_hi, 1)

            def head(cur):
                queries_hi(cur[0], cur[1])
                for j in range(HPG):
                    keys_hi(cur[0], cur[1], j)

            def exps(b, p, g):
                t = G * b + g + 1
                act.wait_ge(max_done, t)
                act.wait_ge(turned_ready, t)
                for j in range(HPG):
                    h = HPG * g + j
                    last = act.activation(probs[:, g % 2, j, :], score[g][0:S, j * S:(j + 1) * S], ACT.Exp,
                                          bias=nmax[:, p, h:h + 1], accum_out=sums[:, p, h:h + 1])
                last.then_inc(probs_ready, 1)

            def body(before, cur, after):
                if cur and not before:
                    exps(cur[0], cur[1], 0)
                for g in range(G):
                    if cur and g < G - 1:
                        exps(cur[0], cur[1], g + 1)
                    elif after and g == G - 1:
                        exps(after[0], after[1], 0)
                    if g == 0 and after:
                        queries_hi(after[0], after[1])
                    for j in SPLIT_K.get(g, ()) if after else ():
                        keys_hi(after[0], after[1], j)
                    if g == 1 and before:
                        act.wait_ge(o_turned, before[0] + 1)
                        act.activation(oT[0][:, :, :], tail[:, 0:DC * S].rearrange("p (c s) -> p c s", c=DC), ACT.Copy).then_inc(o_hi, 1)
                if cur and not before:
                    act.wait_ge(wp_loaded, 16)
                    act.activation(wp[0][:, :, :], wp_raw[:, :, :], ACT.Copy).then_inc(wp_hi, 1)

            batches(act, head, body)

        @block.vector
        def _(dve):
            for signal, credit in ((on_done, 1), (x_done, 1), (pT_copied, 2)):
                dve.sem_inc(signal, credit)
            for n in range(2):
                dve.sem_inc(x_stored[n], 16)

            def queries_lo(b, p):
                dve.wait_ge(q_hi, b + 1)
                dve.tensor_tensor(q[1][:, p, :, :], qkv["q"][:, :, bass.ds(b * S, S)], f32(q[0][:, p, :, :]), ALU.subtract).then_inc(q_split, 1)

            def maximum(b, p, g):
                t = G * b + g + 1
                four = score[g][0:S, 0:HPG * S].rearrange("p (j s) -> p j s", j=HPG)
                t = t if isinstance(t, int) else dve.to_reg(t)
                dve.wait_ge(cleared, 3)
                dve.wait_ge(scores_ready, t)
                dve.copy_predicated(four, keep["later"][:, :].unsqueeze(1).broadcast_to([S, HPG, S]),
                                    lowest[:, :].unsqueeze(1).broadcast_to([S, HPG, S])).then_inc(masked, 1)
                dve.wait_ge(masked, G * b + g + 1)
                dve.tensor_reduce(nmax[:, p, HPG * g:HPG * g + HPG], four, axis=AX.X, op=ALU.max, negate=True).then_inc(max_done, 1)

            def probs_copy(b, g):
                t = G * b + g + 1
                dve.wait_ge(turned_ready, t + 2)
                dve.tensor_copy(pT[:, g % 2, :, :], turned[g % 2][0:S, 0:HPG * S].rearrange("p (j s) -> p j s", j=HPG)).then_inc(pT_copied, 1)

            def normalize_out(b, p, half):
                dve.wait_ge(probs_ready, G * b + G + G)
                dve.reciprocal(rsum[:, :], sums[:, p, :]).then_inc(rsum_done, 1)
                dve.wait_ge(out_ready, b + 1)
                dve.wait_ge(rsum_done, b + 1)
                dve.tensor_tensor(on[:, :].rearrange("p (h d) -> p h d", h=H), outp[0:S, :].rearrange("p (h d) -> p h d", h=H),
                                  rsum[:, :].unsqueeze(2).broadcast_to([S, H, HD]), ALU.mult).then_inc(on_done, 1)

            def out_lo(b, p, half):
                dve.wait_ge(o_hi, b + 1)
                dve.tensor_tensor(oT[1][:, :, :], tail[:, 0:DC * S].rearrange("p (c s) -> p c s", c=DC), f32(oT[0][:, :, :]),
                                  ALU.subtract).then_inc(o_split, 1)

            def finish(b, p, half):
                dve.wait_ge(y_ready, b + 1)
                dve.wait_ge(x_loaded[p], 16 * half + 16)
                dve.wait_ge(x_stored[p], 16 * half + 16)
                dve.scalar_tensor_tensor(out=xout[:, p, :], in0=tail[0:S, :], scalar=keep["gates"][0:S, 3:4], in1=xin[:, p, :],
                                         op0=ALU.mult, op1=ALU.add).then_inc(x_done, 1)

            def body(before, cur, after):
                if cur and not before:
                    for g in range(AHEAD):
                        maximum(cur[0], cur[1], g)
                for g in range(G):
                    if g == 0 and after:
                        queries_lo(after[0], after[1])
                    if cur and g + AHEAD < G:
                        maximum(cur[0], cur[1], g + AHEAD)
                    elif after and g + AHEAD >= G:
                        maximum(after[0], after[1], g + AHEAD - G)
                    if cur:
                        probs_copy(cur[0], g)
                    if before:
                        if g == 0:
                            normalize_out(*before)
                        elif g == 1:
                            out_lo(*before)
                        elif g == 3:
                            finish(*before)
                if cur and not before:
                    dve.wait_ge(wp_hi, 1)
                    dve.tensor_tensor(wp[1][:, :, :], wp_raw[:, :, :], f32(wp[0][:, :, :]), ALU.subtract).then_inc(wp_split, 1)

            batches(dve, lambda cur: queries_lo(cur[0], cur[1]), body)

        @block.tensor
        def _(pe):
            pe.sem_inc(turned_ready, 2)
            ident = keep["ident"]

            def scores(b, p, g):
                if g == 0:
                    pe.wait_ge(q_split, b + 1)
                    pe.wait_ge(k_split, HPG * b + HPG)
                pe.wait_ge(probs_ready, G * b + g + 1)
                for n, (s, r) in enumerate(PASSES):
                    last = pe.matmul(score[g][0:S, 0:HPG * S], q[s][:, p, g, :], k[r][:, p, g, :, :].rearrange("p j s -> p (j s)"),
                                     start=n == 0, stop=n == len(PASSES) - 1)
                last.then_inc(scores_ready, 1)

            def turn(b, g):
                t = G * b + g + 1
                pe.wait_ge(probs_ready, t + G)
                pe.wait_ge(pT_copied, t)
                for j in range(HPG):
                    last = pe.transpose(turned[g % 2][0:S, j * S:(j + 1) * S], probs[:, g % 2, j, :], ident[0:S, 0:S])
                last.then_inc(turned_ready, 1)

            def weigh(b, g):
                pe.wait_ge(pT_copied, G * b + g + 1 + 2)
                if g == 0:
                    pe.wait_ge(on_done, b + 1)
                for j in range(HPG):
                    h = HPG * g + j
                    last = pe.matmul(outp[0:S, h * HD:(h + 1) * HD], pT[:, g % 2, j, :], qkv["v"][:, b, h * HD:(h + 1) * HD],
                                     start=True, stop=True)
                if g == G - 1:
                    last.then_inc(out_ready, 1)

            def turn_out(b):
                pe.wait_ge(on_done, b + 1 + 1)
                pe.wait_ge(x_done, b + 1)
                for c in range(DC):
                    last = pe.transpose(tail[:, c * S:(c + 1) * S], on[:, c * P:(c + 1) * P], ident[0:S, 0:S])
                last.then_inc(o_turned, 1)

            def project(b):
                pe.wait_ge(wp_split, 1)
                pe.wait_ge(o_split, b + 1)
                for n, (s, r) in enumerate(PASSES):
                    for c in range(DC):
                        last = pe.matmul(tail[0:S, :], oT[s][:, c, :], wp[r][:, c, :], start=n == 0 and c == 0,
                                         stop=n == len(PASSES) - 1 and c == DC - 1)
                last.then_inc(y_ready, 1)

            def body(before, cur, after):
                if cur and not before:
                    for g in range(AHEAD):
                        scores(cur[0], cur[1], g)
                for g in range(G):
                    if cur and g + AHEAD < G:
                        scores(cur[0], cur[1], g + AHEAD)
                    elif after and g + AHEAD >= G:
                        scores(after[0], after[1], g + AHEAD - G)
                    if cur:
                        turn(cur[0], g)
                    if before:
                        if g == 0:
                            weigh(before[0], G - 1)
                        elif g == 1:
                            turn_out(before[0])
                        elif g == 2:
                            project(before[0])
                    if cur and g > 0:
                        weigh(cur[0], g - 1)

            batches(pe, lambda cur: None, body)


def flamingo_layers(nc, ins, out):
    io = dict(ins, out=out)
    for name in ("x1", "x2", "x3"):
        io[name] = nc.dram_tensor(name, [B, S, D], F32).ap()
    io["k1"] = nc.dram_tensor("k1", [B, P, G, TE], F32).ap()
    io["v1"] = nc.dram_tensor("v1", [B, KP, KC, D], F32).ap()
    io["q1"] = nc.dram_tensor("q1", [B, P, H, S], F32).ap()
    with Memory(nc, "keep") as m:
        keep = constants(m)
        setup_phase(nc, keep, io)
        phase_a(nc, keep, io)
        phase_b(nc, keep, io)
        phase_c(nc, keep, io)
        phase_d(nc, keep, io)


_INS = {"x": "x", "ctx": "ctx_2048", "g_xattn": "g_xattn", "g_ffn": "g_ffn"}
for _layer, _names in (("L0_ffn", ("SU_ug", "SU_dp", "Wscale_ug", "Wscale_dp", "W_up", "W_gate", "W_down")),
                       ("L1_xattn", ("Wq", "Wk", "Wv", "Wo", "q_norm_w", "k_norm_w")),
                       ("L1_ffn", ("Wa", "Wp", "w_std", "w_rec"))):
    for _name in _names:
        _INS[_name] = f"{_layer}_{_name}"


def kernel(**inputs):
    import numpy as _np
    import concourse.bacc as _bacc
    from concourse import mybir as _mybir
    from concourse.bass_utils import run_bass_kernel_spmd as _run

    nc = _bacc.Bacc("TRN2", target_bir_lowering=False, num_devices=1)
    arrays, ins = {}, {}
    for short, name in _INS.items():
        a = _np.ascontiguousarray(inputs[name])
        arrays[f"in_{name}_dram"] = a
        ins[short] = nc.dram_tensor(f"in_{name}_dram", a.shape, _mybir.dt.from_np(a.dtype), kind="ExternalInput").ap()
    out = nc.dram_tensor("out_0_dram", (B, S, D), F32, kind="ExternalOutput").ap()
    flamingo_layers(nc, ins, out)
    r = _run(nc, [arrays], core_ids=[0])
    return r.results[0]["out_0_dram"]
```

```python
from contextlib import ExitStack

import concourse.bass as bass
from concourse import mybir

F32 = mybir.dt.float32
F32R = mybir.dt.float32r
U8 = mybir.dt.uint8
ALU = mybir.AluOpType
ACT = mybir.ActivationFunctionType
AX = mybir.AxisListType

B, S, T, D = 16, 112, 375, 512
P = 128
DC = D // P
H = 16
HD = D // H
G = 4
HPG = H // G
KC, KP = 3, T // 3
TE = T + 1
XHD = 128
INTER = 2048
R = 8
DS = HD - R
LN_EPS = 1e-5
RMS_EPS = 1e-6
PASSES = ((0, 0), (0, 1), (1, 0))


def f32(ap):
    return ap.bitcast(F32)


class Memory:

    def __init__(self, nc, phase):
        self.nc, self.phase, self.stack = nc, phase, ExitStack()

    def __enter__(self):
        self.semaphores = []
        self.stack.__enter__()
        return self

    def __exit__(self, *what):
        done = self.stack.__exit__(*what)
        if self.semaphores:
            self.nc.clear_and_free_semaphores(self.semaphores)
            self.nc.all_engine_barrier()
        return done

    def sb(self, name, shape, dt=F32):
        return self.stack.enter_context(self.nc.sbuf_tensor(f"{self.phase}_{name}", shape, dt))

    def ps(self, name, shape, dt=F32):
        return self.stack.enter_context(self.nc.psum_tensor(f"{self.phase}_{name}", shape, dt))

    def sem(self, name):
        self.semaphores.append(self.nc.alloc_semaphore(f"{self.phase}_{name}"))
        return self.semaphores[-1]

    def block(self):
        return self.stack.enter_context(self.nc.Block())


def batches(eng, head, body):
    head((0, 0, 0))
    body(None, (0, 0, 0), (1, 1, 0))
    with eng.Fori(0, B // 2 - 1) as i:
        body((2 * i, 0, i), (2 * i + 1, 1, i), (2 * i + 2, 0, i + 1))
        body((2 * i + 1, 1, i), (2 * i + 2, 0, i + 1), (2 * i + 3, 1, i + 1))
    last = B // 2 - 1
    body((B - 2, 0, last), (B - 1, 1, last), None)
    body((B - 1, 1, last), None, None)


def constants(m):
    return {
        "ident": m.sb("ident", [P, P]),
        "hadamard": m.sb("hadamard", [P, P]),
        "neghalf": m.sb("neghalf", [P, H]),
        "rms_eps": m.sb("rms_eps", [P, G]),
        "ln_eps": m.sb("ln_eps", [P, 1]),
        "later": m.sb("later", [S, S], U8),
        "masked_score": m.sb("masked_score", [S, S]),
        "gates": m.sb("gates", [P, 4]),
        "qk_w": m.sb("qk_w", [P, 1]),
        "bn": m.sb("bn", [S, B, 6]),
        "mv": m.sb("mv", [S, B, 2]),
        "ve": m.sb("ve", [S, B]),
        "rstd": m.sb("rstd", [S, B, 1]),
    }


def setup_phase(nc, keep, io):
    with Memory(nc, "s") as m:
        qw = m.sb("qw", [P, 2])
        gate_raw = m.sb("gate_raw", [P, 4])
        had_tmp = m.sb("had_tmp", [P, P])
        ones, later = m.sb("ones", [P, P]), m.sb("later", [S, S])
        zeroed, made, w_loaded = m.sem("zeroed"), m.sem("made"), m.sem("w_loaded")
        block = m.block()

        @block.sync
        def _(sp):
            with nc.allow_non_contiguous_dma(reason="a few words"):
                sp.dma_start(qw[:, 0:1], io["q_norm_w"].rearrange("(p a) -> p a", a=1)).then_inc(w_loaded, 16)
                sp.dma_start(qw[:, 1:2], io["k_norm_w"].rearrange("(p a) -> p a", a=1)).then_inc(w_loaded, 16)
                for n, name in enumerate(("g_xattn", "g_ffn")):
                    row = io[name].rearrange("(a n) -> a n", a=1)
                    sp.dma_start(gate_raw[:, 2 * n:2 * n + 2], row.broadcast_to([P, 2])).then_inc(w_loaded, 16)

        @block.gpsimd
        def _(pool):
            pool.memset(keep["ident"][:, :], 0.0).then_inc(zeroed, 1)
            pool.memset(ones[:, :], 1.0).then_inc(zeroed, 1)
            pool.memset(keep["neghalf"][:, :], -0.5).then_inc(zeroed, 1)
            pool.memset(keep["rms_eps"][:, :], RMS_EPS).then_inc(zeroed, 1)
            pool.memset(keep["ln_eps"][:, :], LN_EPS).then_inc(zeroed, 1)
            pool.wait_ge(zeroed, 5)
            pool.affine_select(out=keep["ident"][:, :], in_=keep["ident"][:, :], compare_op=ALU.not_equal, fill=1.0,
                               base=0, pattern=[[-1, P]], channel_multiplier=1).then_inc(made, 1)
            pool.affine_select(out=later[:, :], in_=ones[0:S, 0:S], compare_op=ALU.is_gt, fill=0.0,
                               base=0, pattern=[[1, S]], channel_multiplier=-1).then_inc(made, 1)

        @block.scalar
        def _(act):
            act.wait_ge(w_loaded, 64)
            act.activation(keep["gates"][:, :], gate_raw[:, :], ACT.Tanh)

        @block.vector
        def _(dve):
            dve.wait_ge(w_loaded, 64)
            dve.scalar_tensor_tensor(out=keep["qk_w"][:, :], in0=qw[:, 0:1], scalar=float(XHD) ** -0.5, in1=qw[:, 1:2],
                                     op0=ALU.mult, op1=ALU.mult)
            dve.memset(keep["masked_score"][:, :], -10000.0)
            dve.wait_ge(made, 2)
            dve.tensor_copy(keep["later"][:, :], later[:, :])
            stages = P.bit_length() - 1
            src = keep["ident"]
            for stage in range(stages):
                dst = had_tmp if (stages - stage) % 2 == 0 else keep["hadamard"]
                dve.wait_ge(made, 2 + 2 * stage)
                pair, out = (t[:, :].rearrange("p (a two n) -> p a two n", two=2, n=1 << stage) for t in (src, dst))
                dve.tensor_tensor(out[:, :, 0, :], pair[:, :, 0, :], pair[:, :, 1, :], ALU.add).then_inc(made, 1)
                dve.tensor_tensor(out[:, :, 1, :], pair[:, :, 0, :], pair[:, :, 1, :], ALU.subtract).then_inc(made, 1)
                src = dst


def norm_semaphores(m):
    return {name: m.sem(name) for name in ("counted", "moments", "shifted")}


def norm_moments(dve, keep, norm):
    dve.wait_ge(norm["counted"], B)
    for b in range(B):
        dve.bn_aggr(keep["mv"][:, b, :], keep["bn"][:, b, :]).then_inc(norm["moments"], 1)
    dve.wait_ge(norm["moments"], B)
    dve.tensor_scalar(keep["ve"][:, :], keep["mv"][:, :, 1], LN_EPS, None, ALU.add).then_inc(norm["shifted"], 1)


def norm_rstd(pool, keep, norm):
    pool.wait_ge(norm["shifted"], 1)
    pool.tensor_tensor(keep["rstd"][:, :, 0], keep["ve"][:, :], keep["neghalf"][0:S, 0:B], ALU.pow)


def phase_a(nc, keep, io):
    FILL = ((0, ("k", 0), 0), (1, ("ctx", 0), 1), (2, ("v", 0), 2), (3, ("back", 0), 1), (4, ("k", 1), 0), (4, ("kt", 0), 2),
            (5, ("ctx", 1), 1), (7, ("v", 1), 2), (8, ("ctx", 2), 0), (8, ("kt", 1), 1), (9, ("q", 0), 2), (11, ("k", 2), 0),
            (13, ("v", 2), 1), (14, ("kt", 2), 2))
    ITEMS = [what for _, what, _ in FILL]
    BANK = {what: n for _, what, n in FILL}
    NEXT, BEFORE = ("ctx", "q"), ("back",)
    SQUARE_K = {1: 0, 5: 1, 12: 2}
    SUM_K = {2: 0, 6: 1, 12: 2}
    SCALE_K = {3: 0, 7: 1, 13: 2}
    WEIGH = {1: -1, 6: 0, 10: 1, 14: 2}
    COPY = {2: -1, 7: 0, 11: 1, 15: 2}
    SPLIT_V = 11
    MOMENTS, NORMALIZE = 7, 8
    FINISH = 4
    AHEAD = 2
    EXPS = 1
    PROBS = 4
    with Memory(nc, "a") as m:
        w_raw = m.sb("w_raw", [P, DC, 2 * D])
        w = [m.sb(f"w_{n}", [P, DC, 2 * D], F32R) for n in ("hi", "lo")]
        xin = m.sb("xin", [S, 2, D])
        xn = m.sb("xn", [S, D])
        x_bn = m.sb("x_bn", [S, 2, 6])
        x_mv = m.sb("x_mv", [S, 2, 2])
        x_ve = m.sb("x_ve", [S, 2])
        x_rstd = m.sb("x_rstd", [S, 2])
        ctx = m.sb("ctx", [KP, 2, KC, D])
        v = [m.sb(f"v_{n}", [KP, 2, KC, D], F32R) for n in ("hi", "lo")]
        kT = [m.sb(f"kT_{n}", [P, 2, DC, TE], F32R) for n in ("hi", "lo")]
        q = [m.sb(f"q_{n}", [P, 2, G, HPG, S], F32R) for n in ("hi", "lo")]
        probs = m.sb("probs", [S, PROBS, T])
        pT = [m.sb(f"pT_{n}", [KP, 2, KC, HPG, S], F32R) for n in ("hi", "lo")]
        oT = m.sb("oT", [P, G, S])
        xout = m.sb("xout", [S, 2, D])
        kraw = m.sb("kraw", [KP, 2, D])
        kn = m.sb("kn", [KP, 2, D])
        vout = m.sb("vout", [KP, KC, D])
        kout = m.sb("kout", [P, DC, TE])
        squares = m.sb("squares", [KP, D])
        ssq = m.sb("ssq", [KP, 2, G])
        ssq_eps = m.sb("ssq_eps", [KP, 2, G])
        rk = m.sb("rk", [KP, 2, G])
        nmax = m.sb("nmax", [S, 2, H])
        sums = m.sb("sums", [S, 2, H])
        rsum = m.sb("rsum", [S, H])
        tmp = m.sb("tmp", [S, D])

        score = [m.ps(f"score{n}", [P, 512]) for n in range(AHEAD)]
        turned = [m.ps(f"turned{n}", [P, 512]) for n in range(2)]
        outp = m.ps("outp", [P, 512])
        shared = [m.ps(f"shared{n}", [P, 512]) for n in range(3)]

        w_loaded, w_hi, w_split, cleared = m.sem("w_loaded"), m.sem("w_hi"), m.sem("w_split"), m.sem("cleared")
        x_loaded = [m.sem(f"x_loaded{n}") for n in range(2)]
        ctx_loaded = [m.sem(f"ctx_loaded{n}") for n in range(2)]
        x_stored = [m.sem(f"x_stored{n}") for n in range(2)]
        k_stored, v_stored = m.sem("k_stored"), m.sem("v_stored")
        x_counted, x_moments, x_shifted, x_scaled, xn_done = (m.sem(n) for n in ("x_counted", "x_moments", "x_shifted", "x_scaled", "xn_done"))
        shared_ready = m.sem("shared_ready")
        kT_hi, v_hi, q_hi = m.sem("kT_hi"), m.sem("v_hi"), m.sem("q_hi")
        kT_split, v_split, q_split = m.sem("kT_split"), m.sem("v_split"), m.sem("q_split")
        scores_ready, masked, max_done = m.sem("scores_ready"), m.sem("masked"), m.sem("max_done")
        probs_ready, turned_ready = m.sem("probs_ready"), m.sem("turned_ready")
        pT_hi, pT_split = m.sem("pT_hi"), m.sem("pT_split")
        out_ready, out_copied, out_copied_too = m.sem("out_ready"), m.sem("out_copied"), m.sem("out_copied_too")
        squared, ssq_done, eps_done, rk_done, kn_done = m.sem("squared"), m.sem("ssq_done"), m.sem("eps_done"), m.sem("rk_done"), m.sem("kn_done")
        k_copied, k_out, v_out = m.sem("k_copied"), m.sem("k_out"), m.sem("v_out")
        rsum_done, tmp_done, x_done = m.sem("rsum_done"), m.sem("tmp_done"), m.sem("x_done")
        norm = norm_semaphores(m)
        block = m.block()

        def bank(what):
            return shared[BANK[what]]

        def missing(e, what):
            if not isinstance(e, int):
                return False
            return (e <= 0 and what[0] in BEFORE or e < 0 and what[0] not in NEXT
                    or e >= B - 1 and what[0] in NEXT or e >= B and what[0] not in BEFORE)

        def written(e, what):
            if isinstance(e, int) and e in (-1, 0, B - 1, B):
                ahead = [n for n in ITEMS if n[0] in NEXT]
                if e == -1:
                    return ahead.index(what) + 1
                order = [n for n in ITEMS if not missing(e, n)] if e < B else [("back", 0)]
                first = len(ahead) + (len(ITEMS) * e - len(BEFORE) if e else 0) - (len(ahead) if e == B else 0)
                return first + order.index(what) + 1
            return 4 - len(BEFORE) + len(ITEMS) * e + ITEMS.index(what) + 1

        def read(e, what):
            name, c = what
            if name == "k":
                return k_copied, KC * e + c + 1
            if name == "v":
                return v_out, KC * e + c + 1
            if name == "kt":
                return k_out, KC * e + c + 1
            if name == "ctx":
                return kT_split, KC * (e + 1) + c + 1
            if name == "q":
                return q_split, e + 2
            return tmp_done, e

        def earlier(e, what):
            own = [n for n in ITEMS if BANK[n] == BANK[what]]
            at = own.index(what)
            while True:
                at, e = (at - 1, e) if at else (len(own) - 1, e - 1)
                if isinstance(e, int) and e < -1:
                    return None
                if not missing(e, own[at]):
                    return e, own[at]

        @block.sync
        def _(sp):
            def load_ctx(b, p, half):
                sp.dma_start(ctx[:, p, :, :], io["ctx"][b, :, :].rearrange("(c p) d -> p c d", p=KP)).then_inc(ctx_loaded[p], 16)

            def load_x(b, p, half):
                sp.dma_start(xin[:, p, :], io["x"][b, :, :]).then_inc(x_loaded[p], 16)

            def head(cur):
                load_x(*cur)
                load_ctx(*cur)
                for n, name in enumerate(("Wk", "Wv")):
                    sp.dma_start(w_raw[:, :, n * D:(n + 1) * D], io[name].rearrange("(c p) n -> p c n", p=P)).then_inc(w_loaded, 16)

            def body(before, cur, after):
                if after:
                    if before:
                        sp.wait_ge(v_split, before[0] + 1)
                        sp.wait_ge(kT_split, KC * before[0] + KC)
                    load_ctx(*after)
                if before:
                    b, p, half = before
                    sp.wait_ge(x_done, b + 1)
                    sp.dma_start(io["x1"][b, :, :], xout[:, p, :]).then_inc(x_stored[p], 16)
                if after:
                    load_x(*after)
                if cur:
                    sp.wait_ge(v_out, KC * cur[0] + KC)
                    sp.dma_start(io["v1"][cur[0], :, :, :], vout[:, :, :]).then_inc(v_stored, 16)
                    sp.wait_ge(k_out, KC * cur[0] + KC)
                    sp.dma_start(io["k1"][cur[0], :, :, :], kout[:, :, :]).then_inc(k_stored, 16)

            batches(sp, head, body)
            for p in range(2):
                sp.wait_ge(x_stored[p], 16 * (B // 2) + 16)
            sp.wait_ge(k_stored, 16 * B + 16)
            sp.wait_ge(v_stored, 16 * B + 16)

        @block.gpsimd
        def _(pool):
            pool.memset(f32(q[0][:, :, :, :, :]), 0.0).then_inc(cleared, 1)
            for part in kT:
                pool.memset(f32(part[:, :, :, T:TE]), 0.0).then_inc(cleared, 1)
            pool.memset(kout[:, :, T:TE], 0.0).then_inc(cleared, 1)

            def deviations(b, p):
                pool.wait_ge(x_moments, b + 1)
                pool.tensor_tensor(x_ve[:, p:p + 1], x_mv[:, p, 1:2], keep["ln_eps"][0:S, :], ALU.add).then_inc(x_shifted, 1)
                pool.wait_ge(x_shifted, b + 1)
                pool.tensor_tensor(x_rstd[:, p:p + 1], x_ve[:, p:p + 1], keep["neghalf"][0:S, 0:1], ALU.pow).then_inc(x_scaled, 1)

            def values_lo(b, p):
                pool.wait_ge(v_hi, b + 1)
                pool.tensor_tensor(v[1][:, p, :, :], ctx[:, p, :, :], f32(v[0][:, p, :, :]), ALU.subtract).then_inc(v_split, 1)

            def head(cur):
                deviations(cur[0], cur[1])
                values_lo(cur[0], cur[1])

            def body(before, cur, after):
                for c in range(KC if cur else 0):
                    if c == KC - 1 and after:
                        deviations(after[0], after[1])
                    n = KC * cur[0] + c + 1
                    pool.wait_ge(ssq_done, n)
                    pool.tensor_tensor(ssq_eps[:, c % 2, :], ssq[:, c % 2, :], keep["rms_eps"][0:KP, :], ALU.add).then_inc(eps_done, 1)
                    pool.wait_ge(eps_done, n)
                    pool.tensor_tensor(rk[:, c % 2, :], ssq_eps[:, c % 2, :], keep["neghalf"][0:KP, 0:G], ALU.pow).then_inc(rk_done, 1)
                if after:
                    values_lo(after[0], after[1])

            batches(pool, head, body)
            norm_rstd(pool, keep, norm)

        @block.scalar
        def _(act):
            for signal, credit in ((probs_ready, AHEAD), (out_copied, 1)):
                act.sem_inc(signal, credit)

            def weights_hi():
                act.wait_ge(w_loaded, 32)
                for c in range(DC):
                    act.activation(w[0][:, c, :], w_raw[:, c, :], ACT.Copy).then_inc(w_hi, 1)

            def ctx_hi(b, p, c):
                act.wait_ge(shared_ready, written(b - 1, ("ctx", c)))
                src = bank(("ctx", c))[:, 0:DC * KP].rearrange("p (c k) -> p c k", c=DC)
                act.activation(kT[0][:, p, :, c * KP:(c + 1) * KP], src, ACT.Copy).then_inc(kT_hi, 1)

            def values_hi(b, p):
                act.activation(v[0][:, p, :, :], ctx[:, p, :, :], ACT.Copy).then_inc(v_hi, 1)

            def query_hi(b, p):
                act.wait_ge(shared_ready, written(b - 1, ("q", 0)))
                for j in range(HPG):
                    r = slice(HD * j, HD * j + HD)
                    src = bank(("q", 0))[r, 0:DC * S].rearrange("p (g s) -> p g s", g=G)
                    act.activation(q[0][r, p, :, j, :], src, ACT.Copy, scale=float(HD) ** -0.5).then_inc(q_hi, 1)

            def head(cur):
                for c in range(KC):
                    ctx_hi(cur[0], cur[1], c)
                act.wait_ge(cleared, 5)
                query_hi(cur[0], cur[1])
                values_hi(cur[0], cur[1])

            def exps(b, p, h):
                act.wait_ge(max_done, H * b + h + 1)
                act.wait_ge(turned_ready, H * b + h + 1)
                act.activation(probs[:, h % PROBS, :], score[h % AHEAD][0:S, 0:T], ACT.Exp, bias=nmax[:, p, h:h + 1],
                               accum_out=sums[:, p, h:h + 1]).then_inc(probs_ready, 1)

            def keys_copy(b, c):
                act.wait_ge(shared_ready, written(b, ("k", c)))
                act.wait_ge(kn_done, KC * b + c + 1)
                act.activation(kraw[:, c % 2, :], bank(("k", c))[0:KP, :], ACT.Copy).then_inc(k_copied, 1)

            def square_keys(b, c):
                act.wait_ge(k_copied, KC * b + c + 1)
                act.activation(squares[:, :], kraw[:, c % 2, :], ACT.Square, scale=float(XHD) ** -0.5).then_inc(squared, 1)

            def values_out(b, c):
                act.wait_ge(shared_ready, written(b, ("v", c)))
                act.wait_ge(v_stored, 16 * b + 16)
                act.activation(vout[:, c, :], bank(("v", c))[0:KP, :], ACT.Copy).then_inc(v_out, 1)

            def keys_out(b, c):
                act.wait_ge(shared_ready, written(b, ("kt", c)))
                act.wait_ge(k_stored, 16 * b + 16)
                src = bank(("kt", c))[:, 0:DC * KP].rearrange("p (c k) -> p c k", c=DC)
                act.activation(kout[:, :, c * KP:(c + 1) * KP], src, ACT.Copy, scale=keep["qk_w"][:, 0:1]).then_inc(k_out, 1)

            def probs_hi(b, h):
                g, j = divmod(h, HPG)
                act.wait_ge(turned_ready, H * b + h + 1 + PROBS)
                src = turned[h % 2][0:KP, 0:KC * S].rearrange("p (c s) -> p c s", c=KC)
                act.activation(pT[0][:, g % 2, :, j, :], src, ACT.Copy).then_inc(pT_hi, 1)

            def copy_out(b, g):
                act.wait_ge(out_ready, G * b + g + 1)
                for j in range(HPG // 2):
                    r = slice(HD * j, HD * j + HD)
                    last = act.activation(oT[r, g, :], outp[r, j * S:(j + 1) * S], ACT.Copy)
                last.then_inc(out_copied, 1)

            def body(before, cur, after):
                if cur and not before:
                    for h in range(EXPS):
                        exps(cur[0], cur[1], h)
                    weights_hi()
                for h in range(H):
                    for _, (what, c), _ in (f for f in FILL if f[0] + 1 == h):
                        if what == "k" and cur:
                            keys_copy(cur[0], c)
                        elif what == "v" and cur:
                            values_out(cur[0], c)
                        elif what == "kt" and cur:
                            keys_out(cur[0], c)
                        elif what == "ctx" and after:
                            ctx_hi(after[0], after[1], c)
                        elif what == "q" and after:
                            query_hi(after[0], after[1])
                    if cur and h + EXPS < H:
                        exps(cur[0], cur[1], h + EXPS)
                    elif after and h + EXPS >= H:
                        exps(after[0], after[1], h + EXPS - H)
                    if cur:
                        probs_hi(cur[0], h)
                    if h == SPLIT_V and after:
                        values_hi(after[0], after[1])
                    if h in SQUARE_K and cur:
                        square_keys(cur[0], SQUARE_K[h])
                    if h in COPY:
                        if COPY[h] < 0 and before:
                            copy_out(before[0], G - 1)
                        elif COPY[h] >= 0 and cur:
                            copy_out(cur[0], COPY[h])

            batches(act, head, body)

        @block.vector
        def _(dve):
            dve.sem_inc(out_copied_too, 1)
            dve.sem_inc(pT_split, 2)
            dve.sem_inc(kn_done, 2)
            dve.sem_inc(v_stored, 16)
            dve.sem_inc(k_stored, 16)
            for n in range(2):
                dve.sem_inc(x_stored[n], 16)
            dve.memset(f32(q[1][:, :, :, :, :]), 0.0).then_inc(cleared, 1)

            def weights_lo():
                for c in range(DC):
                    dve.wait_ge(w_hi, c + 1)
                    dve.tensor_tensor(w[1][:, c, :], w_raw[:, c, :], f32(w[0][:, c, :]), ALU.subtract).then_inc(w_split, 1)

            def moments(b, p, half):
                dve.wait_ge(x_loaded[p], 16 * half + 16)
                dve.bn_stats(x_bn[:, p, :], xin[:, p, :]).then_inc(x_counted, 1)
                batch = b + 1
                batch = batch if isinstance(batch, int) else dve.to_reg(batch)
                dve.wait_ge(cleared, 5)
                dve.wait_ge(x_counted, batch)
                dve.bn_aggr(x_mv[:, p, :], x_bn[:, p, :]).then_inc(x_moments, 1)

            def normalize(b, p):
                dve.wait_ge(x_scaled, b + 1)
                dve.tensor_scalar(xn[:, :], xin[:, p, :], x_mv[:, p, 0:1], x_rstd[:, p:p + 1], ALU.subtract, ALU.mult).then_inc(xn_done, 1)

            def ctx_lo(b, p, c):
                dve.wait_ge(kT_hi, KC * b + c + 1)
                src = bank(("ctx", c))[:, 0:DC * KP].rearrange("p (c k) -> p c k", c=DC)
                cols = slice(c * KP, (c + 1) * KP)
                dve.tensor_tensor(kT[1][:, p, :, cols], src, f32(kT[0][:, p, :, cols]), ALU.subtract).then_inc(kT_split, 1)

            def query_lo(b, p):
                dve.wait_ge(q_hi, HPG * b + HPG)
                for j in range(HPG):
                    r = slice(HD * j, HD * j + HD)
                    src = bank(("q", 0))[r, 0:DC * S].rearrange("p (g s) -> p g s", g=G)
                    last = dve.scalar_tensor_tensor(out=q[1][r, p, :, j, :], in0=src, scalar=float(HD) ** -0.5,
                                                    in1=f32(q[0][r, p, :, j, :]), op0=ALU.mult, op1=ALU.subtract)
                last.then_inc(q_split, 1)

            def head(cur):
                moments(*cur)
                normalize(cur[0], cur[1])
                for c in range(KC):
                    ctx_lo(cur[0], cur[1], c)
                query_lo(cur[0], cur[1])

            def maximum(b, p, h):
                head = H * b + h + 1
                head = head if isinstance(head, int) else dve.to_reg(head)
                dve.wait_ge(cleared, 5)
                dve.wait_ge(scores_ready, head)
                dve.copy_predicated(score[h % AHEAD][0:S, T - S:T], keep["later"][:, :], keep["masked_score"][:, :]).then_inc(masked, 1)
                dve.wait_ge(masked, H * b + h + 1)
                dve.tensor_reduce(nmax[:, p, h:h + 1], score[h % AHEAD][0:S, 0:T], axis=AX.X, op=ALU.max, negate=True).then_inc(max_done, 1)

            def sum_keys(b, c):
                dve.wait_ge(squared, KC * b + c + 1)
                dve.tensor_reduce(ssq[:, c % 2, :], squares[:, :].rearrange("p (g d) -> p g d", g=G), axis=AX.X, op=ALU.add).then_inc(ssq_done, 1)

            def scale_keys(b, c):
                dve.wait_ge(rk_done, KC * b + c + 1)
                src = kraw[:, c % 2, :].rearrange("p (g d) -> p g d", g=G)
                dve.tensor_tensor(kn[:, c % 2, :].rearrange("p (g d) -> p g d", g=G), src,
                                  rk[:, c % 2, :].unsqueeze(2).broadcast_to([KP, G, P]), ALU.mult).then_inc(kn_done, 1)

            def probs_lo(b, h):
                g, j = divmod(h, HPG)
                dve.wait_ge(pT_hi, H * b + h + 1)
                src = turned[h % 2][0:KP, 0:KC * S].rearrange("p (c s) -> p c s", c=KC)
                dve.tensor_tensor(pT[1][:, g % 2, :, j, :], src, f32(pT[0][:, g % 2, :, j, :]), ALU.subtract).then_inc(pT_split, 1)

            def copy_out(b, g):
                dve.wait_ge(out_ready, G * b + g + 1)
                for j in range(HPG // 2, HPG):
                    r = slice(HD * j, HD * j + HD)
                    last = dve.tensor_copy(oT[r, g, :], outp[r, j * S:(j + 1) * S])
                last.then_inc(out_copied_too, 1)

            def finish(b, p, half):
                dve.wait_ge(probs_ready, H * b + H + AHEAD)
                dve.reciprocal(rsum[:, :], sums[:, p, :]).then_inc(rsum_done, 1)
                dve.wait_ge(shared_ready, written(b + 1, ("back", 0)))
                dve.wait_ge(rsum_done, b + 1)
                dve.tensor_tensor(tmp[:, :].rearrange("p (h d) -> p h d", h=H), bank(("back", 0))[0:S, :].rearrange("p (h d) -> p h d", h=H),
                                  rsum[:, :].unsqueeze(2).broadcast_to([S, H, HD]), ALU.mult).then_inc(tmp_done, 1)
                dve.wait_ge(tmp_done, b + 1)
                dve.wait_ge(x_stored[p], 16 * half + 16)
                dve.scalar_tensor_tensor(out=xout[:, p, :], in0=tmp[:, :], scalar=keep["gates"][0:S, 0:1], in1=xin[:, p, :],
                                         op0=ALU.mult, op1=ALU.add).then_inc(x_done, 1)
                dve.wait_ge(x_done, b + 1)
                dve.bn_stats(keep["bn"][:, b, :], xout[:, p, :]).then_inc(norm["counted"], 1)

            def body(before, cur, after):
                if cur and not before:
                    for h in range(AHEAD):
                        maximum(cur[0], cur[1], h)
                    weights_lo()
                for h in range(H):
                    if h == NORMALIZE and after:
                        normalize(after[0], after[1])
                    if cur:
                        if h + AHEAD < H:
                            maximum(cur[0], cur[1], h + AHEAD)
                        elif after:
                            maximum(after[0], after[1], h + AHEAD - H)
                        probs_lo(cur[0], h)
                    for _, (what, c), _ in (f for f in FILL if f[0] + 1 == h and after):
                        if what == "ctx":
                            ctx_lo(after[0], after[1], c)
                        elif what == "q":
                            query_lo(after[0], after[1])
                    if cur:
                        if h in SUM_K:
                            sum_keys(cur[0], SUM_K[h])
                        if h in SCALE_K:
                            scale_keys(cur[0], SCALE_K[h])
                    if h in COPY:
                        if COPY[h] < 0 and before:
                            copy_out(before[0], G - 1)
                        elif COPY[h] >= 0 and cur:
                            copy_out(cur[0], COPY[h])
                    if h == MOMENTS and after:
                        moments(*after)
                    if h == FINISH and before:
                        finish(*before)

            batches(dve, head, body)
            norm_moments(dve, keep, norm)

        @block.tensor
        def _(pe):
            pe.sem_inc(turned_ready, PROBS)
            ident = keep["ident"]

            def bank_free(e, what):
                before = earlier(e, what)
                if before:
                    pe.wait_ge(*read(*before))

            def turn_ctx(b, p, half, c):
                if c == 0:
                    pe.wait_ge(ctx_loaded[p], 16 * half + 16)
                bank_free(b - 1, ("ctx", c))
                for n in range(DC):
                    last = pe.transpose(bank(("ctx", c))[:, n * KP:(n + 1) * KP], ctx[:, p, c, n * P:(n + 1) * P], ident[0:KP, 0:KP])
                last.then_inc(shared_ready, 1)

            def turn_queries(b):
                pe.wait_ge(xn_done, b + 1)
                bank_free(b - 1, ("q", 0))
                for n in range(DC):
                    last = pe.transpose(bank(("q", 0))[:, n * S:(n + 1) * S], xn[:, n * P:(n + 1) * P], ident[0:S, 0:S])
                last.then_inc(shared_ready, 1)

            def head(cur):
                for c in range(KC):
                    turn_ctx(*cur, c)
                turn_queries(cur[0])

            def scores(b, p, h):
                g, j = divmod(h, HPG)
                if h == 0:
                    pe.wait_ge(q_split, b + 1)
                    pe.wait_ge(kT_split, KC * b + KC)
                pe.wait_ge(probs_ready, H * b + h + 1)
                for n, (s, r) in enumerate(PASSES):
                    last = pe.matmul(score[h % AHEAD][0:S, 0:TE], q[s][:, p, g, j, :], kT[r][:, p, g, :],
                                     start=n == 0, stop=n == len(PASSES) - 1)
                last.then_inc(scores_ready, 1)

            def project(b, p, what):
                name, c = what
                bank_free(b, what)
                cols = slice(0, D) if name == "k" else slice(D, 2 * D)
                for n, (s, r) in enumerate(PASSES):
                    for k in range(DC):
                        last = pe.matmul(bank(what)[0:KP, :], kT[s][:, p, k, c * KP:(c + 1) * KP], w[r][:, k, cols],
                                         start=n == 0 and k == 0, stop=n == len(PASSES) - 1 and k == DC - 1)
                last.then_inc(shared_ready, 1)

            def turn_keys(b, c):
                pe.wait_ge(kn_done, KC * b + c + 1 + 2)
                bank_free(b, ("kt", c))
                for n in range(DC):
                    last = pe.transpose(bank(("kt", c))[:, n * KP:(n + 1) * KP], kn[:, c % 2, n * P:(n + 1) * P], ident[0:KP, 0:KP])
                last.then_inc(shared_ready, 1)

            def turn_probs(b, h):
                pe.wait_ge(probs_ready, H * b + h + 1 + AHEAD)
                pe.wait_ge(pT_split, H * b + h + 1)
                for c in range(KC):
                    last = pe.transpose(turned[h % 2][0:KP, c * S:(c + 1) * S], probs[:, h % PROBS, c * KP:(c + 1) * KP], ident[0:S, 0:S])
                last.then_inc(turned_ready, 1)

            def weigh(b, p, g):
                pe.wait_ge(pT_split, H * b + HPG * (g + 1) + 2)
                pe.wait_ge(out_copied, G * b + g + 1)
                pe.wait_ge(out_copied_too, G * b + g + 1)
                if g == 0:
                    pe.wait_ge(v_split, b + 1)
                for n, (s, r) in enumerate(PASSES):
                    for c in range(KC):
                        last = pe.matmul(outp[:, 0:HPG * S], v[s][:, p, c, g * P:(g + 1) * P],
                                         pT[r][:, g % 2, c, :, :].rearrange("p j s -> p (j s)"),
                                         start=n == 0 and c == 0, stop=n == len(PASSES) - 1 and c == KC - 1)
                last.then_inc(out_ready, 1)

            def turn_back(b):
                pe.wait_ge(out_copied, G * b + G + 1)
                pe.wait_ge(out_copied_too, G * b + G + 1)
                bank_free(b + 1, ("back", 0))
                for g in range(G):
                    last = pe.transpose(bank(("back", 0))[0:S, g * P:(g + 1) * P], oT[:, g, :], ident[:, :])
                last.then_inc(shared_ready, 1)

            def body(before, cur, after):
                if cur and not before:
                    for h in range(AHEAD):
                        scores(cur[0], cur[1], h)
                    pe.wait_ge(w_split, DC)
                for h in range(H):
                    if cur:
                        turn_probs(cur[0], h)
                        if h + AHEAD < H:
                            scores(cur[0], cur[1], h + AHEAD)
                        elif after:
                            scores(after[0], after[1], h + AHEAD - H)
                    if h in WEIGH:
                        if WEIGH[h] < 0 and before:
                            weigh(before[0], before[1], G - 1)
                        elif WEIGH[h] >= 0 and cur:
                            weigh(cur[0], cur[1], WEIGH[h])
                    for _, (what, c), _ in (f for f in FILL if f[0] == h):
                        if what in ("k", "v") and cur:
                            project(cur[0], cur[1], (what, c))
                        elif what == "kt" and cur:
                            turn_keys(cur[0], c)
                        elif what == "ctx" and after:
                            turn_ctx(*after, c)
                        elif what == "q" and after:
                            turn_queries(after[0])
                        elif what == "back" and before:
                            turn_back(before[0])

            batches(pe, head, body)


IC = INTER // P
NG = 4
BPG = B // NG
GS = BPG * S


def phase_b_prepare(nc, keep, io, big):
    wug, wdn, xT = big["wug"], big["wdn"], big["xT"]
    BLOCKS = IC // NG
    STAGES = 4
    CREDIT = 2 * STAGES - 1
    with Memory(nc, "p") as m:
        ug_raw = m.sb("ug_raw", [P, 4, D])
        down_raw = m.sb("down_raw", [P, INTER])
        down = [m.sb(f"down{n}", [P, INTER]) for n in range(2)]
        signs = m.sb("signs", [S, D])
        xin = m.sb("xin", [S, 2, D])
        z = [m.sb(f"z{n}", [S, D]) for n in range(3)]
        zT = m.sb("zT", [P, DC, GS])
        z_bank = [m.ps(f"z_bank{n}", [P, 512]) for n in range(2)]
        h_bank = [m.ps(f"h_bank{n}", [P, 512]) for n in range(2)]
        u_bank = [m.ps(f"u_bank{n}", [P, 512]) for n in range(2)]
        d_bank = [m.ps(f"d_bank{n}", [P, 512]) for n in range(2)]
        small_loaded, d_loaded = m.sem("small_loaded"), m.sem("d_loaded")
        u_loaded = [m.sem(f"u_loaded{n}") for n in range(4)]
        x_loaded = [m.sem(f"x_loaded{n}") for n in range(2)]
        xn_done, signed, z_sums, z_done, z_turned, z_copied = (m.sem(n) for n in ("xn_done", "signed", "z_sums", "z_done", "z_turned", "z_copied"))
        rotated, x_hi, x_split = m.sem("rotated"), m.sem("x_hi"), m.sem("x_split")
        u_turned, u_copied = m.sem("u_turned"), m.sem("u_copied")
        d_sums, d_turned, d_copied, d_rotated, d_signed = (m.sem(n) for n in ("d_sums", "d_turned", "d_copied", "d_rotated", "d_signed"))
        block = m.block()

        def pairs(buffer, h):
            halves = buffer.rearrange("p (a two n) -> p a two n", two=2, n=h)
            return halves[:, :, 0, :], halves[:, :, 1, :]

        @block.sync
        def _(sp):
            with nc.allow_non_contiguous_dma(reason="scales by partition"):
                sp.dma_start(signs[:, :], io["SU_ug"].rearrange("(a n) -> a n", a=1).broadcast_to([S, D])).then_inc(small_loaded, 16)
                sp.dma_start(big["down_scale"][:, :], io["Wscale_dp"].rearrange("(a n) -> a n", a=1).broadcast_to([S, D])).then_inc(small_loaded, 16)
                sp.dma_start(big["down_signs"][:, :], io["SU_dp"].rearrange("(c p) -> p c", p=P)).then_inc(small_loaded, 16)
                sp.dma_start(big["ug_scale"][:, :], io["Wscale_ug"].rearrange("(c p) -> p c", p=P)).then_inc(small_loaded, 16)
            with sp.Fori(0, NG) as i:
                sp.wait_ge(d_sums, 2 * STAGES * i + 1)
                sp.dma_start(down_raw[:, :], io["W_down"].rearrange("(q p) n -> q p n", p=P)[i, :, :]).then_inc(d_loaded, 16)
                for k in range(BPG):
                    j = BPG * i + k
                    sp.wait_ge(signed, j + 1)
                    sp.dma_start(xin[:, k % 2, :], io["x1"][j, :, :]).then_inc(x_loaded[k % 2], 16)
                    for n, name in enumerate(("W_up", "W_gate")):
                        u = 2 * k + n
                        sp.wait_ge(u_turned, 2 * BLOCKS * i + u + 1)
                        sp.dma_start(ug_raw[:, u % 4, :], io[name].rearrange("(c p) n -> c p n", p=P)[j, :, :]).then_inc(u_loaded[u % 4], 16)

        @block.gpsimd
        def _(pool):
            pool.wait_ge(small_loaded, 64)
            with pool.Fori(0, NG) as i:
                for k in range(BPG):
                    j = BPG * i + k
                    pool.wait_ge(xn_done, j + 1)
                    pool.tensor_tensor(z[0][:, :], xin[:, k % 2, :], signs[:, :], ALU.mult).then_inc(signed, 1)
                    (a, b), (s, d) = pairs(z[0][:, :], P), pairs(z[1][:, :], P)
                    pool.wait_ge(signed, j + 1 + 2)
                    pool.wait_ge(z_sums, 4 * j + 4)
                    pool.tensor_tensor(s, a, b, ALU.add).then_inc(z_sums, 1)
                    pool.tensor_tensor(d, a, b, ALU.subtract).then_inc(z_sums, 1)

        @block.scalar
        def _(act):
            for signal, credit in ((z_copied, 2), (u_copied, 2), (d_copied, 2), (d_signed, 2)):
                act.sem_inc(signal, credit)
            with act.Fori(0, NG) as i:
                for k in range(BPG):
                    j = BPG * i + k
                    for n in range(2):
                        u = 2 * k + n
                        act.wait_ge(u_turned, 2 * BLOCKS * i + u + 1 + 4)
                        act.activation(wug[:, :, n, bass.ds(j * P, P)], u_bank[n][:, :].rearrange("p (c n) -> p c n", c=DC),
                                       ACT.Copy).then_inc(u_copied, 1)
                    act.wait_ge(z_turned, j + 1 + 1)
                    if k == 0:
                        act.wait_ge(rotated, DC * i + 1)
                    act.activation(zT[:, :, k * S:(k + 1) * S], z_bank[k % 2][:, 0:DC * S].rearrange("p (c s) -> p c s", c=DC),
                                   ACT.Copy).then_inc(z_copied, 1)
                for c in range(DC):
                    act.wait_ge(d_turned, DC * i + c + 1 + 4)
                    act.activation(wdn[:, 4 * c:4 * c + 4, bass.ds(i * P, P)], d_bank[c % 2][:, :].rearrange("p (c n) -> p c n", c=4),
                                   ACT.Copy).then_inc(d_copied, 1)
                    act.wait_ge(rotated, DC * i + c + 1 + 1)
                    act.activation(xT[0][:, c, bass.ds(i * GS, GS)], h_bank[c % 2][:, 0:GS], ACT.Copy, scale=float(D) ** -0.5).then_inc(x_hi, 1)
            with act.Fori(0, IC // 2) as i:
                for n in range(2):
                    act.wait_ge(d_rotated, 2 * i + n + 1)
                    act.activation(wdn[:, 2 * i + n, :], d_bank[n][:, :], ACT.Copy,
                                   scale=big["down_signs"][:, bass.ds(2 * i + n, 1)]).then_inc(d_signed, 1)

        @block.vector
        def _(dve):
            for signal, credit in ((signed, 2), (z_sums, 4), (x_split, 2), (d_sums, CREDIT)):
                dve.sem_inc(signal, credit)
            dve.wait_ge(small_loaded, 64)
            dve.tensor_scalar(big["down_scale"][:, :], big["down_scale"][:, :], float(INTER) ** -0.5, keep["gates"][0:S, 2:3],
                              ALU.mult, ALU.mult)

            def normalize(i, k):
                j = BPG * i + k
                dve.wait_ge(x_loaded[k % 2], 32 * i + 16 * (k // 2) + 16)
                dve.tensor_scalar(xin[:, k % 2, :], xin[:, k % 2, :], keep["mv"][:, j, 0:1], keep["rstd"][:, j, :],
                                  ALU.subtract, ALU.mult).then_inc(xn_done, 1)

            def rotate_batch(i, k):
                j = BPG * i + k
                (a, b), (s, d) = pairs(z[1][:, :], 2 * P), pairs(z[2][:, :], 2 * P)
                dve.wait_ge(z_sums, 4 * j + 2 + 4)
                dve.wait_ge(z_turned, j + 1)
                dve.tensor_tensor(s, a, b, ALU.add).then_inc(z_sums, 1)
                dve.tensor_tensor(d, a, b, ALU.subtract).then_inc(z_sums, 1)

            def rotate_down(i, stage):
                src, dst = down[1 - stage % 2] if stage else down_raw, down[stage % 2]
                dve.wait_ge(d_sums, 2 * STAGES * i + 2 * stage + CREDIT)
                if stage == 0:
                    dve.wait_ge(d_loaded, 16 * i + 16)
                if stage == 1:
                    dve.wait_ge(d_turned, 4 * i + 4)
                (a, b), (s, d) = pairs(src[:, :], P << stage), pairs(dst[:, :], P << stage)
                dve.tensor_tensor(s, a, b, ALU.add).then_inc(d_sums, 1)
                dve.tensor_tensor(d, a, b, ALU.subtract).then_inc(d_sums, 1)

            def x_lo(i, chunks):
                for c in chunks:
                    dve.wait_ge(x_hi, DC * i + c + 1)
                    cols = bass.ds(i * GS, GS)
                    dve.scalar_tensor_tensor(out=xT[1][:, c, cols], in0=h_bank[c % 2][:, 0:GS], scalar=float(D) ** -0.5,
                                             in1=f32(xT[0][:, c, cols]), op0=ALU.mult, op1=ALU.subtract).then_inc(x_split, 1)

            def step(i, before):
                for k in range(BPG):
                    normalize(i, k)
                    rotate_down(i, k)
                    if k < 2 and before is not None:
                        x_lo(before, (2 * k, 2 * k + 1))
                    rotate_batch(i, k)

            step(0, None)
            with dve.Fori(1, NG) as i:
                step(i, i - 1)
            x_lo(NG - 1, range(DC))

        @block.tensor
        def _(pe):
            for signal, credit in ((z_turned, 1), (rotated, 1), (u_turned, 4), (d_turned, 4)):
                pe.sem_inc(signal, credit)
            ident, had = keep["ident"], keep["hadamard"]
            with pe.Fori(0, NG) as i:
                for k in range(BPG):
                    j = BPG * i + k
                    for n in range(2):
                        u = 2 * k + n
                        pe.wait_ge(u_loaded[u % 4], 32 * i + 16 * (u // 4) + 16)
                        pe.wait_ge(u_copied, 2 * BLOCKS * i + u + 1)
                        for c in range(DC):
                            last = pe.transpose(u_bank[n][:, c * P:(c + 1) * P], ug_raw[:, u % 4, c * P:(c + 1) * P], ident[:, :])
                        last.then_inc(u_turned, 1)
                    pe.wait_ge(z_sums, 4 * j + 4 + 4)
                    pe.wait_ge(z_copied, j + 1)
                    for c in range(DC):
                        last = pe.transpose(z_bank[k % 2][:, c * S:(c + 1) * S], z[2][:, c * P:(c + 1) * P], ident[0:S, 0:S])
                    last.then_inc(z_turned, 1)
                for c in range(NG):
                    pe.wait_ge(d_sums, 2 * STAGES * i + 2 * STAGES + CREDIT)
                    pe.wait_ge(d_copied, NG * i + c + 1)
                    for n in range(4):
                        r = slice((4 * c + n) * P, (4 * c + n + 1) * P)
                        last = pe.transpose(d_bank[c % 2][:, n * P:(n + 1) * P], down[1][:, r], ident[:, :])
                    last.then_inc(d_turned, 1)
                    if c == 0:
                        pe.wait_ge(z_copied, BPG * i + BPG + 2)
                    pe.wait_ge(x_split, DC * i + c + 1)
                    pe.matmul(h_bank[c % 2][:, 0:GS], had[:, :], zT[:, c, :], start=True, stop=True).then_inc(rotated, 1)
            pe.wait_ge(d_copied, NG * NG + 2)
            with pe.Fori(0, IC // 2) as i:
                for n in range(2):
                    pe.wait_ge(d_signed, 2 * i + n + 1)
                    pe.matmul(d_bank[n][:, :], had[:, :], wdn[:, 2 * i + n, :], start=True, stop=True).then_inc(d_rotated, 1)


def phase_b(nc, keep, io):
    with Memory(nc, "f") as outer:
        big = {
            "wug": outer.sb("wug", [P, DC, 2, INTER]),
            "wdn": outer.sb("wdn", [P, IC, D]),
            "xT": [outer.sb(f"xT_{n}", [P, DC, B * S], F32R) for n in ("hi", "lo")],
            "down_signs": outer.sb("down_signs", [P, IC]),
            "down_scale": outer.sb("down_scale", [S, D]),
            "ug_scale": outer.sb("ug_scale", [P, 2 * IC]),
        }
        phase_b_prepare(nc, keep, io, big)
        phase_b_run(nc, keep, io, big)


def phase_b_run(nc, keep, io, big):
    wug, wdn, xT, ug_scale = big["wug"], big["wdn"], big["xT"], big["ug_scale"]
    with Memory(nc, "b") as m:
        wu = [m.sb(f"wu_{n}", [P, 2, DC, 2, P], F32R) for n in ("hi", "lo")]
        wd = [m.sb(f"wd_{n}", [P, 2, D], F32R) for n in ("hi", "lo")]
        silu = m.sb("silu", [P, 2, GS])
        hidden = m.sb("hidden", [P, 2, GS])
        hT = [m.sb(f"hT_{n}", [P, 2, GS], F32R) for n in ("hi", "lo")]
        xio = m.sb("xio", [S, BPG, D])
        up = [m.ps(f"up{n}", [P, 512]) for n in range(2)]
        gate = [m.ps(f"gate{n}", [P, 512]) for n in range(2)]
        y = [m.ps(f"y{n}", [P, 512]) for n in range(BPG)]
        x_loaded, x_stored, x_done, y_ready = m.sem("x_loaded"), m.sem("x_stored"), m.sem("x_done"), m.sem("y_ready")
        y_scaled = m.sem("y_scaled")
        wu_hi, wu_split, wd_hi, wd_split = m.sem("wu_hi"), m.sem("wu_split"), m.sem("wd_hi"), m.sem("wd_split")
        gu_ready, silu_done, h_done, h_hi, h_split = (m.sem(n) for n in ("gu_ready", "silu_done", "h_done", "h_hi", "h_split"))
        norm = norm_semaphores(m)
        block = m.block()

        @block.sync
        def _(sp):
            with sp.Fori(0, NG) as g:
                sp.wait_ge(x_stored, 16 * g + 16)
                sp.dma_start(xio[:, :, :], io["x1"][bass.ds(BPG * g, BPG), :, :].rearrange("b s d -> s b d")).then_inc(x_loaded, 16)
                sp.wait_ge(x_done, BPG * g + BPG)
                sp.wait_ge(norm["counted"], BPG * g + BPG)
                sp.dma_start(io["x2"][bass.ds(BPG * g, BPG), :, :].rearrange("b s d -> s b d"), xio[:, :, :]).then_inc(x_stored, 16)
            sp.wait_ge(x_stored, 16 * NG + 16)

        @block.gpsimd
        def _(pool):
            pool.sem_inc(x_stored, 16)
            norm_rstd(pool, keep, norm)

        @block.scalar
        def _(act):
            for p in range(2):
                act.activation(wu[0][:, p, :, :, :], wug[:, :, :, p * P:(p + 1) * P], ACT.Copy).then_inc(wu_hi, 1)
            with act.Fori(0, NG) as g:
                with act.Fori(0, IC // 2) as i:
                    for p in range(2):
                        c, t = 2 * i + p, IC * g + 2 * i + p
                        act.wait_ge(gu_ready, t + 1 + 1)
                        act.activation(silu[:, p, :], gate[p][:, 0:GS], ACT.Silu, scale=ug_scale[:, bass.ds(IC + c, 1)]).then_inc(silu_done, 1)
                        act.activation(wd[0][:, p, :], wdn[:, c, :], ACT.Copy).then_inc(wd_hi, 1)
                        act.wait_ge(h_done, t + 1 + 2)
                        act.activation(hT[0][:, p, :], hidden[:, p, :], ACT.Copy).then_inc(h_hi, 1)
                        act.activation(wu[0][:, p, :, :, :], wug[:, :, :, bass.ds(((c + 2) % IC) * P, P)], ACT.Copy).then_inc(wu_hi, 1)

        @block.vector
        def _(dve):
            dve.sem_inc(h_done, 2)
            dve.sem_inc(x_done, 1)
            for p in range(2):
                dve.wait_ge(wu_hi, p + 1)
                dve.tensor_tensor(wu[1][:, p, :, :, :], wug[:, :, :, p * P:(p + 1) * P], f32(wu[0][:, p, :, :, :]),
                                  ALU.subtract).then_inc(wu_split, 1)
            with dve.Fori(0, NG) as g:
                with dve.Fori(0, IC // 2) as i:
                    for p in range(2):
                        c, t = 2 * i + p, IC * g + 2 * i + p
                        dve.wait_ge(silu_done, t + 1)
                        dve.scalar_tensor_tensor(out=hidden[:, p, :], in0=up[p][:, 0:GS], scalar=ug_scale[:, bass.ds(c, 1)], in1=silu[:, p, :],
                                                 op0=ALU.mult, op1=ALU.mult).then_inc(h_done, 1)
                        dve.wait_ge(wd_hi, t + 1)
                        dve.tensor_tensor(wd[1][:, p, :], wdn[:, c, :], f32(wd[0][:, p, :]), ALU.subtract).then_inc(wd_split, 1)
                        dve.wait_ge(h_hi, t + 1)
                        dve.tensor_tensor(hT[1][:, p, :], hidden[:, p, :], f32(hT[0][:, p, :]), ALU.subtract).then_inc(h_split, 1)
                        dve.wait_ge(wu_hi, t + 3)
                        dve.tensor_tensor(wu[1][:, p, :, :, :], wug[:, :, :, bass.ds(((c + 2) % IC) * P, P)],
                                          f32(wu[0][:, p, :, :, :]), ALU.subtract).then_inc(wu_split, 1)
                dve.wait_ge(x_loaded, 16 * g + 16)
                dve.wait_ge(y_ready, g + 1)
                for k in range(BPG):
                    dve.tensor_tensor(y[k][0:S, :], y[k][0:S, :], big["down_scale"][:, :], ALU.mult).then_inc(y_scaled, 1)
                for k in range(BPG):
                    dve.wait_ge(y_scaled, BPG * g + k + 1)
                    dve.tensor_tensor(xio[:, k, :], y[k][0:S, :], xio[:, k, :], ALU.add).then_inc(x_done, 1)
                for k in range(BPG):
                    dve.wait_ge(x_done, BPG * g + k + 1 + 1)
                    dve.bn_stats(keep["bn"][:, BPG * g + k, :], xio[:, k, :]).then_inc(norm["counted"], 1)
            norm_moments(dve, keep, norm)

        @block.tensor
        def _(pe):
            pe.sem_inc(gu_ready, 1)

            def project(g, c, t, p):
                pe.wait_ge(wu_split, t + 1)
                pe.wait_ge(h_done, t + 1)
                for n, out in ((1, gate[p]), (0, up[p])):
                    for k, (s, r) in enumerate(PASSES):
                        for d in range(DC):
                            last = pe.matmul(out[:, 0:GS], wu[s][:, p, d, n, :], xT[r][:, d, bass.ds(g * GS, GS)],
                                             start=k == 0 and d == 0, stop=k == len(PASSES) - 1 and d == DC - 1)
                last.then_inc(gu_ready, 1)

            def reduce(t, p, first, final):
                pe.wait_ge(h_split, t + 1)
                pe.wait_ge(wd_split, t + 1)
                for b in range(BPG):
                    for k, (s, r) in enumerate(PASSES):
                        last = pe.matmul(y[b][0:S, :], hT[s][:, p, b * S:(b + 1) * S], wd[r][:, p, :],
                                         start=first and k == 0, stop=final and k == len(PASSES) - 1)
                if final:
                    last.then_inc(y_ready, 1)

            with pe.Fori(0, NG) as g:
                project(g, 0, IC * g, 0)
                project(g, 1, IC * g + 1, 1)
                pe.wait_ge(x_done, BPG * g + 1)
                reduce(IC * g, 0, True, False)
                with pe.Fori(1, IC // 2) as i:
                    for p in range(2):
                        t = IC * g + 2 * i + p
                        project(g, 2 * i + p, t, p)
                        reduce(t - 1, 1 - p, False, False)
                reduce(IC * g + IC - 1, 1, False, True)


def phase_c(nc, keep, io):
    with Memory(nc, "o") as outer:
        wo = [outer.sb(f"wo_{n}", [P, H, D], F32R) for n in ("hi", "lo")]
        phase_c_queries(nc, keep, io, wo)
        phase_c_attention(nc, keep, io, wo)


def phase_c_queries(nc, keep, io, wo):
    LAG = 2
    QW = G * D
    TURN_X = 1
    with Memory(nc, "q") as m:
        w_raw = m.sb("w_raw", [P, DC, QW])
        w = [m.sb(f"w_{n}", [P, DC, QW], F32R) for n in ("hi", "lo")]
        xin = m.sb("xin", [S, 2, D])
        xn = m.sb("xn", [S, D])
        xT = [m.sb(f"xT_{n}", [P, 2, DC, S], F32R) for n in ("hi", "lo")]
        squares = m.sb("squares", [S, D])
        ssq = m.sb("ssq", [S, 2, G])
        ssq_eps = m.sb("ssq_eps", [S, 2, G])
        rq = m.sb("rq", [S, 2, G])
        qn = m.sb("qn", [S, 2, D])
        qT = m.sb("qT", [P, 2, H, S])
        x_bank = m.ps("x_bank", [P, 512])
        q_bank = [m.ps(f"q_bank{n}", [P, 512]) for n in range(G)]
        t_bank = [m.ps(f"t_bank{n}", [P, 512]) for n in range(2)]
        w_loaded = [m.sem(f"w_loaded{n}") for n in range(G)]
        w_hi, w_split, wo_loaded, wo_hi, wo_split = (m.sem(n) for n in ("w_hi", "w_split", "wo_loaded", "wo_hi", "wo_split"))
        x_loaded = [m.sem(f"x_loaded{n}") for n in range(2)]
        q_stored = [m.sem(f"q_stored{n}") for n in range(2)]
        xn_done, x_turned, x_hi, x_split = (m.sem(n) for n in ("xn_done", "x_turned", "x_hi", "x_split"))
        q_ready, squared, ssq_done, eps_done, rq_done = (m.sem(n) for n in ("q_ready", "squared", "ssq_done", "eps_done", "rq_done"))
        qn_done, q_turned, q_copied = m.sem("qn_done"), m.sem("q_turned"), m.sem("q_copied")
        block = m.block()

        def splits_wo(cur, after):
            return cur and not after

        @block.sync
        def _(sp):
            def load_x(b, p, half):
                sp.dma_start(xin[:, p, :], io["x2"][b, :, :]).then_inc(x_loaded[p], 16)

            def head(cur):
                load_x(*cur)
                wq = io["Wq"].rearrange("(c p) n -> p c n", p=P)
                for n in range(G):
                    cols = slice(n * D, (n + 1) * D)
                    sp.dma_start(w_raw[:, :, cols], wq[:, :, cols]).then_inc(w_loaded[n], 16)

            def body(before, cur, after):
                if after:
                    if before:
                        sp.wait_ge(xn_done, before[0] + 1)
                    load_x(*after)
                if cur and not before:
                    sp.wait_ge(w_split, G)
                    sp.dma_start(w_raw[:, :, :].rearrange("p c n -> p (c n)"),
                                 io["Wo"].rearrange("(h p) n -> p h n", p=P)).then_inc(wo_loaded, 16)
                if before:
                    b, p, half = before
                    sp.wait_ge(q_copied, G * b + G + 2)
                    sp.dma_start(io["q1"][b, :, :, :], qT[:, p, :, :]).then_inc(q_stored[p], 16)

            batches(sp, head, body)
            for p in range(2):
                sp.wait_ge(q_stored[p], 16 * (B // 2) + 16)

        @block.gpsimd
        def _(pool):
            def body(before, cur, after):
                for n in range(G if cur else 0):
                    t = G * cur[0] + n + 1
                    pool.wait_ge(ssq_done, t + 1)
                    pool.tensor_tensor(ssq_eps[:, n % 2, :], ssq[:, n % 2, :], keep["rms_eps"][0:S, :], ALU.add).then_inc(eps_done, 1)
                    pool.wait_ge(eps_done, t)
                    pool.tensor_tensor(rq[:, n % 2, :], ssq_eps[:, n % 2, :], keep["neghalf"][0:S, 0:G], ALU.pow).then_inc(rq_done, 1)

            batches(pool, lambda cur: None, body)

        @block.scalar
        def _(act):
            act.sem_inc(q_copied, 2)

            def weights_hi(n):
                act.wait_ge(w_loaded[n], 16)
                cols = slice(n * D, (n + 1) * D)
                act.activation(w[0][:, :, cols], w_raw[:, :, cols], ACT.Copy).then_inc(w_hi, 1)

            def head(cur):
                b, p, half = cur
                act.wait_ge(x_turned, b + 1)
                act.activation(xT[0][:, p, :, :], x_bank[:, 0:DC * S].rearrange("p (c s) -> p c s", c=DC), ACT.Copy).then_inc(x_hi, 1)

            def copy_queries(b, p, half, n):
                t = G * b + n + 1
                act.wait_ge(q_turned, t + 2)
                act.wait_ge(q_stored[p], 16 * half + 16)
                act.activation(qT[:, p, G * n:G * n + G, :], t_bank[n % 2][:, 0:G * S].rearrange("p (h s) -> p h s", h=G),
                               ACT.Copy).then_inc(q_copied, 1)

            def body(before, cur, after):
                if cur and not before:
                    weights_hi(0)
                for n in range(G):
                    if cur and not before and n + 1 < G:
                        weights_hi(n + 1)
                    if cur:
                        act.wait_ge(q_ready, G * cur[0] + n + 1)
                        act.wait_ge(ssq_done, G * cur[0] + n + 1)
                        act.activation(squares[:, :], q_bank[n][0:S, :], ACT.Square, scale=float(XHD) ** -0.5).then_inc(squared, 1)
                    if splits_wo(cur, after):
                        act.wait_ge(wo_loaded, 16)
                        act.activation(wo[0][:, n * G:n * G + G, :].rearrange("p h n -> p (h n)"), w_raw[:, n, :], ACT.Copy).then_inc(wo_hi, 1)
                    late = cur if n >= LAG else before
                    if late:
                        copy_queries(*late, (n - LAG) % G)
                    if n == TURN_X and after:
                        head(after)

            batches(act, head, body)

        @block.vector
        def _(dve):
            for signal, credit in ((qn_done, G), (x_split, 1), (ssq_done, 1)):
                dve.sem_inc(signal, credit)
            for n in range(2):
                dve.sem_inc(q_stored[n], 16)

            def normalize(b, p, half):
                dve.wait_ge(x_loaded[p], 16 * half + 16)
                dve.tensor_scalar(xn[:, :], xin[:, p, :], keep["mv"][:, b, 0:1], keep["rstd"][:, b, :],
                                  ALU.subtract, ALU.mult).then_inc(xn_done, 1)

            def x_lo(b, p, half):
                dve.wait_ge(x_hi, b + 1)
                dve.tensor_tensor(xT[1][:, p, :, :], x_bank[:, 0:DC * S].rearrange("p (c s) -> p c s", c=DC),
                                  f32(xT[0][:, p, :, :]), ALU.subtract).then_inc(x_split, 1)

            def head(cur):
                normalize(*cur)
                x_lo(*cur)

            def weights_lo(n):
                dve.wait_ge(w_hi, n + 1)
                cols = slice(n * D, (n + 1) * D)
                dve.tensor_tensor(w[1][:, :, cols], w_raw[:, :, cols], f32(w[0][:, :, cols]), ALU.subtract).then_inc(w_split, 1)

            def scale(b, n):
                t = G * b + n + 1
                dve.wait_ge(squared, t)
                dve.tensor_reduce(ssq[:, n % 2, :], squares[:, :].rearrange("p (h d) -> p h d", h=G), axis=AX.X, op=ALU.add).then_inc(ssq_done, 1)
                dve.wait_ge(rq_done, t)
                dve.wait_ge(q_turned, t)
                dve.tensor_tensor(qn[:, n % 2, :].rearrange("p (h d) -> p h d", h=G), q_bank[n][0:S, :].rearrange("p (h d) -> p h d", h=G),
                                  rq[:, n % 2, :].unsqueeze(2).broadcast_to([S, G, XHD]), ALU.mult).then_inc(qn_done, 1)

            def body(before, cur, after):
                if cur and not before:
                    weights_lo(0)
                for n in range(G):
                    if cur and not before and n + 1 < G:
                        weights_lo(n + 1)
                    if n == 0 and after:
                        normalize(*after)
                    if cur:
                        scale(cur[0], n)
                    if splits_wo(cur, after):
                        dve.wait_ge(wo_hi, n + 1)
                        dve.tensor_tensor(wo[1][:, n * G:n * G + G, :].rearrange("p h n -> p (h n)"), w_raw[:, n, :],
                                          f32(wo[0][:, n * G:n * G + G, :]).rearrange("p h n -> p (h n)"), ALU.subtract).then_inc(wo_split, 1)
                    if n == TURN_X and after:
                        x_lo(*after)

            batches(dve, head, body)

        @block.tensor
        def _(pe):
            pe.sem_inc(q_turned, 2)
            ident = keep["ident"]

            def head(cur):
                b = cur[0]
                pe.wait_ge(xn_done, b + 1)
                pe.wait_ge(x_split, b + 1)
                for c in range(DC):
                    last = pe.transpose(x_bank[:, c * S:(c + 1) * S], xn[:, c * P:(c + 1) * P], ident[0:S, 0:S])
                last.then_inc(x_turned, 1)

            def project(b, p, n):
                if n == 0:
                    pe.wait_ge(x_split, b + 1 + 1)
                pe.wait_ge(qn_done, G * b + n + 1)
                for k, (s, r) in enumerate(PASSES):
                    for c in range(DC):
                        last = pe.matmul(q_bank[n][0:S, :], xT[s][:, p, c, :], w[r][:, c, n * D:(n + 1) * D],
                                         start=k == 0 and c == 0, stop=k == len(PASSES) - 1 and c == DC - 1)
                last.then_inc(q_ready, 1)

            def turn(b, n):
                t = G * b + n + 1
                pe.wait_ge(qn_done, t + G)
                pe.wait_ge(q_copied, t)
                for h in range(G):
                    last = pe.transpose(t_bank[n % 2][:, h * S:(h + 1) * S], qn[:, n % 2, h * P:(h + 1) * P], ident[0:S, 0:S])
                last.then_inc(q_turned, 1)

            def body(before, cur, after):
                for n in range(G):
                    if cur and not before:
                        pe.wait_ge(w_split, n + 1)
                    if cur:
                        project(cur[0], cur[1], n)
                    late = cur if n >= LAG else before
                    if late:
                        turn(late[0], (n - LAG) % G)
                    if n == TURN_X and after:
                        head(after)

            batches(pe, head, body)


def phase_c_attention(nc, keep, io, wo):
    AHEAD = 4
    EXPS = 3
    RECIPROCAL = 2
    WEIGH = {2: -1, 6: 0, 10: 1, 14: 2}
    SPLIT_OUT = {3: -1, 7: 0, 11: 1, 15: 2}
    PROJECT = {0: -2, 4: -1, 8: 0, 12: 1}
    FINISH = 5
    SPLIT_K = {4: 0, 8: 1, 10: 2, 13: 3}
    SPLIT_Q = {6: 0, 9: 1, 12: 2, 14: 3}
    SPLIT_V, SPLIT_V_LOW = {8: 0, 10: 1, 12: 2}, {11: 0, 13: 1, 15: 2}
    with Memory(nc, "c") as m:
        q_raw = m.sb("q_raw", [P, H, S])
        k_raw = m.sb("k_raw", [P, G, TE])
        v_raw = m.sb("v_raw", [KP, KC, D])
        q = [m.sb(f"q_{n}", [P, 2, H, S], F32R) for n in ("hi", "lo")]
        k = [m.sb(f"k_{n}", [P, 2, G, TE], F32R) for n in ("hi", "lo")]
        v = [m.sb(f"v_{n}", [KP, 2, KC, D], F32R) for n in ("hi", "lo")]
        xin = m.sb("xin", [S, 2, D])
        xout = m.sb("xout", [S, 2, D])
        probs = m.sb("probs", [S, AHEAD, T])
        pT = [m.sb(f"pT_{n}", [KP, 2, KC, HPG, S], F32R) for n in ("hi", "lo")]
        oT = [m.sb(f"oT_{n}", [P, 2, HPG, S], F32R) for n in ("hi", "lo")]
        nmax = m.sb("nmax", [S, 2, H])
        sums = m.sb("sums", [S, 2, H])
        rsum = m.sb("rsum", [S, 2, H])
        score = [m.ps(f"score{n}", [P, 512]) for n in range(AHEAD)]
        turned = [m.ps(f"turned{n}", [P, 512]) for n in range(2)]
        outp = m.ps("outp", [P, 512])
        y = m.ps("y", [P, 512])
        q_loaded, k_loaded, v_loaded = m.sem("q_loaded"), m.sem("k_loaded"), m.sem("v_loaded")
        x_loaded = [m.sem(f"x_loaded{n}") for n in range(2)]
        x_stored = [m.sem(f"x_stored{n}") for n in range(2)]
        q_hi, q_split, k_hi, k_split, v_hi, v_split = (m.sem(n) for n in ("q_hi", "q_split", "k_hi", "k_split", "v_hi", "v_split"))
        scores_ready, max_done, probs_ready, rsum_done, scaled = (m.sem(n) for n in ("scores_ready", "max_done", "probs_ready", "rsum_done", "scaled"))
        turned_ready, pT_hi, pT_split = m.sem("turned_ready"), m.sem("pT_hi"), m.sem("pT_split")
        out_ready, o_hi, o_split, y_ready, x_done = (m.sem(n) for n in ("out_ready", "o_hi", "o_split", "y_ready", "x_done"))
        norm = norm_semaphores(m)
        block = m.block()

        def group(slots, h, before, cur):
            if h not in slots:
                return None
            which = before if slots[h] < 0 else cur
            return which and (*which, slots[h] % G)

        @block.sync
        def _(sp):
            def load(b, p, half):
                sp.dma_start(q_raw[:, :, :], io["q1"][b, :, :, :]).then_inc(q_loaded, 16)
                sp.dma_start(k_raw[:, :, :], io["k1"][b, :, :, :]).then_inc(k_loaded, 16)

                sp.dma_start(v_raw[:, :, :], io["v1"][b, :, :, :]).then_inc(v_loaded, 16)

            def load_x(b, p, half):
                sp.dma_start(xin[:, p, :], io["x2"][b, :, :]).then_inc(x_loaded[p], 16)

            def head(cur):
                load(*cur)
                load_x(*cur)

            def body(before, cur, after):
                if after:
                    sp.wait_ge(q_split, G * cur[0] + G)
                    sp.wait_ge(k_split, G * cur[0] + G)
                    sp.wait_ge(v_split, KC * cur[0] + KC)
                    load(*after)
                if before:
                    b, p, half = before
                    sp.wait_ge(x_done, b + 1 + 1)
                    sp.dma_start(io["x3"][b, :, :], xout[:, p, :]).then_inc(x_stored[p], 16)
                if after:
                    load_x(*after)

            batches(sp, head, body)
            for p in range(2):
                sp.wait_ge(x_stored[p], 16 * (B // 2) + 16)

        @block.gpsimd
        def _(pool):
            def scale(b, p, h):
                pool.wait_ge(rsum_done, H * b + h + 1)
                pool.tensor_tensor(probs[:, h % AHEAD, :], probs[:, h % AHEAD, :], rsum[:, p, h:h + 1].broadcast_to([S, T]),
                                   ALU.mult).then_inc(scaled, 1)

            def values_lo(b, p, c):
                pool.wait_ge(v_hi, KC * b + c + 1)
                pool.tensor_tensor(v[1][:, p, c, :], v_raw[:, c, :], f32(v[0][:, p, c, :]), ALU.subtract).then_inc(v_split, 1)

            def head(cur):
                for c in range(KC):
                    values_lo(cur[0], cur[1], c)

            def body(before, cur, after):
                for h in range(H if cur else 0):
                    scale(cur[0], cur[1], h)
                    if h in SPLIT_V_LOW and after:
                        values_lo(after[0], after[1], SPLIT_V_LOW[h])

            batches(pool, head, body)
            norm_rstd(pool, keep, norm)

        @block.scalar
        def _(act):
            act.sem_inc(probs_ready, AHEAD)

            def queries_hi(b, p, g):
                act.wait_ge(q_loaded, 16 * b + 16)
                act.activation(q[0][:, p, HPG * g:HPG * g + HPG, :], q_raw[:, HPG * g:HPG * g + HPG, :], ACT.Copy).then_inc(q_hi, 1)

            def keys_hi(b, p, g):
                act.wait_ge(k_loaded, 16 * b + 16)
                act.activation(k[0][:, p, g, :], k_raw[:, g, :], ACT.Copy).then_inc(k_hi, 1)

            def values_hi(b, p, c):
                act.wait_ge(v_loaded, 16 * b + 16)
                act.activation(v[0][:, p, c, :], v_raw[:, c, :], ACT.Copy).then_inc(v_hi, 1)

            def head(cur):
                for g in range(G):
                    keys_hi(cur[0], cur[1], g)
                    queries_hi(cur[0], cur[1], g)
                for c in range(KC):
                    values_hi(cur[0], cur[1], c)

            def exps(b, p, h):
                act.wait_ge(max_done, H * b + h + 1)
                act.wait_ge(turned_ready, H * b + h + 1)
                act.activation(probs[:, h % AHEAD, :], score[h % AHEAD][0:S, 0:T], ACT.Exp, bias=nmax[:, p, h:h + 1],
                               accum_out=sums[:, p, h:h + 1]).then_inc(probs_ready, 1)

            def probs_hi(b, h):
                g, j = divmod(h, HPG)
                act.wait_ge(turned_ready, H * b + h + 1 + AHEAD)
                src = turned[h % 2][0:KP, 0:KC * S].rearrange("p (c s) -> p c s", c=KC)
                act.activation(pT[0][:, g % 2, :, j, :], src, ACT.Copy).then_inc(pT_hi, 1)

            def out_hi(b, p, half, g):
                act.wait_ge(out_ready, G * b + g + 1)
                act.activation(oT[0][:, g % 2, :, :], outp[:, 0:HPG * S].rearrange("p (j s) -> p j s", j=HPG), ACT.Copy).then_inc(o_hi, 1)

            def body(before, cur, after):
                if cur and not before:
                    for h in range(EXPS):
                        exps(cur[0], cur[1], h)
                for h in range(H):
                    done = group(SPLIT_OUT, h, before, cur)
                    if done:
                        out_hi(*done)
                    if cur:
                        probs_hi(cur[0], h)
                        if h + EXPS < H:
                            exps(cur[0], cur[1], h + EXPS)
                        elif after:
                            exps(after[0], after[1], h + EXPS - H)
                    if h in SPLIT_K and after:
                        keys_hi(after[0], after[1], SPLIT_K[h])
                    if h in SPLIT_Q and after:
                        queries_hi(after[0], after[1], SPLIT_Q[h])
                    if h in SPLIT_V and after:
                        values_hi(after[0], after[1], SPLIT_V[h])

            batches(act, head, body)

        @block.vector
        def _(dve):
            for signal, credit in ((pT_split, 2), (o_split, 1), (x_done, 1)):
                dve.sem_inc(signal, credit)
            for n in range(2):
                dve.sem_inc(x_stored[n], 16)

            def queries_lo(b, p, g):
                dve.wait_ge(q_hi, G * b + g + 1)
                heads = slice(HPG * g, HPG * g + HPG)
                dve.tensor_tensor(q[1][:, p, heads, :], q_raw[:, heads, :], f32(q[0][:, p, heads, :]), ALU.subtract).then_inc(q_split, 1)

            def keys_lo(b, p, g):
                dve.wait_ge(k_hi, G * b + g + 1)
                dve.tensor_tensor(k[1][:, p, g, :], k_raw[:, g, :], f32(k[0][:, p, g, :]), ALU.subtract).then_inc(k_split, 1)

            def head(cur):
                for g in range(G):
                    keys_lo(cur[0], cur[1], g)
                    queries_lo(cur[0], cur[1], g)

            def maximum(b, p, h):
                dve.wait_ge(scores_ready, H * b + h + 1)
                dve.tensor_reduce(nmax[:, p, h:h + 1], score[h % AHEAD][0:S, 0:T], axis=AX.X, op=ALU.max, negate=True).then_inc(max_done, 1)

            def reciprocal(b, p, h):
                dve.wait_ge(probs_ready, H * b + h + 1 + AHEAD)
                dve.reciprocal(rsum[:, p, h:h + 1], sums[:, p, h:h + 1]).then_inc(rsum_done, 1)

            def probs_lo(b, h):
                g, j = divmod(h, HPG)
                dve.wait_ge(pT_hi, H * b + h + 1)
                src = turned[h % 2][0:KP, 0:KC * S].rearrange("p (c s) -> p c s", c=KC)
                dve.tensor_tensor(pT[1][:, g % 2, :, j, :], src, f32(pT[0][:, g % 2, :, j, :]), ALU.subtract).then_inc(pT_split, 1)

            def out_lo(b, p, half, g):
                dve.wait_ge(o_hi, G * b + g + 1)
                dve.tensor_tensor(oT[1][:, g % 2, :, :], outp[:, 0:HPG * S].rearrange("p (j s) -> p j s", j=HPG),
                                  f32(oT[0][:, g % 2, :, :]), ALU.subtract).then_inc(o_split, 1)

            def finish(b, p, half):
                dve.wait_ge(y_ready, b + 1)
                dve.wait_ge(x_loaded[p], 16 * half + 16)
                dve.wait_ge(x_stored[p], 16 * half + 16)
                dve.scalar_tensor_tensor(out=xout[:, p, :], in0=y[0:S, :], scalar=keep["gates"][0:S, 1:2], in1=xin[:, p, :],
                                         op0=ALU.mult, op1=ALU.add).then_inc(x_done, 1)
                dve.wait_ge(x_done, b + 1 + 1)
                dve.bn_stats(keep["bn"][:, b, :], xout[:, p, :]).then_inc(norm["counted"], 1)

            def body(before, cur, after):
                def ahead(what, n):
                    if n < H:
                        what(cur[0], cur[1], n)
                    elif after:
                        what(after[0], after[1], n - H)

                if cur and not before:
                    for h in range(AHEAD):
                        maximum(cur[0], cur[1], h)
                    for h in range(RECIPROCAL):
                        reciprocal(cur[0], cur[1], h)
                for h in range(H):
                    done = group(SPLIT_OUT, h, before, cur)
                    if done:
                        out_lo(*done)
                    if cur:
                        ahead(reciprocal, h + RECIPROCAL)
                        ahead(maximum, h + AHEAD)
                        probs_lo(cur[0], h)
                    if h == FINISH and before:
                        finish(*before)
                    if h in SPLIT_K and after:
                        keys_lo(after[0], after[1], SPLIT_K[h])
                    if h in SPLIT_Q and after:
                        queries_lo(after[0], after[1], SPLIT_Q[h])

            batches(dve, head, body)
            norm_moments(dve, keep, norm)

        @block.tensor
        def _(pe):
            pe.sem_inc(turned_ready, AHEAD)
            ident = keep["ident"]

            def scores(b, p, h):
                if h % HPG == 0:
                    pe.wait_ge(q_split, G * b + h // HPG + 1)
                    pe.wait_ge(k_split, G * b + h // HPG + 1)
                pe.wait_ge(probs_ready, H * b + h + 1)
                for n, (s, r) in enumerate(PASSES):
                    last = pe.matmul(score[h % AHEAD][0:S, 0:TE], q[s][:, p, h, :], k[r][:, p, h // HPG, :],
                                     start=n == 0, stop=n == len(PASSES) - 1)
                last.then_inc(scores_ready, 1)

            def turn(b, h):
                pe.wait_ge(scaled, H * b + h + 1)
                pe.wait_ge(pT_split, H * b + h + 1)
                for c in range(KC):
                    last = pe.transpose(turned[h % 2][0:KP, c * S:(c + 1) * S], probs[:, h % AHEAD, c * KP:(c + 1) * KP], ident[0:S, 0:S])
                last.then_inc(turned_ready, 1)

            def weigh(b, p, half, g):
                pe.wait_ge(pT_split, H * b + HPG * (g + 1) + 2)
                pe.wait_ge(o_split, G * b + g + 1)
                if g == 0:
                    pe.wait_ge(v_split, KC * b + KC)
                for n, (s, r) in enumerate(PASSES):
                    for c in range(KC):
                        last = pe.matmul(outp[:, 0:HPG * S], v[s][:, p, c, g * P:(g + 1) * P],
                                         pT[r][:, g % 2, c, :, :].rearrange("p j s -> p (j s)"),
                                         start=n == 0 and c == 0, stop=n == len(PASSES) - 1 and c == KC - 1)
                last.then_inc(out_ready, 1)

            def project(b, p, half, g):
                pe.wait_ge(o_split, G * b + g + 1 + 1)
                if g == 0:
                    pe.wait_ge(x_done, b + 1)
                for n, (s, r) in enumerate(PASSES):
                    for j in range(HPG):
                        last = pe.matmul(y[0:S, :], oT[s][:, g % 2, j, :], wo[r][:, HPG * g + j, :],
                                         start=g == 0 and n == 0 and j == 0, stop=g == G - 1 and n == len(PASSES) - 1 and j == HPG - 1)
                if g == G - 1:
                    last.then_inc(y_ready, 1)

            def body(before, cur, after):
                if cur and not before:
                    for h in range(AHEAD):
                        scores(cur[0], cur[1], h)
                for h in range(H):
                    if cur:
                        turn(cur[0], h)
                        if h + AHEAD < H:
                            scores(cur[0], cur[1], h + AHEAD)
                        elif after:
                            scores(after[0], after[1], h + AHEAD - H)
                    done = group(WEIGH, h, before, cur)
                    if done:
                        weigh(*done)
                    done = group(PROJECT, h, before, cur)
                    if done:
                        project(*done)

            batches(pe, lambda cur: None, body)


def phase_d(nc, keep, io):
    with Memory(nc, "e") as outer:
        qkv = {
            "q": outer.sb("q", [P, G, B * S]),
            "k": outer.sb("k", [P, G, B * S]),
            "v": outer.sb("v", [S, B, D]),
        }
        phase_d_project(nc, keep, io, qkv)
        phase_d_attention(nc, keep, io, qkv)


def phase_d_project(nc, keep, io, qkv):
    THRESHOLD = 0.1
    CLIP = 1e-8
    QS, KS, V0, QL, KL = 0, H * DS, 2 * H * DS, 2 * H * DS + D, 2 * H * DS + D + H * R
    WIDTH = KL + H * R
    BLOCKS = 2 * G + BPG
    RAW = 3
    NEXT = 2
    with Memory(nc, "g") as m:
        raw = m.sb("raw", [P, RAW, WIDTH])
        wf = m.sb("wf", [P, 2, 2 * D])
        low = m.sb("low", [P, 2, 2, H, R])
        w = [m.sb(f"w_{n}", [P, DC, 3 * D], F32R) for n in ("hi", "lo")]
        head_raw = m.sb("head_raw", [P, 2, H])
        head_clip = m.sb("head_clip", [P, 2, H])
        head_scale = m.sb("head_scale", [P, 2, H])
        half = m.sb("half", [P, 2, H])
        swap = m.sb("swap", [P, H, R], U8)
        xn = m.sb("xn", [S, BPG, D])
        xT = [m.sb(f"xT_{n}", [P, 2, DC, GS], F32R) for n in ("hi", "lo")]
        x_bank = [m.ps(f"x_bank{n}", [P, 512]) for n in range(2)]
        out_bank = [m.ps(f"out_bank{n}", [P, 512]) for n in range(4)]
        head_loaded, clipped, scaled, swapped = (m.sem(n) for n in ("head_loaded", "clipped", "scaled", "swapped"))
        w_loaded = [m.sem(f"w_loaded{n}") for n in range(DC)]
        low_done, w_done, w_chosen, w_hi, w_split = (m.sem(n) for n in ("low_done", "w_done", "w_chosen", "w_hi", "w_split"))
        x_loaded, xn_done, x_turned, x_hi, x_split = (m.sem(n) for n in ("x_loaded", "xn_done", "x_turned", "x_hi", "x_split"))
        ready, copied = m.sem("ready"), [m.sem(f"copied{n}") for n in range(2)]
        block = m.block()

        def groups(eng, head, body):
            head((0, 0))
            body((0, 0), (1, 1))
            with eng.Fori(0, NG // 2 - 1) as i:
                body((2 * i + 1, 1), (2 * i + 2, 0))
                body((2 * i + 2, 0), (2 * i + 3, 1))
            body((NG - 1, 1), None)

        @block.sync
        def _(sp):
            for n, name in enumerate(("w_std", "w_rec")):
                with nc.allow_non_contiguous_dma(reason="a few words"):
                    sp.dma_start(head_raw[:, n, :], io[name].rearrange("(a n) -> a n", a=1).broadcast_to([P, H])).then_inc(head_loaded, 16)

            def head(cur):
                sp.wait_ge(x_turned, DC * cur[0] + 1)
                first = BPG * cur[0]
                sp.dma_start(xn[:, :, :], io["x3"][bass.ds(first, BPG), :, :].rearrange("b s d -> s b d")).then_inc(x_loaded, 16)
                if isinstance(cur[0], int) and cur[0] == 0:
                    for c in range(DC):
                        if c >= RAW:
                            sp.wait_ge(w_split, c - RAW + 1)
                        sp.dma_start(raw[:, c % RAW, :], io["Wa"].rearrange("(c p) n -> c p n", p=P)[c, :, :]).then_inc(w_loaded[c], 16)

            groups(sp, head, lambda cur, after: after and head(after))

        @block.gpsimd
        def _(pool):
            pool.memset(half[:, :, :], 0.5).then_inc(clipped, 1)
            pool.wait_ge(clipped, 2)
            pool.tensor_tensor(head_scale[:, :, :], head_clip[:, :, :], half[:, :, :], ALU.pow).then_inc(scaled, 1)

        def columns(c, n, width):
            return wf[:, c % 2, n * D:(n + 1) * D].rearrange("p (h d) -> p h d", h=H)[:, :, width]

        @block.scalar
        def _(act):
            act.sem_inc(copied[0], 2)

            def x_hi_chunk(cur, c):
                act.wait_ge(x_turned, DC * cur[0] + c + 1 + 1)
                act.activation(xT[0][:, cur[1], c, :], x_bank[c % 2][:, 0:GS], ACT.Copy).then_inc(x_hi, 1)

            for c in range(DC):
                act.wait_ge(w_loaded[c], 16)
                act.activation(w[0][:, c, 2 * D:], raw[:, c % RAW, V0:V0 + D], ACT.Copy).then_inc(w_hi, 1)
                act.wait_ge(w_chosen, 2 * c + 2)
                act.activation(w[0][:, c, 0:2 * D], wf[:, c % 2, :], ACT.Copy).then_inc(w_hi, 1)
                x_hi_chunk((0, 0), c)

            def head(cur):
                for c in range(DC):
                    x_hi_chunk(cur, c)

            def body(cur, after):
                g = cur[0]
                for n in range(0, BLOCKS, 2):
                    act.wait_ge(ready, BLOCKS * g + n + 1)
                    if n < G:
                        act.activation(qkv["q"][:, n, bass.ds(g * GS, GS)], out_bank[n % 4][:, 0:GS], ACT.Copy,
                                       scale=float(HD) ** -0.5).then_inc(copied[0], 1)
                    elif n < 2 * G:
                        act.activation(qkv["k"][:, n - G, bass.ds(g * GS, GS)], out_bank[n % 4][:, 0:GS], ACT.Copy).then_inc(copied[0], 1)
                    else:
                        act.activation(qkv["v"][:, BPG * g + n - 2 * G, :], out_bank[n % 4][0:S, :], ACT.Copy).then_inc(copied[0], 1)
                    if n == NEXT and after:
                        head(after)

            groups(act, lambda cur: None, body)

        @block.vector
        def _(dve):
            dve.sem_inc(copied[1], 2)
            dve.sem_inc(x_split, 2)
            dve.wait_ge(head_loaded, 32)
            dve.tensor_scalar(head_clip[:, :, :], head_raw[:, :, :], CLIP, None, ALU.max).then_inc(clipped, 1)
            dve.tensor_scalar(swap[:, :, :], head_raw[:, 1, :].unsqueeze(2).broadcast_to([P, H, R]), THRESHOLD, None, ALU.is_gt).then_inc(swapped, 1)

            def normalize(cur):
                g = cur[0]
                dve.wait_ge(x_loaded, 16 * g + 16)
                for n in range(BPG):
                    b = BPG * g + n
                    last = dve.tensor_scalar(xn[:, n, :], xn[:, n, :], keep["mv"][:, b, 0:1], keep["rstd"][:, b, :],
                                             ALU.subtract, ALU.mult)
                last.then_inc(xn_done, 1)

            def x_lo(cur, c):
                dve.wait_ge(x_hi, DC * cur[0] + c + 1)
                dve.tensor_tensor(xT[1][:, cur[1], c, :], x_bank[c % 2][:, 0:GS], f32(xT[0][:, cur[1], c, :]), ALU.subtract).then_inc(x_split, 1)

            def head(cur):
                normalize(cur)
                for c in range(DC):
                    x_lo(cur, c)

            def order_weights(c):
                dve.wait_ge(scaled, 1)
                dve.wait_ge(w_loaded[c], 16)
                for n, first in enumerate((QL, KL)):
                    dve.tensor_tensor(low[:, c % 2, n, :, :], raw[:, c % RAW, first:first + H * R].rearrange("p (h r) -> p h r", h=H),
                                      head_scale[:, 1, :].unsqueeze(2).broadcast_to([P, H, R]), ALU.mult).then_inc(low_done, 1)
                if c > 1:
                    dve.wait_ge(w_split, c - 1)
                for n, first in enumerate((QS, KS)):
                    dve.tensor_tensor(columns(c, n, slice(0, DS)), raw[:, c % RAW, first:first + H * DS].rearrange("p (h d) -> p h d", h=H),
                                      head_scale[:, 0, :].unsqueeze(2).broadcast_to([P, H, DS]), ALU.mult)
                dve.wait_ge(low_done, 2 * c + 2)
                for n in range(2):
                    dve.tensor_copy(columns(c, n, slice(DS, HD)), low[:, c % 2, n, :, :]).then_inc(w_done, 1)
                dve.wait_ge(w_done, 2 * c + 2)
                dve.wait_ge(swapped, 1)
                for n in range(2):
                    dve.copy_predicated(columns(c, n, slice(DS, HD)), swap[:, :, :], low[:, c % 2, 1 - n, :, :]).then_inc(w_chosen, 1)

            def weights_lo(c):
                dve.wait_ge(w_hi, 2 * c + 2)
                dve.tensor_tensor(w[1][:, c, 0:2 * D], wf[:, c % 2, :], f32(w[0][:, c, 0:2 * D]), ALU.subtract)
                dve.tensor_tensor(w[1][:, c, 2 * D:], raw[:, c % RAW, V0:V0 + D], f32(w[0][:, c, 2 * D:]), ALU.subtract).then_inc(w_split, 1)

            def weights():
                normalize((0, 0))
                order_weights(0)
                for c in range(DC):
                    if c + 1 < DC:
                        order_weights(c + 1)
                    weights_lo(c)
                    x_lo((0, 0), c)

            def body(cur, after):
                g = cur[0]
                for n in range(1, BLOCKS, 2):
                    dve.wait_ge(ready, BLOCKS * g + n + 1)
                    if n < G:
                        dve.tensor_scalar(qkv["q"][:, n, bass.ds(g * GS, GS)], out_bank[n % 4][:, 0:GS], float(HD) ** -0.5, None,
                                          ALU.mult).then_inc(copied[1], 1)
                    elif n < 2 * G:
                        dve.tensor_copy(qkv["k"][:, n - G, bass.ds(g * GS, GS)], out_bank[n % 4][:, 0:GS]).then_inc(copied[1], 1)
                    else:
                        dve.tensor_copy(qkv["v"][:, BPG * g + n - 2 * G, :], out_bank[n % 4][0:S, :]).then_inc(copied[1], 1)
                    if n == NEXT - 1 and after:
                        head(after)

            weights()
            groups(dve, lambda cur: None, body)

        @block.tensor
        def _(pe):
            pe.sem_inc(x_turned, 1)
            ident = keep["ident"]

            def head(cur):
                g = cur[0]
                pe.wait_ge(xn_done, g + 1)
                for c in range(DC):
                    pe.wait_ge(x_split, DC * g + c + 1)
                    for n in range(BPG):
                        last = pe.transpose(x_bank[c % 2][:, n * S:(n + 1) * S], xn[:, n, c * P:(c + 1) * P], ident[0:S, 0:S])
                    last.then_inc(x_turned, 1)

            def body(cur, after):
                g, p = cur
                if isinstance(g, int) and g == 0:
                    pe.wait_ge(w_split, DC)
                pe.wait_ge(x_split, DC * g + DC + 2)
                for n in range(BLOCKS):
                    pe.wait_ge(copied[n % 2], BLOCKS // 2 * g + n // 2 + 1)
                    for k, (s, r) in enumerate(PASSES):
                        for c in range(DC):
                            flags = dict(start=k == 0 and c == 0, stop=k == len(PASSES) - 1 and c == DC - 1)
                            if n < 2 * G:
                                last = pe.matmul(out_bank[n % 4][:, 0:GS], w[s][:, c, n * P:(n + 1) * P], xT[r][:, p, c, :], **flags)
                            else:
                                b = n - 2 * G
                                last = pe.matmul(out_bank[n % 4][0:S, :], xT[s][:, p, c, b * S:(b + 1) * S], w[r][:, c, 2 * D:], **flags)
                    last.then_inc(ready, 1)
                    if n == NEXT and after:
                        head(after)

            groups(pe, head, body)


def phase_d_attention(nc, keep, io, qkv):
    AHEAD = 3
    EXPS = 2
    LOWEST = -3.4028234663852886e38
    SPLIT_Q, SPLIT_K = 1, {1: (0,), 2: (1, 2), 3: (3,)}
    with Memory(nc, "d") as m:
        wp_raw = m.sb("wp_raw", [P, DC, D])
        wp = [m.sb(f"wp_{n}", [P, DC, D], F32R) for n in ("hi", "lo")]
        lowest = m.sb("lowest", [S, S])
        q = [m.sb(f"q_{n}", [P, 2, G, S], F32R) for n in ("hi", "lo")]
        k = [m.sb(f"k_{n}", [P, 2, G, HPG, S], F32R) for n in ("hi", "lo")]
        probs = m.sb("probs", [S, G, HPG, S])
        pT = m.sb("pT", [S, 2, HPG, S])
        nmax = m.sb("nmax", [S, 2, H])
        sums = m.sb("sums", [S, 2, H])
        rsum = m.sb("rsum", [S, H])
        on = m.sb("on", [S, D])
        oT = [m.sb(f"oT_{n}", [P, DC, S], F32R) for n in ("hi", "lo")]
        xin = m.sb("xin", [S, 2, D])
        xout = m.sb("xout", [S, 2, D])
        score = [m.ps(f"score{n}", [P, 512]) for n in range(G)]
        turned = m.ps("turned", [P, 512])
        outp = [m.ps(f"outp{n}", [P, 512]) for n in range(2)]
        tail = m.ps("tail", [P, 512])
        wp_loaded, wp_hi, wp_split, cleared = m.sem("wp_loaded"), m.sem("wp_hi"), m.sem("wp_split"), m.sem("cleared")
        x_loaded = [m.sem(f"x_loaded{n}") for n in range(2)]
        x_stored = [m.sem(f"x_stored{n}") for n in range(2)]
        q_hi, q_split, k_hi, k_split = m.sem("q_hi"), m.sem("q_split"), m.sem("k_hi"), m.sem("k_split")
        scores_ready, masked, max_done, probs_ready = (m.sem(n) for n in ("scores_ready", "masked", "max_done", "probs_ready"))
        turned_ready, pT_copied, out_ready, rsum_done, on_done = (m.sem(n) for n in ("turned_ready", "pT_copied", "out_ready", "rsum_done", "on_done"))
        o_turned, o_hi, o_split, y_ready, x_done = (m.sem(n) for n in ("o_turned", "o_hi", "o_split", "y_ready", "x_done"))
        block = m.block()

        def rounds(eng, head, body):
            head((0, 0, 0))
            head((1, 1, 0))
            body(None, (0, 0, 0), (1, 1, 0), (2, 0, 1))
            with eng.Fori(0, B // 2 - 2) as i:
                body((2 * i, 0, i), (2 * i + 1, 1, i), (2 * i + 2, 0, i + 1), (2 * i + 3, 1, i + 1))
                body((2 * i + 1, 1, i), (2 * i + 2, 0, i + 1), (2 * i + 3, 1, i + 1), (2 * i + 4, 0, i + 2))
            last = B // 2 - 1
            body((B - 4, 0, last - 1), (B - 3, 1, last - 1), (B - 2, 0, last), (B - 1, 1, last))
            body((B - 3, 1, last - 1), (B - 2, 0, last), (B - 1, 1, last), None)
            body((B - 2, 0, last), (B - 1, 1, last), None, None)
            body((B - 1, 1, last), None, None, None)

        @block.sync
        def _(sp):
            sp.dma_start(wp_raw[:, :, :], io["Wp"].rearrange("(c p) n -> p c n", p=P)).then_inc(wp_loaded, 16)

            def load(b, p, half):
                sp.dma_start(xin[:, p, :], io["x3"][b, :, :]).then_inc(x_loaded[p], 16)

            def body(before, cur, after, further):
                if before:
                    b, p, half = before
                    sp.wait_ge(x_done, b + 1 + 1)
                    sp.dma_start(io["out"][b, :, :], xout[:, p, :]).then_inc(x_stored[p], 16)
                if after and before:
                    load(*after)

            rounds(sp, lambda cur: load(*cur), body)
            for p in range(2):
                sp.wait_ge(x_stored[p], 16 * (B // 2) + 16)

        @block.gpsimd
        def _(pool):
            for part in k:
                pool.memset(f32(part[:, :, :, :, :]), 0.0).then_inc(cleared, 1)
            pool.memset(lowest[:, :], LOWEST).then_inc(cleared, 1)
            pool.wait_ge(cleared, 3)

            def keys_lo(b, p, j):
                pool.wait_ge(k_hi, HPG * b + j + 1)
                r = slice(HD * j, HD * j + HD)
                pool.tensor_tensor(k[1][r, p, :, j, :], qkv["k"][r, :, bass.ds(b * S, S)], f32(k[0][r, p, :, j, :]), ALU.subtract).then_inc(k_split, 1)

            def head(cur):
                for j in range(HPG):
                    keys_lo(cur[0], cur[1], j)

            rounds(pool, head, lambda before, cur, after, further: further and head(further))

        @block.scalar
        def _(act):
            act.sem_inc(probs_ready, G)
            act.wait_ge(cleared, 3)

            def keys_hi(b, p, j):
                r = slice(HD * j, HD * j + HD)
                act.activation(k[0][r, p, :, j, :], qkv["k"][r, :, bass.ds(b * S, S)], ACT.Copy).then_inc(k_hi, 1)

            def queries_hi(b, p):
                act.activation(q[0][:, p, :, :], qkv["q"][:, :, bass.ds(b * S, S)], ACT.Copy).then_inc(q_hi, 1)

            def head(cur):
                queries_hi(cur[0], cur[1])
                for j in range(HPG):
                    keys_hi(cur[0], cur[1], j)

            def exps(b, p, g):
                t = G * b + g + 1
                act.wait_ge(max_done, t)
                act.wait_ge(turned_ready, t)
                for j in range(HPG):
                    h = HPG * g + j
                    last = act.activation(probs[:, g, j, :], score[g][0:S, j * S:(j + 1) * S], ACT.Exp,
                                          bias=nmax[:, p, h:h + 1], accum_out=sums[:, p, h:h + 1])
                last.then_inc(probs_ready, 1)

            def body(before, cur, after, further):
                if cur and not before:
                    for g in range(EXPS):
                        exps(cur[0], cur[1], g)
                for g in range(G):
                    if cur and g + EXPS < G:
                        exps(cur[0], cur[1], g + EXPS)
                    elif after and g + EXPS >= G:
                        exps(after[0], after[1], g + EXPS - G)
                    if g == 2 and before:
                        act.wait_ge(o_turned, before[0] + 1)
                        act.activation(oT[0][:, :, :], tail[:, 0:DC * S].rearrange("p (c s) -> p c s", c=DC), ACT.Copy).then_inc(o_hi, 1)
                    if g == SPLIT_Q and further:
                        queries_hi(further[0], further[1])
                    for j in SPLIT_K.get(g, ()) if further else ():
                        keys_hi(further[0], further[1], j)
                if cur and not before:
                    act.wait_ge(wp_loaded, 16)
                    act.activation(wp[0][:, :, :], wp_raw[:, :, :], ACT.Copy).then_inc(wp_hi, 1)

            rounds(act, head, body)

        @block.vector
        def _(dve):
            for signal, credit in ((on_done, 2), (x_done, 1), (pT_copied, 1)):
                dve.sem_inc(signal, credit)
            for n in range(2):
                dve.sem_inc(x_stored[n], 16)

            def queries_lo(b, p):
                dve.wait_ge(q_hi, b + 1)
                dve.tensor_tensor(q[1][:, p, :, :], qkv["q"][:, :, bass.ds(b * S, S)], f32(q[0][:, p, :, :]), ALU.subtract).then_inc(q_split, 1)

            def maximum(b, p, g):
                t = G * b + g + 1
                four = score[g][0:S, 0:HPG * S].rearrange("p (j s) -> p j s", j=HPG)
                t = t if isinstance(t, int) else dve.to_reg(t)
                dve.wait_ge(cleared, 3)
                dve.wait_ge(scores_ready, t)
                dve.copy_predicated(four, keep["later"][:, :].unsqueeze(1).broadcast_to([S, HPG, S]),
                                    lowest[:, :].unsqueeze(1).broadcast_to([S, HPG, S])).then_inc(masked, 1)
                dve.wait_ge(masked, G * b + g + 1)
                dve.tensor_reduce(nmax[:, p, HPG * g:HPG * g + HPG], four, axis=AX.X, op=ALU.max, negate=True).then_inc(max_done, 1)

            def probs_copy(b, g):
                t = G * b + g + 1
                dve.wait_ge(turned_ready, t + G)
                dve.tensor_copy(pT[:, g % 2, :, :], turned[0:S, 0:HPG * S].rearrange("p (j s) -> p j s", j=HPG)).then_inc(pT_copied, 1)

            def reciprocals(b, p):
                dve.wait_ge(probs_ready, G * b + G + G)
                dve.reciprocal(rsum[:, :], sums[:, p, :]).then_inc(rsum_done, 1)

            def normalize_out(b, p, half):
                dve.wait_ge(out_ready, b + 1)
                dve.wait_ge(rsum_done, b + 1)
                dve.tensor_tensor(on[:, :].rearrange("p (h d) -> p h d", h=H), outp[p][0:S, :].rearrange("p (h d) -> p h d", h=H),
                                  rsum[:, :].unsqueeze(2).broadcast_to([S, H, HD]), ALU.mult).then_inc(on_done, 1)

            def out_lo(b, p, half):
                dve.wait_ge(o_hi, b + 1)
                dve.tensor_tensor(oT[1][:, :, :], tail[:, 0:DC * S].rearrange("p (c s) -> p c s", c=DC), f32(oT[0][:, :, :]),
                                  ALU.subtract).then_inc(o_split, 1)

            def finish(b, p, half):
                dve.wait_ge(y_ready, b + 1)
                dve.wait_ge(x_loaded[p], 16 * half + 16)
                dve.wait_ge(x_stored[p], 16 * half + 16)
                dve.scalar_tensor_tensor(out=xout[:, p, :], in0=tail[0:S, :], scalar=keep["gates"][0:S, 3:4], in1=xin[:, p, :],
                                         op0=ALU.mult, op1=ALU.add).then_inc(x_done, 1)

            def body(before, cur, after, further):
                if cur and not before:
                    for g in range(AHEAD):
                        maximum(cur[0], cur[1], g)
                for g in range(G):
                    if g == 1 and before:
                        normalize_out(*before)
                    if cur:
                        probs_copy(cur[0], g)
                    if cur and g + AHEAD < G:
                        maximum(cur[0], cur[1], g + AHEAD)
                    elif after and g + AHEAD >= G:
                        maximum(after[0], after[1], g + AHEAD - G)
                    if g == 2 and before:
                        out_lo(*before)
                    elif g == 3 and before:
                        finish(*before)
                    if g == 3 and cur:
                        reciprocals(cur[0], cur[1])
                    if g == SPLIT_Q and further:
                        queries_lo(further[0], further[1])
                if cur and not before:
                    dve.wait_ge(wp_hi, 1)
                    dve.tensor_tensor(wp[1][:, :, :], wp_raw[:, :, :], f32(wp[0][:, :, :]), ALU.subtract).then_inc(wp_split, 1)

            rounds(dve, lambda cur: queries_lo(cur[0], cur[1]), body)

        @block.tensor
        def _(pe):
            pe.sem_inc(turned_ready, G)
            ident = keep["ident"]

            def scores(b, p, g):
                if g == 0:
                    pe.wait_ge(q_split, b + 1)
                    pe.wait_ge(k_split, HPG * b + HPG)
                pe.wait_ge(probs_ready, G * b + g + 1)
                for n, (s, r) in enumerate(PASSES):
                    last = pe.matmul(score[g][0:S, 0:HPG * S], q[s][:, p, g, :], k[r][:, p, g, :, :].rearrange("p j s -> p (j s)"),
                                     start=n == 0, stop=n == len(PASSES) - 1)
                last.then_inc(scores_ready, 1)

            def turn(b, g):
                t = G * b + g + 1
                pe.wait_ge(probs_ready, t + G)
                pe.wait_ge(pT_copied, t)
                for j in range(HPG):
                    last = pe.transpose(turned[0:S, j * S:(j + 1) * S], probs[:, g, j, :], ident[0:S, 0:S])
                last.then_inc(turned_ready, 1)

            def weigh(b, p, g):
                pe.wait_ge(pT_copied, G * b + g + 1 + 1)
                if g == 0:
                    pe.wait_ge(on_done, b + 1)
                for j in range(HPG):
                    h = HPG * g + j
                    last = pe.matmul(outp[p][0:S, h * HD:(h + 1) * HD], pT[:, g % 2, j, :], qkv["v"][:, b, h * HD:(h + 1) * HD],
                                     start=True, stop=True)
                if g == G - 1:
                    last.then_inc(out_ready, 1)

            def turn_out(b):
                pe.wait_ge(on_done, b + 1 + 2)
                pe.wait_ge(x_done, b + 1)
                for c in range(DC):
                    last = pe.transpose(tail[:, c * S:(c + 1) * S], on[:, c * P:(c + 1) * P], ident[0:S, 0:S])
                last.then_inc(o_turned, 1)

            def project(b):
                pe.wait_ge(wp_split, 1)
                pe.wait_ge(o_split, b + 1)
                for n, (s, r) in enumerate(PASSES):
                    for c in range(DC):
                        last = pe.matmul(tail[0:S, :], oT[s][:, c, :], wp[r][:, c, :], start=n == 0 and c == 0,
                                         stop=n == len(PASSES) - 1 and c == DC - 1)
                last.then_inc(y_ready, 1)

            def body(before, cur, after, further):
                if cur and not before:
                    for g in range(AHEAD):
                        scores(cur[0], cur[1], g)
                for g in range(G):
                    if g == 0 and before:
                        weigh(before[0], before[1], G - 1)
                    elif g > 0 and cur:
                        weigh(cur[0], cur[1], g - 1)
                    if cur:
                        turn(cur[0], g)
                    if cur and g + AHEAD < G:
                        scores(cur[0], cur[1], g + AHEAD)
                    elif after and g + AHEAD >= G:
                        scores(after[0], after[1], g + AHEAD - G)
                    if g == 2 and before:
                        turn_out(before[0])
                    elif g == 3 and before:
                        project(before[0])

            rounds(pe, lambda cur: None, body)


def flamingo_layers(nc, ins, out):
    io = dict(ins, out=out)
    for name in ("x1", "x2", "x3"):
        io[name] = nc.dram_tensor(name, [B, S, D], F32).ap()
    io["k1"] = nc.dram_tensor("k1", [B, P, G, TE], F32).ap()
    io["v1"] = nc.dram_tensor("v1", [B, KP, KC, D], F32).ap()
    io["q1"] = nc.dram_tensor("q1", [B, P, H, S], F32).ap()
    with Memory(nc, "keep") as m:
        keep = constants(m)
        setup_phase(nc, keep, io)
        phase_a(nc, keep, io)
        phase_b(nc, keep, io)
        phase_c(nc, keep, io)
        phase_d(nc, keep, io)


_INS = {"x": "x", "ctx": "ctx_2048", "g_xattn": "g_xattn", "g_ffn": "g_ffn"}
for _layer, _names in (("L0_ffn", ("SU_ug", "SU_dp", "Wscale_ug", "Wscale_dp", "W_up", "W_gate", "W_down")),
                       ("L1_xattn", ("Wq", "Wk", "Wv", "Wo", "q_norm_w", "k_norm_w")),
                       ("L1_ffn", ("Wa", "Wp", "w_std", "w_rec"))):
    for _name in _names:
        _INS[_name] = f"{_layer}_{_name}"


def kernel(**inputs):
    import numpy as _np
    import concourse.bacc as _bacc
    from concourse import mybir as _mybir
    from concourse.bass_utils import run_bass_kernel_spmd as _run

    nc = _bacc.Bacc("TRN2", target_bir_lowering=False, num_devices=1)
    arrays, ins = {}, {}
    for short, name in _INS.items():
        a = _np.ascontiguousarray(inputs[name])
        arrays[f"in_{name}_dram"] = a
        ins[short] = nc.dram_tensor(f"in_{name}_dram", a.shape, _mybir.dt.from_np(a.dtype), kind="ExternalInput").ap()
    out = nc.dram_tensor("out_0_dram", (B, S, D), F32, kind="ExternalOutput").ap()
    flamingo_layers(nc, ins, out)
    r = _run(nc, [arrays], core_ids=[0])
    return r.results[0]["out_0_dram"]
```

```python
from contextlib import ExitStack

import concourse.bass as bass
from concourse import mybir

F32 = mybir.dt.float32
F32R = mybir.dt.float32r
U8 = mybir.dt.uint8
ALU = mybir.AluOpType
ACT = mybir.ActivationFunctionType
AX = mybir.AxisListType

B, S, T, D = 16, 112, 375, 512
P = 128
DC = D // P
H = 16
HD = D // H
G = 4
HPG = H // G
KC, KP = 3, T // 3
TE = T + 1
XHD = 128
INTER = 2048
R = 8
DS = HD - R
LN_EPS = 1e-5
RMS_EPS = 1e-6
NORM_EARLY = B - 2
PASSES = ((0, 0), (0, 1), (1, 0))


def f32(ap):
    return ap.bitcast(F32)


class Memory:

    def __init__(self, nc, phase):
        self.nc, self.phase, self.stack = nc, phase, ExitStack()

    def __enter__(self):
        self.semaphores = []
        self.stack.__enter__()
        return self

    def __exit__(self, *what):
        done = self.stack.__exit__(*what)
        if self.semaphores:
            self.nc.clear_and_free_semaphores(self.semaphores)
            self.nc.all_engine_barrier()
        return done

    def sb(self, name, shape, dt=F32):
        return self.stack.enter_context(self.nc.sbuf_tensor(f"{self.phase}_{name}", shape, dt))

    def ps(self, name, shape, dt=F32):
        return self.stack.enter_context(self.nc.psum_tensor(f"{self.phase}_{name}", shape, dt))

    def sem(self, name):
        self.semaphores.append(self.nc.alloc_semaphore(f"{self.phase}_{name}"))
        return self.semaphores[-1]

    def block(self):
        return self.stack.enter_context(self.nc.Block())


def batches(eng, head, body, count=B):
    head((0, 0, 0))
    body(None, (0, 0, 0), (1, 1, 0))
    with eng.Fori(0, count // 2 - 1) as i:
        body((2 * i, 0, i), (2 * i + 1, 1, i), (2 * i + 2, 0, i + 1))
        body((2 * i + 1, 1, i), (2 * i + 2, 0, i + 1), (2 * i + 3, 1, i + 1))
    last = count // 2 - 1
    body((count - 2, 0, last), (count - 1, 1, last), None)
    body((count - 1, 1, last), None, None)


def constants(m):
    return {
        "ident": m.sb("ident", [P, P]),
        "hadamard": m.sb("hadamard", [P, P]),
        "neghalf": m.sb("neghalf", [P, H]),
        "rms_eps": m.sb("rms_eps", [P, G]),
        "ln_eps": m.sb("ln_eps", [P, 1]),
        "later": m.sb("later", [S, S], U8),
        "masked_score": m.sb("masked_score", [S, S]),
        "gates": m.sb("gates", [P, 4]),
        "qk_w": m.sb("qk_w", [P, 1]),
        "bn": m.sb("bn", [S, B, 6]),
        "mv": m.sb("mv", [S, B, 2]),
        "ve": m.sb("ve", [S, B]),
        "rstd": m.sb("rstd", [S, B, 1]),
    }


def setup_phase(nc, keep, io):
    with Memory(nc, "s") as m:
        qw = m.sb("qw", [P, 2])
        gate_raw = m.sb("gate_raw", [P, 4])
        had_tmp = m.sb("had_tmp", [P, P])
        ones, later = m.sb("ones", [P, P]), m.sb("later", [S, S])
        zeroed, made, w_loaded = m.sem("zeroed"), m.sem("made"), m.sem("w_loaded")
        block = m.block()

        @block.sync
        def _(sp):
            with nc.allow_non_contiguous_dma(reason="a few words"):
                sp.dma_start(qw[:, 0:1], io["q_norm_w"].rearrange("(p a) -> p a", a=1)).then_inc(w_loaded, 16)
                sp.dma_start(qw[:, 1:2], io["k_norm_w"].rearrange("(p a) -> p a", a=1)).then_inc(w_loaded, 16)
                for n, name in enumerate(("g_xattn", "g_ffn")):
                    row = io[name].rearrange("(a n) -> a n", a=1)
                    sp.dma_start(gate_raw[:, 2 * n:2 * n + 2], row.broadcast_to([P, 2])).then_inc(w_loaded, 16)

        @block.gpsimd
        def _(pool):
            pool.memset(keep["ident"][:, :], 0.0).then_inc(zeroed, 1)
            pool.memset(ones[:, :], 1.0).then_inc(zeroed, 1)
            pool.memset(keep["neghalf"][:, :], -0.5).then_inc(zeroed, 1)
            pool.memset(keep["rms_eps"][:, :], RMS_EPS).then_inc(zeroed, 1)
            pool.memset(keep["ln_eps"][:, :], LN_EPS).then_inc(zeroed, 1)
            pool.wait_ge(zeroed, 5)
            pool.affine_select(out=keep["ident"][:, :], in_=keep["ident"][:, :], compare_op=ALU.not_equal, fill=1.0,
                               base=0, pattern=[[-1, P]], channel_multiplier=1).then_inc(made, 1)
            pool.affine_select(out=later[:, :], in_=ones[0:S, 0:S], compare_op=ALU.is_gt, fill=0.0,
                               base=0, pattern=[[1, S]], channel_multiplier=-1).then_inc(made, 1)

        @block.scalar
        def _(act):
            act.wait_ge(w_loaded, 64)
            act.activation(keep["gates"][:, :], gate_raw[:, :], ACT.Tanh)

        @block.vector
        def _(dve):
            dve.memset(keep["masked_score"][:, :], -10000.0)
            dve.wait_ge(made, 2)
            dve.tensor_copy(keep["later"][:, :], later[:, :])
            stages = P.bit_length() - 1
            src = keep["ident"]
            for stage in range(stages):
                dst = had_tmp if (stages - stage) % 2 == 0 else keep["hadamard"]
                dve.wait_ge(made, 2 + 2 * stage)
                pair, out = (t[:, :].rearrange("p (a two n) -> p a two n", two=2, n=1 << stage) for t in (src, dst))
                dve.tensor_tensor(out[:, :, 0, :], pair[:, :, 0, :], pair[:, :, 1, :], ALU.add).then_inc(made, 1)
                dve.tensor_tensor(out[:, :, 1, :], pair[:, :, 0, :], pair[:, :, 1, :], ALU.subtract).then_inc(made, 1)
                src = dst
            dve.wait_ge(w_loaded, 64)
            dve.scalar_tensor_tensor(out=keep["qk_w"][:, :], in0=qw[:, 0:1], scalar=float(XHD) ** -0.5, in1=qw[:, 1:2],
                                     op0=ALU.mult, op1=ALU.mult)


def norm_semaphores(m):
    return {name: m.sem(name) for name in ("counted", "moments", "shifted")}


def norm_moments(dve, keep, norm, first=0, last=B):
    dve.wait_ge(norm["counted"], last)
    for b in range(first, last):
        dve.bn_aggr(keep["mv"][:, b, :], keep["bn"][:, b, :]).then_inc(norm["moments"], 1)
    dve.wait_ge(norm["moments"], last)
    dve.tensor_scalar(keep["ve"][:, first:last], keep["mv"][:, first:last, 1], LN_EPS, None, ALU.add).then_inc(norm["shifted"], last - first)


def norm_rstd(pool, keep, norm, first=0, last=B):
    pool.wait_ge(norm["shifted"], last)
    pool.tensor_tensor(keep["rstd"][:, first:last, 0], keep["ve"][:, first:last], keep["neghalf"][0:S, 0:last - first], ALU.pow)


def norm_early(norm_part, eng, keep, norm, cur):
    if cur and isinstance(cur[0], int) and cur[0] == B - 1:
        norm_part(eng, keep, norm, 0, NORM_EARLY)


def phase_a(nc, keep, io):
    FILL = ((0, ("k", 0), 0), (1, ("ctx", 0), 1), (2, ("v", 0), 2), (3, ("back", 0), 1), (4, ("k", 1), 0),
            (5, ("kt", 0), 2), (6, ("ctx", 1), 1), (7, ("v", 1), 2), (8, ("ctx", 2), 0), (8, ("kt", 1), 1),
            (9, ("q", 0), 2), (11, ("k", 2), 0), (12, ("v", 2), 1), (14, ("kt", 2), 2))
    ITEMS = [what for _, what, _ in FILL]
    BANK = {what: n for _, what, n in FILL}
    NEXT, BEFORE = ("ctx", "q"), ("back",)
    SQUARE_K = {1: 0, 5: 1, 12: 2}
    SUM_K = {2: 0, 6: 1, 12: 2}
    SCALE_K = {3: 0, 7: 1, 13: 2}
    WEIGH = {1: -1, 6: 0, 10: 1, 14: 2}
    COPY = {2: -1, 7: 0, 11: 1, 15: 2}
    SPLIT_V = 11
    MOMENTS, NORMALIZE = 6, 8
    FINISH = 4
    AHEAD = 2
    EXPS = 1
    PROBS = 4
    with Memory(nc, "a") as m:
        w_raw = m.sb("w_raw", [P, DC, 2 * D])
        w = [m.sb(f"w_{n}", [P, DC, 2 * D], F32R) for n in ("hi", "lo")]
        xin = m.sb("xin", [S, 2, D])
        xn = m.sb("xn", [S, D])
        x_bn = m.sb("x_bn", [S, 2, 6])
        x_mv = m.sb("x_mv", [S, 2, 2])
        x_ve = m.sb("x_ve", [S, 2])
        x_rstd = m.sb("x_rstd", [S, 2])
        ctx = m.sb("ctx", [KP, 2, KC, D])
        v = [m.sb(f"v_{n}", [KP, 2, KC, D], F32R) for n in ("hi", "lo")]
        kT = [m.sb(f"kT_{n}", [P, 2, DC, TE], F32R) for n in ("hi", "lo")]
        q = [m.sb(f"q_{n}", [P, 2, G, HPG, S], F32R) for n in ("hi", "lo")]
        probs = m.sb("probs", [S, PROBS, T])
        pT = [m.sb(f"pT_{n}", [KP, 2, KC, HPG, S], F32R) for n in ("hi", "lo")]
        oT = m.sb("oT", [P, G, S])
        xout = m.sb("xout", [S, 2, D])
        kraw = m.sb("kraw", [KP, 2, D])
        kn = m.sb("kn", [KP, 2, D])
        vout = m.sb("vout", [KP, KC, D])
        kout = m.sb("kout", [P, DC, TE])
        squares = m.sb("squares", [KP, D])
        ssq = m.sb("ssq", [KP, 2, G])
        ssq_eps = m.sb("ssq_eps", [KP, 2, G])
        rk = m.sb("rk", [KP, 2, G])
        nmax = m.sb("nmax", [S, 2, H])
        sums = m.sb("sums", [S, 2, H])
        rsum = m.sb("rsum", [S, H])
        tmp = m.sb("tmp", [S, D])

        score = [m.ps(f"score{n}", [P, 512]) for n in range(AHEAD)]
        turned = [m.ps(f"turned{n}", [P, 512]) for n in range(2)]
        outp = m.ps("outp", [P, 512])
        shared = [m.ps(f"shared{n}", [P, 512]) for n in range(3)]

        w_hi, w_split, cleared = m.sem("w_hi"), m.sem("w_split"), m.sem("cleared")
        w_loaded = [m.sem(f"w_loaded{n}") for n in range(2)]
        x_loaded = [m.sem(f"x_loaded{n}") for n in range(2)]
        ctx_loaded = [m.sem(f"ctx_loaded{n}") for n in range(2)]
        x_stored = [m.sem(f"x_stored{n}") for n in range(2)]
        k_stored, v_stored = m.sem("k_stored"), m.sem("v_stored")
        x_counted, x_moments, x_shifted, x_scaled, xn_done = (m.sem(n) for n in ("x_counted", "x_moments", "x_shifted", "x_scaled", "xn_done"))
        shared_ready = m.sem("shared_ready")
        kT_hi, v_hi, q_hi = m.sem("kT_hi"), m.sem("v_hi"), m.sem("q_hi")
        kT_split, v_split, q_split = m.sem("kT_split"), m.sem("v_split"), m.sem("q_split")
        scores_ready, masked, max_done = m.sem("scores_ready"), m.sem("masked"), m.sem("max_done")
        probs_ready, turned_ready = m.sem("probs_ready"), m.sem("turned_ready")
        pT_hi, pT_split = m.sem("pT_hi"), m.sem("pT_split")
        out_ready, out_copied, out_copied_too = m.sem("out_ready"), m.sem("out_copied"), m.sem("out_copied_too")
        squared, ssq_done, eps_done, rk_done, kn_done = m.sem("squared"), m.sem("ssq_done"), m.sem("eps_done"), m.sem("rk_done"), m.sem("kn_done")
        k_copied, k_out, v_out = m.sem("k_copied"), m.sem("k_out"), m.sem("v_out")
        rsum_done, tmp_done, x_done = m.sem("rsum_done"), m.sem("tmp_done"), m.sem("x_done")
        norm = norm_semaphores(m)
        block = m.block()

        def bank(what):
            return shared[BANK[what]]

        def missing(e, what):
            if not isinstance(e, int):
                return False
            return (e <= 0 and what[0] in BEFORE or e < 0 and what[0] not in NEXT
                    or e >= B - 1 and what[0] in NEXT or e >= B and what[0] not in BEFORE)

        def written(e, what):
            if isinstance(e, int) and e in (-1, 0, B - 1, B):
                ahead = [n for n in ITEMS if n[0] in NEXT]
                if e == -1:
                    return ahead.index(what) + 1
                order = [n for n in ITEMS if not missing(e, n)] if e < B else [("back", 0)]
                first = len(ahead) + (len(ITEMS) * e - len(BEFORE) if e else 0) - (len(ahead) if e == B else 0)
                return first + order.index(what) + 1
            return 4 - len(BEFORE) + len(ITEMS) * e + ITEMS.index(what) + 1

        def read(e, what):
            name, c = what
            if name == "k":
                return k_copied, KC * e + c + 1
            if name == "v":
                return v_out, KC * e + c + 1
            if name == "kt":
                return k_out, KC * e + c + 1
            if name == "ctx":
                return kT_split, KC * (e + 1) + c + 1
            if name == "q":
                return q_split, e + 2
            return tmp_done, e

        def earlier(e, what):
            own = [n for n in ITEMS if BANK[n] == BANK[what]]
            at = own.index(what)
            while True:
                at, e = (at - 1, e) if at else (len(own) - 1, e - 1)
                if isinstance(e, int) and e < -1:
                    return None
                if not missing(e, own[at]):
                    return e, own[at]

        @block.sync
        def _(sp):
            def load_ctx(b, p, half):
                sp.dma_start(ctx[:, p, :, :], io["ctx"][b, :, :].rearrange("(c p) d -> p c d", p=KP)).then_inc(ctx_loaded[p], 16)

            def load_x(b, p, half):
                sp.dma_start(xin[:, p, :], io["x"][b, :, :]).then_inc(x_loaded[p], 16)

            def head(cur):
                load_x(*cur)
                load_ctx(*cur)
                for n, name in enumerate(("Wk", "Wv")):
                    sp.dma_start(w_raw[:, :, n * D:(n + 1) * D], io[name].rearrange("(c p) n -> p c n", p=P)).then_inc(w_loaded[n], 16)

            def body(before, cur, after):
                if after:
                    if before:
                        sp.wait_ge(v_split, before[0] + 1)
                        sp.wait_ge(kT_split, KC * before[0] + KC)
                    load_ctx(*after)
                if before:
                    b, p, half = before
                    sp.wait_ge(x_done, b + 1)
                    sp.dma_start(io["x1"][b, :, :], xout[:, p, :]).then_inc(x_stored[p], 16)
                if after:
                    load_x(*after)
                if cur:
                    sp.wait_ge(v_out, KC * cur[0] + KC)
                    sp.dma_start(io["v1"][cur[0], :, :, :], vout[:, :, :]).then_inc(v_stored, 16)
                    sp.wait_ge(k_out, KC * cur[0] + KC)
                    sp.dma_start(io["k1"][cur[0], :, :, :], kout[:, :, :]).then_inc(k_stored, 16)

            batches(sp, head, body)
            for p in range(2):
                sp.wait_ge(x_stored[p], 16 * (B // 2) + 16)
            sp.wait_ge(k_stored, 16 * B + 16)
            sp.wait_ge(v_stored, 16 * B + 16)

        @block.gpsimd
        def _(pool):
            pool.memset(f32(q[0][:, :, :, :, :]), 0.0).then_inc(cleared, 1)
            for part in kT:
                pool.memset(f32(part[:, :, :, T:TE]), 0.0).then_inc(cleared, 1)
            pool.memset(kout[:, :, T:TE], 0.0).then_inc(cleared, 1)

            def deviations(b, p):
                pool.wait_ge(x_moments, b + 1)
                pool.tensor_tensor(x_ve[:, p:p + 1], x_mv[:, p, 1:2], keep["ln_eps"][0:S, :], ALU.add).then_inc(x_shifted, 1)
                pool.wait_ge(x_shifted, b + 1)
                pool.tensor_tensor(x_rstd[:, p:p + 1], x_ve[:, p:p + 1], keep["neghalf"][0:S, 0:1], ALU.pow).then_inc(x_scaled, 1)

            def values_lo(b, p):
                pool.wait_ge(v_hi, b + 1)
                pool.tensor_tensor(v[1][:, p, :, :], ctx[:, p, :, :], f32(v[0][:, p, :, :]), ALU.subtract).then_inc(v_split, 1)

            def head(cur):
                deviations(cur[0], cur[1])
                values_lo(cur[0], cur[1])

            def body(before, cur, after):
                for c in range(KC if cur else 0):
                    if c == KC - 1 and after:
                        deviations(after[0], after[1])
                    n = KC * cur[0] + c + 1
                    pool.wait_ge(ssq_done, n)
                    pool.tensor_tensor(ssq_eps[:, c % 2, :], ssq[:, c % 2, :], keep["rms_eps"][0:KP, :], ALU.add).then_inc(eps_done, 1)
                    pool.wait_ge(eps_done, n)
                    pool.tensor_tensor(rk[:, c % 2, :], ssq_eps[:, c % 2, :], keep["neghalf"][0:KP, 0:G], ALU.pow).then_inc(rk_done, 1)
                if after:
                    values_lo(after[0], after[1])
                norm_early(norm_rstd, pool, keep, norm, cur)

            batches(pool, head, body)
            norm_rstd(pool, keep, norm, NORM_EARLY, B)

        @block.scalar
        def _(act):
            for signal, credit in ((probs_ready, AHEAD), (out_copied, 1)):
                act.sem_inc(signal, credit)

            def weights_hi(n):
                act.wait_ge(w_loaded[n], 16)
                cols = slice(n * D, (n + 1) * D)
                act.activation(w[0][:, :, cols], w_raw[:, :, cols], ACT.Copy).then_inc(w_hi, 1)

            def ctx_hi(b, p, c):
                act.wait_ge(shared_ready, written(b - 1, ("ctx", c)))
                src = bank(("ctx", c))[:, 0:DC * KP].rearrange("p (c k) -> p c k", c=DC)
                act.activation(kT[0][:, p, :, c * KP:(c + 1) * KP], src, ACT.Copy).then_inc(kT_hi, 1)

            def values_hi(b, p):
                act.activation(v[0][:, p, :, :], ctx[:, p, :, :], ACT.Copy).then_inc(v_hi, 1)

            def query_hi(b, p):
                act.wait_ge(shared_ready, written(b - 1, ("q", 0)))
                for j in range(HPG):
                    r = slice(HD * j, HD * j + HD)
                    src = bank(("q", 0))[r, 0:DC * S].rearrange("p (g s) -> p g s", g=G)
                    act.activation(q[0][r, p, :, j, :], src, ACT.Copy, scale=float(HD) ** -0.5).then_inc(q_hi, 1)

            def head(cur):
                for c in range(KC):
                    ctx_hi(cur[0], cur[1], c)
                act.wait_ge(cleared, 5)
                query_hi(cur[0], cur[1])
                values_hi(cur[0], cur[1])

            def exps(b, p, h):
                act.wait_ge(max_done, H * b + h + 1)
                act.wait_ge(turned_ready, H * b + h + 1)
                act.activation(probs[:, h % PROBS, :], score[h % AHEAD][0:S, 0:T], ACT.Exp, bias=nmax[:, p, h:h + 1],
                               accum_out=sums[:, p, h:h + 1]).then_inc(probs_ready, 1)

            def keys_copy(b, c):
                act.wait_ge(shared_ready, written(b, ("k", c)))
                act.wait_ge(kn_done, KC * b + c + 1)
                act.activation(kraw[:, c % 2, :], bank(("k", c))[0:KP, :], ACT.Copy).then_inc(k_copied, 1)

            def square_keys(b, c):
                act.wait_ge(k_copied, KC * b + c + 1)
                act.activation(squares[:, :], kraw[:, c % 2, :], ACT.Square, scale=float(XHD) ** -0.5).then_inc(squared, 1)

            def values_out(b, c):
                act.wait_ge(shared_ready, written(b, ("v", c)))
                act.wait_ge(v_stored, 16 * b + 16)
                act.activation(vout[:, c, :], bank(("v", c))[0:KP, :], ACT.Copy).then_inc(v_out, 1)

            def keys_out(b, c):
                act.wait_ge(shared_ready, written(b, ("kt", c)))
                act.wait_ge(k_stored, 16 * b + 16)
                src = bank(("kt", c))[:, 0:DC * KP].rearrange("p (c k) -> p c k", c=DC)
                act.activation(kout[:, :, c * KP:(c + 1) * KP], src, ACT.Copy, scale=keep["qk_w"][:, 0:1]).then_inc(k_out, 1)

            def probs_hi(b, h):
                g, j = divmod(h, HPG)
                act.wait_ge(turned_ready, H * b + h + 1 + PROBS)
                src = turned[h % 2][0:KP, 0:KC * S].rearrange("p (c s) -> p c s", c=KC)
                act.activation(pT[0][:, g % 2, :, j, :], src, ACT.Copy).then_inc(pT_hi, 1)

            def copy_out(b, g):
                act.wait_ge(out_ready, G * b + g + 1)
                for j in range(HPG // 2):
                    r = slice(HD * j, HD * j + HD)
                    last = act.activation(oT[r, g, :], outp[r, j * S:(j + 1) * S], ACT.Copy)
                last.then_inc(out_copied, 1)

            def body(before, cur, after):
                if cur and not before:
                    weights_hi(0)
                    for h in range(EXPS):
                        exps(cur[0], cur[1], h)
                    weights_hi(1)
                for h in range(H):
                    if cur and h + EXPS < H:
                        exps(cur[0], cur[1], h + EXPS)
                    elif after and h + EXPS >= H:
                        exps(after[0], after[1], h + EXPS - H)
                    for _, (what, c), _ in (f for f in FILL if f[0] + 1 == h):
                        if what == "k" and cur:
                            keys_copy(cur[0], c)
                        elif what == "v" and cur:
                            values_out(cur[0], c)
                        elif what == "kt" and cur:
                            keys_out(cur[0], c)
                        elif what == "ctx" and after:
                            ctx_hi(after[0], after[1], c)
                        elif what == "q" and after:
                            query_hi(after[0], after[1])
                    if h == SPLIT_V and after:
                        values_hi(after[0], after[1])
                    if h in SQUARE_K and cur:
                        square_keys(cur[0], SQUARE_K[h])
                    if cur:
                        probs_hi(cur[0], h)
                    if h in COPY:
                        if COPY[h] < 0 and before:
                            copy_out(before[0], G - 1)
                        elif COPY[h] >= 0 and cur:
                            copy_out(cur[0], COPY[h])

            batches(act, head, body)

        @block.vector
        def _(dve):
            dve.sem_inc(out_copied_too, 1)
            dve.sem_inc(pT_split, 2)
            dve.sem_inc(kn_done, 2)
            dve.sem_inc(v_stored, 16)
            dve.sem_inc(k_stored, 16)
            for n in range(2):
                dve.sem_inc(x_stored[n], 16)
            dve.memset(f32(q[1][:, :, :, :, :]), 0.0).then_inc(cleared, 1)

            def weights_lo(n):
                dve.wait_ge(w_hi, n + 1)
                cols = slice(n * D, (n + 1) * D)
                dve.tensor_tensor(w[1][:, :, cols], w_raw[:, :, cols], f32(w[0][:, :, cols]), ALU.subtract).then_inc(w_split, 1)

            def moments(b, p, half):
                dve.wait_ge(x_loaded[p], 16 * half + 16)
                dve.bn_stats(x_bn[:, p, :], xin[:, p, :]).then_inc(x_counted, 1)
                batch = b + 1
                batch = batch if isinstance(batch, int) else dve.to_reg(batch)
                dve.wait_ge(cleared, 5)
                dve.wait_ge(x_counted, batch)
                dve.bn_aggr(x_mv[:, p, :], x_bn[:, p, :]).then_inc(x_moments, 1)

            def normalize(b, p):
                dve.wait_ge(x_scaled, b + 1)
                dve.tensor_scalar(xn[:, :], xin[:, p, :], x_mv[:, p, 0:1], x_rstd[:, p:p + 1], ALU.subtract, ALU.mult).then_inc(xn_done, 1)

            def ctx_lo(b, p, c):
                dve.wait_ge(kT_hi, KC * b + c + 1)
                src = bank(("ctx", c))[:, 0:DC * KP].rearrange("p (c k) -> p c k", c=DC)
                cols = slice(c * KP, (c + 1) * KP)
                dve.tensor_tensor(kT[1][:, p, :, cols], src, f32(kT[0][:, p, :, cols]), ALU.subtract).then_inc(kT_split, 1)

            def query_lo(b, p):
                dve.wait_ge(q_hi, HPG * b + HPG)
                for j in range(HPG):
                    r = slice(HD * j, HD * j + HD)
                    src = bank(("q", 0))[r, 0:DC * S].rearrange("p (g s) -> p g s", g=G)
                    last = dve.scalar_tensor_tensor(out=q[1][r, p, :, j, :], in0=src, scalar=float(HD) ** -0.5,
                                                    in1=f32(q[0][r, p, :, j, :]), op0=ALU.mult, op1=ALU.subtract)
                last.then_inc(q_split, 1)

            def head(cur):
                moments(*cur)
                normalize(cur[0], cur[1])
                for c in range(KC):
                    ctx_lo(cur[0], cur[1], c)
                query_lo(cur[0], cur[1])

            def maximum(b, p, h):
                head = H * b + h + 1
                head = head if isinstance(head, int) else dve.to_reg(head)
                dve.wait_ge(cleared, 5)
                dve.wait_ge(scores_ready, head)
                dve.copy_predicated(score[h % AHEAD][0:S, T - S:T], keep["later"][:, :], keep["masked_score"][:, :]).then_inc(masked, 1)
                dve.wait_ge(masked, H * b + h + 1)
                dve.tensor_reduce(nmax[:, p, h:h + 1], score[h % AHEAD][0:S, 0:T], axis=AX.X, op=ALU.max, negate=True).then_inc(max_done, 1)

            def sum_keys(b, c):
                dve.wait_ge(squared, KC * b + c + 1)
                dve.tensor_reduce(ssq[:, c % 2, :], squares[:, :].rearrange("p (g d) -> p g d", g=G), axis=AX.X, op=ALU.add).then_inc(ssq_done, 1)

            def scale_keys(b, c):
                dve.wait_ge(rk_done, KC * b + c + 1)
                src = kraw[:, c % 2, :].rearrange("p (g d) -> p g d", g=G)
                dve.tensor_tensor(kn[:, c % 2, :].rearrange("p (g d) -> p g d", g=G), src,
                                  rk[:, c % 2, :].unsqueeze(2).broadcast_to([KP, G, P]), ALU.mult).then_inc(kn_done, 1)

            def probs_lo(b, h):
                g, j = divmod(h, HPG)
                dve.wait_ge(pT_hi, H * b + h + 1)
                src = turned[h % 2][0:KP, 0:KC * S].rearrange("p (c s) -> p c s", c=KC)
                dve.tensor_tensor(pT[1][:, g % 2, :, j, :], src, f32(pT[0][:, g % 2, :, j, :]), ALU.subtract).then_inc(pT_split, 1)

            def copy_out(b, g):
                dve.wait_ge(out_ready, G * b + g + 1)
                for j in range(HPG // 2, HPG):
                    r = slice(HD * j, HD * j + HD)
                    last = dve.tensor_copy(oT[r, g, :], outp[r, j * S:(j + 1) * S])
                last.then_inc(out_copied_too, 1)

            def finish(b, p, half):
                dve.wait_ge(probs_ready, H * b + H + AHEAD)
                dve.reciprocal(rsum[:, :], sums[:, p, :]).then_inc(rsum_done, 1)
                dve.wait_ge(shared_ready, written(b + 1, ("back", 0)))
                dve.wait_ge(rsum_done, b + 1)
                dve.tensor_tensor(tmp[:, :].rearrange("p (h d) -> p h d", h=H), bank(("back", 0))[0:S, :].rearrange("p (h d) -> p h d", h=H),
                                  rsum[:, :].unsqueeze(2).broadcast_to([S, H, HD]), ALU.mult).then_inc(tmp_done, 1)
                dve.wait_ge(tmp_done, b + 1)
                dve.wait_ge(x_stored[p], 16 * half + 16)
                dve.scalar_tensor_tensor(out=xout[:, p, :], in0=tmp[:, :], scalar=keep["gates"][0:S, 0:1], in1=xin[:, p, :],
                                         op0=ALU.mult, op1=ALU.add).then_inc(x_done, 1)
                dve.wait_ge(x_done, b + 1)
                dve.bn_stats(keep["bn"][:, b, :], xout[:, p, :]).then_inc(norm["counted"], 1)

            def body(before, cur, after):
                norm_early(norm_moments, dve, keep, norm, cur)
                if cur and not before:
                    weights_lo(0)
                    for h in range(AHEAD):
                        maximum(cur[0], cur[1], h)
                    weights_lo(1)
                for h in range(H):
                    if cur and h + AHEAD < H:
                        maximum(cur[0], cur[1], h + AHEAD)
                    elif after and h + AHEAD >= H:
                        maximum(after[0], after[1], h + AHEAD - H)
                    for _, (what, c), _ in (f for f in FILL if f[0] + 1 == h and after):
                        if what == "ctx":
                            ctx_lo(after[0], after[1], c)
                        elif what == "q":
                            query_lo(after[0], after[1])
                    if h in SUM_K and cur:
                        sum_keys(cur[0], SUM_K[h])
                    if h in SCALE_K and cur:
                        scale_keys(cur[0], SCALE_K[h])
                    if h in COPY:
                        if COPY[h] < 0 and before:
                            copy_out(before[0], G - 1)
                        elif COPY[h] >= 0 and cur:
                            copy_out(cur[0], COPY[h])
                    if h == NORMALIZE and after:
                        normalize(after[0], after[1])
                    if h == MOMENTS and after:
                        moments(*after)
                    if cur:
                        probs_lo(cur[0], h)
                    if h == FINISH and before:
                        finish(*before)

            batches(dve, head, body)
            norm_moments(dve, keep, norm, NORM_EARLY, B)

        @block.tensor
        def _(pe):
            pe.sem_inc(turned_ready, PROBS)
            ident = keep["ident"]

            def bank_free(e, what):
                before = earlier(e, what)
                if before:
                    pe.wait_ge(*read(*before))

            def turn_ctx(b, p, half, c):
                if c == 0:
                    pe.wait_ge(ctx_loaded[p], 16 * half + 16)
                bank_free(b - 1, ("ctx", c))
                for n in range(DC):
                    last = pe.transpose(bank(("ctx", c))[:, n * KP:(n + 1) * KP], ctx[:, p, c, n * P:(n + 1) * P], ident[0:KP, 0:KP])
                last.then_inc(shared_ready, 1)

            def turn_queries(b):
                pe.wait_ge(xn_done, b + 1)
                bank_free(b - 1, ("q", 0))
                for n in range(DC):
                    last = pe.transpose(bank(("q", 0))[:, n * S:(n + 1) * S], xn[:, n * P:(n + 1) * P], ident[0:S, 0:S])
                last.then_inc(shared_ready, 1)

            def head(cur):
                for c in range(KC):
                    turn_ctx(*cur, c)
                turn_queries(cur[0])

            def scores(b, p, h):
                g, j = divmod(h, HPG)
                if h == 0:
                    pe.wait_ge(q_split, b + 1)
                    pe.wait_ge(kT_split, KC * b + KC)
                pe.wait_ge(probs_ready, H * b + h + 1)
                for n, (s, r) in enumerate(PASSES):
                    last = pe.matmul(score[h % AHEAD][0:S, 0:TE], q[s][:, p, g, j, :], kT[r][:, p, g, :],
                                     start=n == 0, stop=n == len(PASSES) - 1)
                last.then_inc(scores_ready, 1)

            def project(b, p, what):
                name, c = what
                bank_free(b, what)
                if isinstance(b, int) and b == 0 and c == 0:
                    pe.wait_ge(w_split, 1 if name == "k" else 2)
                cols = slice(0, D) if name == "k" else slice(D, 2 * D)
                for n, (s, r) in enumerate(PASSES):
                    for k in range(DC):
                        last = pe.matmul(bank(what)[0:KP, :], kT[s][:, p, k, c * KP:(c + 1) * KP], w[r][:, k, cols],
                                         start=n == 0 and k == 0, stop=n == len(PASSES) - 1 and k == DC - 1)
                last.then_inc(shared_ready, 1)

            def turn_keys(b, c):
                pe.wait_ge(kn_done, KC * b + c + 1 + 2)
                bank_free(b, ("kt", c))
                for n in range(DC):
                    last = pe.transpose(bank(("kt", c))[:, n * KP:(n + 1) * KP], kn[:, c % 2, n * P:(n + 1) * P], ident[0:KP, 0:KP])
                last.then_inc(shared_ready, 1)

            def turn_probs(b, h):
                pe.wait_ge(probs_ready, H * b + h + 1 + AHEAD)
                pe.wait_ge(pT_split, H * b + h + 1)
                for c in range(KC):
                    last = pe.transpose(turned[h % 2][0:KP, c * S:(c + 1) * S], probs[:, h % PROBS, c * KP:(c + 1) * KP], ident[0:S, 0:S])
                last.then_inc(turned_ready, 1)

            def weigh(b, p, g):
                pe.wait_ge(pT_split, H * b + HPG * (g + 1) + 2)
                pe.wait_ge(out_copied, G * b + g + 1)
                pe.wait_ge(out_copied_too, G * b + g + 1)
                if g == 0:
                    pe.wait_ge(v_split, b + 1)
                for n, (s, r) in enumerate(PASSES):
                    for c in range(KC):
                        last = pe.matmul(outp[:, 0:HPG * S], v[s][:, p, c, g * P:(g + 1) * P],
                                         pT[r][:, g % 2, c, :, :].rearrange("p j s -> p (j s)"),
                                         start=n == 0 and c == 0, stop=n == len(PASSES) - 1 and c == KC - 1)
                last.then_inc(out_ready, 1)

            def turn_back(b):
                pe.wait_ge(out_copied, G * b + G + 1)
                pe.wait_ge(out_copied_too, G * b + G + 1)
                bank_free(b + 1, ("back", 0))
                for g in range(G):
                    last = pe.transpose(bank(("back", 0))[0:S, g * P:(g + 1) * P], oT[:, g, :], ident[:, :])
                last.then_inc(shared_ready, 1)

            def body(before, cur, after):
                if cur and not before:
                    for h in range(AHEAD):
                        scores(cur[0], cur[1], h)
                for h in range(H):
                    if cur and h + AHEAD < H:
                        scores(cur[0], cur[1], h + AHEAD)
                    elif after and h + AHEAD >= H:
                        scores(after[0], after[1], h + AHEAD - H)
                    if cur:
                        turn_probs(cur[0], h)
                    if h in WEIGH:
                        if WEIGH[h] < 0 and before:
                            weigh(before[0], before[1], G - 1)
                        elif WEIGH[h] >= 0 and cur:
                            weigh(cur[0], cur[1], WEIGH[h])
                    for _, (what, c), _ in (f for f in FILL if f[0] == h):
                        if what in ("k", "v") and cur:
                            project(cur[0], cur[1], (what, c))
                        elif what == "kt" and cur:
                            turn_keys(cur[0], c)
                        elif what == "ctx" and after:
                            turn_ctx(*after, c)
                        elif what == "q" and after:
                            turn_queries(after[0])
                        elif what == "back" and before:
                            turn_back(before[0])

            batches(pe, head, body)


IC = INTER // P
NG = 4
BPG = B // NG
GS = BPG * S


def phase_b_prepare(nc, keep, io, big):
    wug, wdn, xT = big["wug"], big["wdn"], big["xT"]
    BLOCKS = IC // NG
    STAGES = 4
    CREDIT = 2 * STAGES - 1
    X_AHEAD = 2
    Z_CREDIT = 4 * BPG
    with Memory(nc, "p") as m:
        ug_raw = m.sb("ug_raw", [P, 4, D])
        down_raw = m.sb("down_raw", [P, INTER])
        down = [m.sb(f"down{n}", [P, INTER]) for n in range(2)]
        signs = m.sb("signs", [S, D])
        xin = m.sb("xin", [S, BPG, D])
        z = [m.sb(f"z{n}", [S, D]) for n in range(2)]
        zT = m.sb("zT", [P, DC, GS])
        z_bank = [m.ps(f"z_bank{n}", [P, 512]) for n in range(2)]
        h_bank = [m.ps(f"h_bank{n}", [P, 512]) for n in range(2)]
        u_bank = [m.ps(f"u_bank{n}", [P, 512]) for n in range(2)]
        d_bank = [m.ps(f"d_bank{n}", [P, 512]) for n in range(2)]
        signs_loaded, scales_loaded, d_loaded = m.sem("signs_loaded"), m.sem("scales_loaded"), m.sem("d_loaded")
        u_loaded = [m.sem(f"u_loaded{n}") for n in range(4)]
        x_loaded = [m.sem(f"x_loaded{n}") for n in range(BPG)]
        xn_done, signed, z_sums, z_done, z_turned, z_copied = (m.sem(n) for n in ("xn_done", "signed", "z_sums", "z_done", "z_turned", "z_copied"))
        rotated, x_hi, x_split = m.sem("rotated"), m.sem("x_hi"), m.sem("x_split")
        u_turned, u_copied = m.sem("u_turned"), m.sem("u_copied")
        d_sums, d_turned, d_copied, d_rotated, d_signed = (m.sem(n) for n in ("d_sums", "d_turned", "d_copied", "d_rotated", "d_signed"))
        block = m.block()

        def pairs(buffer, h):
            halves = buffer.rearrange("p (a two n) -> p a two n", two=2, n=h)
            return halves[:, :, 0, :], halves[:, :, 1, :]

        @block.sync
        def _(sp):
            def load_x(i, k):
                j = BPG * i + k
                sp.wait_ge(z_sums, 4 * j + 2)
                sp.dma_start(xin[:, k, :], io["x1"][j, :, :]).then_inc(x_loaded[k], 16)

            def step(i, last=False):
                sp.wait_ge(d_sums, 2 * STAGES * i + 1)
                sp.dma_start(down_raw[:, :], io["W_down"].rearrange("(q p) n -> q p n", p=P)[i, :, :]).then_inc(d_loaded, 16)
                for k in range(BPG):
                    if k + X_AHEAD < BPG:
                        load_x(i, k + X_AHEAD)
                    elif not last:
                        load_x(i + 1, k + X_AHEAD - BPG)
                    for n, name in enumerate(("W_up", "W_gate")):
                        u = 2 * k + n
                        sp.wait_ge(u_turned, 2 * BLOCKS * i + u + 1)
                        sp.dma_start(ug_raw[:, u % 4, :], io[name].rearrange("(c p) n -> c p n", p=P)[BPG * i + k, :, :]).then_inc(u_loaded[u % 4], 16)

            for k in range(X_AHEAD):
                load_x(0, k)
            sp.dma_start(signs[:, :], io["SU_ug"].rearrange("(a n) -> a n", a=1).broadcast_to([S, D])).then_inc(signs_loaded, 16)
            step(0)
            with nc.allow_non_contiguous_dma(reason="scales by partition"):
                sp.dma_start(big["down_signs"][:, :], io["SU_dp"].rearrange("(c p) -> p c", p=P)).then_inc(scales_loaded, 16)
                sp.dma_start(big["ug_scale"][:, :], io["Wscale_ug"].rearrange("(c p) -> p c", p=P)).then_inc(scales_loaded, 16)
            with sp.Fori(1, NG - 1) as i:
                step(i)
            step(NG - 1, last=True)

        @block.gpsimd
        def _(pool):
            pool.wait_ge(signs_loaded, 16)
            with pool.Fori(0, NG) as i:
                for k in range(BPG):
                    j = BPG * i + k
                    pool.wait_ge(xn_done, j + 1)
                    pool.tensor_tensor(xin[:, k, :], xin[:, k, :], signs[:, :], ALU.mult).then_inc(signed, 1)
                    (a, b), (s, d) = pairs(xin[:, k, :], P), pairs(z[0][:, :], P)
                    pool.wait_ge(signed, j + 1)
                    pool.wait_ge(z_sums, 4 * j + Z_CREDIT)
                    pool.tensor_tensor(s, a, b, ALU.add).then_inc(z_sums, 1)
                    pool.tensor_tensor(d, a, b, ALU.subtract).then_inc(z_sums, 1)

        @block.scalar
        def _(act):
            for signal, credit in ((z_copied, 2), (u_copied, 2), (d_copied, 2), (d_signed, 2)):
                act.sem_inc(signal, credit)
            with act.Fori(0, NG) as i:
                for k in range(BPG):
                    j = BPG * i + k
                    for n in range(2):
                        u = 2 * k + n
                        act.wait_ge(u_turned, 2 * BLOCKS * i + u + 1 + 4)
                        act.activation(wug[:, :, n, bass.ds(j * P, P)], u_bank[n][:, :].rearrange("p (c n) -> p c n", c=DC),
                                       ACT.Copy).then_inc(u_copied, 1)
                    act.wait_ge(z_turned, j + 1 + 1)
                    if k == 0:
                        act.wait_ge(rotated, DC * i + 1)
                    act.activation(zT[:, :, k * S:(k + 1) * S], z_bank[k % 2][:, 0:DC * S].rearrange("p (c s) -> p c s", c=DC),
                                   ACT.Copy).then_inc(z_copied, 1)
                for c in range(DC):
                    act.wait_ge(d_turned, DC * i + c + 1 + 4)
                    act.activation(wdn[:, 4 * c:4 * c + 4, bass.ds(i * P, P)], d_bank[c % 2][:, :].rearrange("p (c n) -> p c n", c=4),
                                   ACT.Copy).then_inc(d_copied, 1)
                    act.wait_ge(rotated, DC * i + c + 1 + 1)
                    act.activation(xT[0][:, c, bass.ds(i * GS, GS)], h_bank[c % 2][:, 0:GS], ACT.Copy, scale=float(D) ** -0.5).then_inc(x_hi, 1)
            act.wait_ge(scales_loaded, 32)
            with act.Fori(0, IC // 2) as i:
                for n in range(2):
                    act.wait_ge(d_rotated, 2 * i + n + 1)
                    act.activation(wdn[:, 2 * i + n, :], d_bank[n][:, :], ACT.Copy,
                                   scale=big["down_signs"][:, bass.ds(2 * i + n, 1)]).then_inc(d_signed, 1)

        @block.vector
        def _(dve):
            for signal, credit in ((z_sums, Z_CREDIT), (x_split, 2), (d_sums, CREDIT)):
                dve.sem_inc(signal, credit)

            def normalize(i, k):
                j = BPG * i + k
                dve.wait_ge(x_loaded[k], 16 * i + 16)
                dve.tensor_scalar(xin[:, k, :], xin[:, k, :], keep["mv"][:, j, 0:1], keep["rstd"][:, j, :],
                                  ALU.subtract, ALU.mult).then_inc(xn_done, 1)

            def rotate_batch(i, k):
                j = BPG * i + k
                (a, b), (s, d) = pairs(z[0][:, :], 2 * P), pairs(z[1][:, :], 2 * P)
                dve.wait_ge(z_sums, 4 * j + 2 + Z_CREDIT)
                dve.wait_ge(z_turned, j + 1)
                dve.tensor_tensor(s, a, b, ALU.add).then_inc(z_sums, 1)
                dve.tensor_tensor(d, a, b, ALU.subtract).then_inc(z_sums, 1)

            def rotate_down(i, stage):
                src, dst = down[1 - stage % 2] if stage else down_raw, down[stage % 2]
                dve.wait_ge(d_sums, 2 * STAGES * i + 2 * stage + CREDIT)
                if stage == 0:
                    dve.wait_ge(d_loaded, 16 * i + 16)
                if stage == 1:
                    dve.wait_ge(d_turned, 4 * i + 4)
                (a, b), (s, d) = pairs(src[:, :], P << stage), pairs(dst[:, :], P << stage)
                dve.tensor_tensor(s, a, b, ALU.add).then_inc(d_sums, 1)
                dve.tensor_tensor(d, a, b, ALU.subtract).then_inc(d_sums, 1)

            def x_lo(i, chunks):
                for c in chunks:
                    dve.wait_ge(x_hi, DC * i + c + 1)
                    cols = bass.ds(i * GS, GS)
                    dve.scalar_tensor_tensor(out=xT[1][:, c, cols], in0=h_bank[c % 2][:, 0:GS], scalar=float(D) ** -0.5,
                                             in1=f32(xT[0][:, c, cols]), op0=ALU.mult, op1=ALU.subtract).then_inc(x_split, 1)

            def step(i, before, last=False):
                for k in range(BPG):
                    if k + 1 < BPG:
                        normalize(i, k + 1)
                    elif not last:
                        normalize(i + 1, 0)
                    rotate_down(i, k)
                    rotate_batch(i, k)
                    if k < 2 and before is not None:
                        x_lo(before, (2 * k, 2 * k + 1))

            normalize(0, 0)
            step(0, None)
            with dve.Fori(1, NG - 1) as i:
                step(i, i - 1)
            step(NG - 1, NG - 2, last=True)
            x_lo(NG - 1, range(DC))

        @block.tensor
        def _(pe):
            for signal, credit in ((z_turned, 1), (rotated, 1), (u_turned, 4), (d_turned, 4)):
                pe.sem_inc(signal, credit)
            ident, had = keep["ident"], keep["hadamard"]
            with pe.Fori(0, NG) as i:
                for k in range(BPG):
                    j = BPG * i + k
                    for n in range(2):
                        u = 2 * k + n
                        pe.wait_ge(u_loaded[u % 4], 32 * i + 16 * (u // 4) + 16)
                        pe.wait_ge(u_copied, 2 * BLOCKS * i + u + 1)
                        for c in range(DC):
                            last = pe.transpose(u_bank[n][:, c * P:(c + 1) * P], ug_raw[:, u % 4, c * P:(c + 1) * P], ident[:, :])
                        last.then_inc(u_turned, 1)
                    pe.wait_ge(z_sums, 4 * j + 4 + Z_CREDIT)
                    pe.wait_ge(z_copied, j + 1)
                    for c in range(DC):
                        last = pe.transpose(z_bank[k % 2][:, c * S:(c + 1) * S], z[1][:, c * P:(c + 1) * P], ident[0:S, 0:S])
                    last.then_inc(z_turned, 1)
                for c in range(NG):
                    pe.wait_ge(d_sums, 2 * STAGES * i + 2 * STAGES + CREDIT)
                    pe.wait_ge(d_copied, NG * i + c + 1)
                    for n in range(4):
                        r = slice((4 * c + n) * P, (4 * c + n + 1) * P)
                        last = pe.transpose(d_bank[c % 2][:, n * P:(n + 1) * P], down[1][:, r], ident[:, :])
                    last.then_inc(d_turned, 1)
                    if c == 0:
                        pe.wait_ge(z_copied, BPG * i + BPG + 2)
                    pe.wait_ge(x_split, DC * i + c + 1)
                    pe.matmul(h_bank[c % 2][:, 0:GS], had[:, :], zT[:, c, :], start=True, stop=True).then_inc(rotated, 1)
            pe.wait_ge(d_copied, NG * NG + 2)
            with pe.Fori(0, IC // 2) as i:
                for n in range(2):
                    pe.wait_ge(d_signed, 2 * i + n + 1)
                    pe.matmul(d_bank[n][:, :], had[:, :], wdn[:, 2 * i + n, :], start=True, stop=True).then_inc(d_rotated, 1)


def phase_b(nc, keep, io):
    with Memory(nc, "f") as outer:
        big = {
            "wug": outer.sb("wug", [P, DC, 2, INTER]),
            "wdn": outer.sb("wdn", [P, IC, D]),
            "xT": [outer.sb(f"xT_{n}", [P, DC, B * S], F32R) for n in ("hi", "lo")],
            "down_signs": outer.sb("down_signs", [P, IC]),
            "ug_scale": outer.sb("ug_scale", [P, 2 * IC]),
        }
        phase_b_prepare(nc, keep, io, big)
        phase_b_run(nc, keep, io, big)


def phase_b_run(nc, keep, io, big):
    wug, wdn, xT, ug_scale = big["wug"], big["wdn"], big["xT"], big["ug_scale"]
    with Memory(nc, "b") as m:
        wu = [m.sb(f"wu_{n}", [P, 2, DC, 2, P], F32R) for n in ("hi", "lo")]
        wd = [m.sb(f"wd_{n}", [P, 2, D], F32R) for n in ("hi", "lo")]
        silu = m.sb("silu", [P, 2, GS])
        hidden = m.sb("hidden", [P, 2, GS])
        hT = [m.sb(f"hT_{n}", [P, 2, GS], F32R) for n in ("hi", "lo")]
        xio = m.sb("xio", [S, BPG, D])
        down_scale = m.sb("down_scale", [S, D])
        up = [m.ps(f"up{n}", [P, 512]) for n in range(2)]
        gate = [m.ps(f"gate{n}", [P, 512]) for n in range(2)]
        y = [m.ps(f"y{n}", [P, 512]) for n in range(BPG)]
        x_loaded, x_stored, x_done, y_ready = m.sem("x_loaded"), m.sem("x_stored"), m.sem("x_done"), m.sem("y_ready")
        y_scaled, scale_loaded, scale_done = m.sem("y_scaled"), m.sem("scale_loaded"), m.sem("scale_done")
        wu_hi, wu_split, wd_hi, wd_split = m.sem("wu_hi"), m.sem("wu_split"), m.sem("wd_hi"), m.sem("wd_split")
        gu_ready, silu_done, h_done, h_hi, h_split = (m.sem(n) for n in ("gu_ready", "silu_done", "h_done", "h_hi", "h_split"))
        block = m.block()

        @block.sync
        def _(sp):
            sp.dma_start(down_scale[:, :], io["Wscale_dp"].rearrange("(a n) -> a n", a=1).broadcast_to([S, D])).then_inc(scale_loaded, 16)

            def load(g):
                sp.dma_start(xio[:, :, :], io["x1"][bass.ds(BPG * g, BPG), :, :].rearrange("b s d -> s b d")).then_inc(x_loaded, 16)

            def store(g):
                for k in range(BPG):
                    sp.wait_ge(x_done, BPG * g + k + 1 + 1)
                    sp.dma_start(io["x2"][BPG * g + k, :, :], xio[:, k, :]).then_inc(x_stored, 16)

            load(0)
            with sp.Fori(0, NG - 1) as g:
                store(g)
                sp.wait_ge(x_stored, 16 * BPG * g + 16 * BPG)
                load(g + 1)
            store(NG - 1)
            sp.wait_ge(x_stored, 16 * B)

        @block.scalar
        def _(act):
            for p in range(2):
                act.activation(wu[0][:, p, :, :, :], wug[:, :, :, p * P:(p + 1) * P], ACT.Copy).then_inc(wu_hi, 1)
            with act.Fori(0, NG) as g:
                with act.Fori(0, IC // 2) as i:
                    for p in range(2):
                        c, t = 2 * i + p, IC * g + 2 * i + p
                        act.wait_ge(gu_ready, t + 1 + 1)
                        act.activation(silu[:, p, :], gate[p][:, 0:GS], ACT.Silu, scale=ug_scale[:, bass.ds(IC + c, 1)]).then_inc(silu_done, 1)
                        act.activation(wd[0][:, p, :], wdn[:, c, :], ACT.Copy).then_inc(wd_hi, 1)
                        act.wait_ge(h_done, t + 1 + 2)
                        act.activation(hT[0][:, p, :], hidden[:, p, :], ACT.Copy).then_inc(h_hi, 1)
                        act.activation(wu[0][:, p, :, :, :], wug[:, :, :, bass.ds(((c + 2) % IC) * P, P)], ACT.Copy).then_inc(wu_hi, 1)

        @block.vector
        def _(dve):
            dve.sem_inc(h_done, 2)
            dve.sem_inc(x_done, 1)
            for p in range(2):
                dve.wait_ge(wu_hi, p + 1)
                dve.tensor_tensor(wu[1][:, p, :, :, :], wug[:, :, :, p * P:(p + 1) * P], f32(wu[0][:, p, :, :, :]),
                                  ALU.subtract).then_inc(wu_split, 1)
            dve.wait_ge(scale_loaded, 16)
            dve.tensor_scalar(down_scale[:, :], down_scale[:, :], float(INTER) ** -0.5, keep["gates"][0:S, 2:3],
                              ALU.mult, ALU.mult).then_inc(scale_done, 1)

            def group(g):
                with dve.Fori(0, IC // 2) as i:
                    for p in range(2):
                        c, t = 2 * i + p, IC * g + 2 * i + p
                        dve.wait_ge(silu_done, t + 1)
                        dve.scalar_tensor_tensor(out=hidden[:, p, :], in0=up[p][:, 0:GS], scalar=ug_scale[:, bass.ds(c, 1)], in1=silu[:, p, :],
                                                 op0=ALU.mult, op1=ALU.mult).then_inc(h_done, 1)
                        dve.wait_ge(wd_hi, t + 1)
                        dve.tensor_tensor(wd[1][:, p, :], wdn[:, c, :], f32(wd[0][:, p, :]), ALU.subtract).then_inc(wd_split, 1)
                        dve.wait_ge(h_hi, t + 1)
                        dve.tensor_tensor(hT[1][:, p, :], hidden[:, p, :], f32(hT[0][:, p, :]), ALU.subtract).then_inc(h_split, 1)
                        dve.wait_ge(wu_hi, t + 3)
                        dve.tensor_tensor(wu[1][:, p, :, :, :], wug[:, :, :, bass.ds(((c + 2) % IC) * P, P)],
                                          f32(wu[0][:, p, :, :, :]), ALU.subtract).then_inc(wu_split, 1)
                dve.wait_ge(x_loaded, 16 * g + 16)
                dve.wait_ge(scale_done, 1)
                for k in range(BPG):
                    dve.wait_ge(y_ready, BPG * g + k + 1)
                    dve.tensor_tensor(y[k][0:S, :], y[k][0:S, :], down_scale[:, :], ALU.mult).then_inc(y_scaled, 1)
                for k in range(BPG):
                    dve.wait_ge(y_scaled, BPG * g + k + 1)
                    dve.tensor_tensor(xio[:, k, :], y[k][0:S, :], xio[:, k, :], ALU.add).then_inc(x_done, 1)

            with dve.Fori(0, NG) as g:
                group(g)

        @block.tensor
        def _(pe):
            pe.sem_inc(gu_ready, 1)

            def project(g, c, t, p):
                pe.wait_ge(wu_split, t + 1)
                pe.wait_ge(h_done, t + 1)
                for n, out in ((1, gate[p]), (0, up[p])):
                    for k, (s, r) in enumerate(PASSES):
                        for d in range(DC):
                            last = pe.matmul(out[:, 0:GS], wu[s][:, p, d, n, :], xT[r][:, d, bass.ds(g * GS, GS)],
                                             start=k == 0 and d == 0, stop=k == len(PASSES) - 1 and d == DC - 1)
                last.then_inc(gu_ready, 1)

            def reduce(t, p, first, final):
                pe.wait_ge(h_split, t + 1)
                pe.wait_ge(wd_split, t + 1)
                for b in range(BPG):
                    for k, (s, r) in enumerate(PASSES):
                        last = pe.matmul(y[b][0:S, :], hT[s][:, p, b * S:(b + 1) * S], wd[r][:, p, :],
                                         start=first and k == 0, stop=final and k == len(PASSES) - 1)
                    if final:
                        last.then_inc(y_ready, 1)

            with pe.Fori(0, NG) as g:
                project(g, 0, IC * g, 0)
                project(g, 1, IC * g + 1, 1)
                pe.wait_ge(x_done, BPG * g + 1)
                reduce(IC * g, 0, True, False)
                with pe.Fori(1, IC // 2) as i:
                    for p in range(2):
                        t = IC * g + 2 * i + p
                        project(g, 2 * i + p, t, p)
                        reduce(t - 1, 1 - p, False, False)
                reduce(IC * g + IC - 1, 1, False, True)


def phase_c(nc, keep, io):
    with Memory(nc, "o") as outer:
        wo = [outer.sb(f"wo_{n}", [P, H, D], F32R) for n in ("hi", "lo")]
        phase_c_queries(nc, keep, io, wo)
        phase_c_attention(nc, keep, io, wo)


def phase_c_queries(nc, keep, io, wo):
    TILES = B * S // P
    LAG = 2
    QW = G * D
    SPLIT_WO = 2
    TURN_X = 1
    with Memory(nc, "q") as m:
        w_raw = m.sb("w_raw", [P, DC, QW])
        w = [m.sb(f"w_{n}", [P, DC, QW], F32R) for n in ("hi", "lo")]
        xin = m.sb("xin", [P, 2, D])
        x_bn, x_mv = m.sb("x_bn", [P, 2, 6]), m.sb("x_mv", [P, 2, 2])
        x_ve, x_rstd = m.sb("x_ve", [P, 2]), m.sb("x_rstd", [P, 2])
        xn = m.sb("xn", [P, D])
        xT = [m.sb(f"xT_{n}", [P, 2, DC, P], F32R) for n in ("hi", "lo")]
        squares = m.sb("squares", [P, D])
        ssq = m.sb("ssq", [P, 2, G])
        ssq_eps = m.sb("ssq_eps", [P, 2, G])
        rq = m.sb("rq", [P, 2, G])
        qn = m.sb("qn", [P, 2, D])
        qT = m.sb("qT", [P, 2, H, P])
        x_bank = m.ps("x_bank", [P, 512])
        q_bank = [m.ps(f"q_bank{n}", [P, 512]) for n in range(G)]
        t_bank = [m.ps(f"t_bank{n}", [P, 512]) for n in range(2)]
        w_loaded = [m.sem(f"w_loaded{n}") for n in range(G)]
        w_hi, w_split, wo_hi, wo_split = (m.sem(n) for n in ("w_hi", "w_split", "wo_hi", "wo_split"))
        wo_loaded, wo_rest_loaded = [m.sem(f"wo_loaded{n}") for n in range(2)], m.sem("wo_rest_loaded")
        x_loaded = [m.sem(f"x_loaded{n}") for n in range(2)]
        q_stored = [m.sem(f"q_stored{n}") for n in range(2)]
        x_counted, x_moments, x_shifted, x_scaled = (m.sem(n) for n in ("x_counted", "x_moments", "x_shifted", "x_scaled"))
        xn_done, x_turned, x_hi, x_split = (m.sem(n) for n in ("xn_done", "x_turned", "x_hi", "x_split"))
        q_ready, squared, ssq_done, eps_done, rq_done = (m.sem(n) for n in ("q_ready", "squared", "ssq_done", "eps_done", "rq_done"))
        qn_done, q_turned, q_copied = m.sem("qn_done"), m.sem("q_turned"), m.sem("q_copied")
        block = m.block()

        wo_raw = w_raw[:, :, :].rearrange("p c n -> p (c n)").rearrange("p (h n) -> p h n", h=H)

        @block.sync
        def _(sp):
            def load_x(b, p, half):
                sp.dma_start(xin[:, p, :], io["x2"].rearrange("b s d -> (b s) d").rearrange("(t p) d -> t p d", p=P)[b, :, :]).then_inc(x_loaded[p], 16)

            def head(cur):
                load_x(*cur)
                wq = io["Wq"].rearrange("(c p) n -> p c n", p=P)
                for n in range(G):
                    cols = slice(n * D, (n + 1) * D)
                    sp.dma_start(w_raw[:, :, cols], wq[:, :, cols]).then_inc(w_loaded[n], 16)

            def body(before, cur, after):
                if after:
                    if before:
                        sp.wait_ge(xn_done, before[0] + 1)
                    load_x(*after)
                if cur and not before:
                    sp.wait_ge(w_split, G)
                wo_heads = io["Wo"].rearrange("(h p) n -> p h n", p=P)
                if cur:
                    if before:
                        sp.wait_ge(wo_split, before[0] + 1)
                    sp.dma_start(wo_raw[:, cur[0], :], wo_heads[:, cur[0], :]).then_inc(wo_loaded[cur[1]], 16)
                if cur and not after:
                    sp.dma_start(wo_raw[:, TILES:H, :], wo_heads[:, TILES:H, :]).then_inc(wo_rest_loaded, 16)
                if before:
                    b, p, half = before
                    sp.wait_ge(q_copied, G * b + G + 2)
                    sp.dma_start(io["q1"][:, :, bass.ds(b * P, P)], qT[:, p, :, :]).then_inc(q_stored[p], 16)

            batches(sp, head, body, TILES)
            for p in range(2):
                sp.wait_ge(q_stored[p], 16 * (TILES // 2) + 16)

        @block.gpsimd
        def _(pool):
            def deviations(b, p, half):
                pool.wait_ge(x_moments, b + 1)
                pool.tensor_tensor(x_ve[:, p:p + 1], x_mv[:, p, 1:2], keep["ln_eps"][:, :], ALU.add).then_inc(x_shifted, 1)
                pool.wait_ge(x_shifted, b + 1)
                pool.tensor_tensor(x_rstd[:, p:p + 1], x_ve[:, p:p + 1], keep["neghalf"][:, 0:1], ALU.pow).then_inc(x_scaled, 1)

            def body(before, cur, after):
                if after:
                    deviations(*after)
                for n in range(G if cur else 0):
                    t = G * cur[0] + n + 1
                    pool.wait_ge(ssq_done, t + 1)
                    pool.tensor_tensor(ssq_eps[:, n % 2, :], ssq[:, n % 2, :], keep["rms_eps"][:, :], ALU.add).then_inc(eps_done, 1)
                    pool.wait_ge(eps_done, t)
                    pool.tensor_tensor(rq[:, n % 2, :], ssq_eps[:, n % 2, :], keep["neghalf"][:, 0:G], ALU.pow).then_inc(rq_done, 1)

            batches(pool, lambda cur: deviations(*cur), body, TILES)

        @block.scalar
        def _(act):
            act.sem_inc(q_copied, 2)

            def weights_hi(n):
                act.wait_ge(w_loaded[n], 16)
                cols = slice(n * D, (n + 1) * D)
                act.activation(w[0][:, :, cols], w_raw[:, :, cols], ACT.Copy).then_inc(w_hi, 1)

            def head(cur):
                b, p, half = cur
                act.wait_ge(x_turned, b + 1)
                act.activation(xT[0][:, p, :, :], x_bank[:, 0:DC * P].rearrange("p (c s) -> p c s", c=DC), ACT.Copy).then_inc(x_hi, 1)

            def copy_queries(b, p, half, n):
                t = G * b + n + 1
                act.wait_ge(q_turned, t + 2)
                act.wait_ge(q_stored[p], 16 * half + 16)
                act.activation(qT[:, p, G * n:G * n + G, :], t_bank[n % 2][:, 0:G * P].rearrange("p (h s) -> p h s", h=G),
                               ACT.Copy).then_inc(q_copied, 1)

            def body(before, cur, after):
                if cur and not before:
                    weights_hi(0)
                for n in range(G):
                    if cur and not before and n + 1 < G:
                        weights_hi(n + 1)
                    if cur:
                        act.wait_ge(q_ready, G * cur[0] + n + 1)
                        act.wait_ge(ssq_done, G * cur[0] + n + 1)
                        act.activation(squares[:, :], q_bank[n][:, :], ACT.Square, scale=float(XHD) ** -0.5).then_inc(squared, 1)
                    if n == SPLIT_WO and before:
                        h, p, half = before
                        act.wait_ge(wo_loaded[p], 16 * half + 16)
                        act.activation(wo[0][:, h, :], wo_raw[:, h, :], ACT.Copy).then_inc(wo_hi, 1)
                        if not cur:
                            act.wait_ge(wo_rest_loaded, 16)
                            act.activation(wo[0][:, TILES:H, :], wo_raw[:, TILES:H, :], ACT.Copy).then_inc(wo_hi, 1)
                    late = cur if n >= LAG else before
                    if late:
                        copy_queries(*late, (n - LAG) % G)
                    if n == TURN_X and after:
                        head(after)

            batches(act, head, body, TILES)

        @block.vector
        def _(dve):
            for signal, credit in ((qn_done, G), (x_split, 1), (ssq_done, 1), (wo_split, 1)):
                dve.sem_inc(signal, credit)
            for n in range(2):
                dve.sem_inc(q_stored[n], 16)

            def moments(b, p, half):
                dve.wait_ge(x_loaded[p], 16 * half + 16)
                dve.bn_stats(x_bn[:, p, :], xin[:, p, :]).then_inc(x_counted, 1)
                tile = b + 1
                if not isinstance(tile, int):
                    tile = dve.to_reg(tile)
                    dve.wait_ge(w_loaded[0], 16)
                dve.wait_ge(x_counted, tile)
                dve.bn_aggr(x_mv[:, p, :], x_bn[:, p, :]).then_inc(x_moments, 1)

            def normalize(b, p, half):
                dve.wait_ge(x_scaled, b + 1)
                dve.tensor_scalar(xn[:, :], xin[:, p, :], x_mv[:, p, 0:1], x_rstd[:, p:p + 1],
                                  ALU.subtract, ALU.mult).then_inc(xn_done, 1)

            def x_lo(b, p, half):
                dve.wait_ge(x_hi, b + 1)
                dve.tensor_tensor(xT[1][:, p, :, :], x_bank[:, 0:DC * P].rearrange("p (c s) -> p c s", c=DC),
                                  f32(xT[0][:, p, :, :]), ALU.subtract).then_inc(x_split, 1)

            def head(cur):
                moments(*cur)
                normalize(*cur)
                x_lo(*cur)

            def weights_lo(n):
                dve.wait_ge(w_hi, n + 1)
                cols = slice(n * D, (n + 1) * D)
                dve.tensor_tensor(w[1][:, :, cols], w_raw[:, :, cols], f32(w[0][:, :, cols]), ALU.subtract).then_inc(w_split, 1)

            def sum_squares(b, n):
                t = G * b + n + 1
                dve.wait_ge(squared, t)
                dve.tensor_reduce(ssq[:, n % 2, :], squares[:, :].rearrange("p (h d) -> p h d", h=G), axis=AX.X, op=ALU.add).then_inc(ssq_done, 1)

            def scale(b, n):
                t = G * b + n + 1
                dve.wait_ge(rq_done, t)
                dve.wait_ge(q_turned, t)
                dve.tensor_tensor(qn[:, n % 2, :].rearrange("p (h d) -> p h d", h=G), q_bank[n][:, :].rearrange("p (h d) -> p h d", h=G),
                                  rq[:, n % 2, :].unsqueeze(2).broadcast_to([P, G, XHD]), ALU.mult).then_inc(qn_done, 1)

            def body(before, cur, after):
                if cur and not before:
                    weights_lo(0)
                for n in range(G):
                    if cur and not before and n + 1 < G:
                        weights_lo(n + 1)
                    if n == 0 and after:
                        moments(*after)
                    if cur:
                        sum_squares(cur[0], n)
                    if n == 0 and after:
                        normalize(*after)
                    if cur:
                        scale(cur[0], n)
                    if n == SPLIT_WO and before:
                        h = before[0]
                        dve.wait_ge(wo_hi, h + 1)
                        dve.tensor_tensor(wo[1][:, h, :], wo_raw[:, h, :], f32(wo[0][:, h, :]), ALU.subtract).then_inc(wo_split, 1)
                        if not cur:
                            dve.wait_ge(wo_hi, TILES + 1)
                            dve.tensor_tensor(wo[1][:, TILES:H, :], wo_raw[:, TILES:H, :], f32(wo[0][:, TILES:H, :]), ALU.subtract).then_inc(wo_split, 1)
                    if n == TURN_X and after:
                        x_lo(*after)

            batches(dve, head, body, TILES)

        @block.tensor
        def _(pe):
            pe.sem_inc(q_turned, 2)
            ident = keep["ident"]

            def head(cur):
                b = cur[0]
                pe.wait_ge(xn_done, b + 1)
                pe.wait_ge(x_split, b + 1)
                for c in range(DC):
                    last = pe.transpose(x_bank[:, c * P:(c + 1) * P], xn[:, c * P:(c + 1) * P], ident[:, :])
                last.then_inc(x_turned, 1)

            def project(b, p, n):
                if n == 0:
                    pe.wait_ge(x_split, b + 1 + 1)
                pe.wait_ge(qn_done, G * b + n + 1)
                for k, (s, r) in enumerate(PASSES):
                    for c in range(DC):
                        last = pe.matmul(q_bank[n][:, :], xT[s][:, p, c, :], w[r][:, c, n * D:(n + 1) * D],
                                         start=k == 0 and c == 0, stop=k == len(PASSES) - 1 and c == DC - 1)
                last.then_inc(q_ready, 1)

            def turn(b, n):
                t = G * b + n + 1
                pe.wait_ge(qn_done, t + G)
                pe.wait_ge(q_copied, t)
                for h in range(G):
                    last = pe.transpose(t_bank[n % 2][:, h * P:(h + 1) * P], qn[:, n % 2, h * P:(h + 1) * P], ident[:, :])
                last.then_inc(q_turned, 1)

            def body(before, cur, after):
                for n in range(G):
                    if cur and not before:
                        pe.wait_ge(w_split, n + 1)
                    if cur:
                        project(cur[0], cur[1], n)
                    late = cur if n >= LAG else before
                    if late:
                        turn(late[0], (n - LAG) % G)
                    if n == TURN_X and after:
                        head(after)

            batches(pe, head, body, TILES)


def phase_c_attention(nc, keep, io, wo):
    AHEAD = 4
    EXPS = 3
    RECIPROCAL = 2
    WEIGH = {2: -1, 6: 0, 10: 1, 14: 2}
    SPLIT_OUT = {3: -1, 7: 0, 11: 1, 15: 2}
    PROJECT = {0: -2, 4: -1, 8: 0, 12: 1}
    FINISH = 6
    SPLIT_K = {4: 0, 8: 1, 10: 2, 13: 3}
    SPLIT_Q = {7: 0, 9: 1, 12: 2, 14: 3}
    SPLIT_V, SPLIT_V_LOW = {8: 0, 10: 1, 12: 2}, {11: 0, 13: 1, 15: 2}
    with Memory(nc, "c") as m:
        q_raw = m.sb("q_raw", [P, H, S])
        k_raw = m.sb("k_raw", [P, G, TE])
        v_raw = m.sb("v_raw", [KP, KC, D])
        q = [m.sb(f"q_{n}", [P, 2, H, S], F32R) for n in ("hi", "lo")]
        k = [m.sb(f"k_{n}", [P, 2, G, TE], F32R) for n in ("hi", "lo")]
        v = [m.sb(f"v_{n}", [KP, 2, KC, D], F32R) for n in ("hi", "lo")]
        xin = m.sb("xin", [S, 2, D])
        xout = m.sb("xout", [S, 2, D])
        probs = m.sb("probs", [S, AHEAD, T])
        pT = [m.sb(f"pT_{n}", [KP, 2, KC, HPG, S], F32R) for n in ("hi", "lo")]
        oT = [m.sb(f"oT_{n}", [P, 2, HPG, S], F32R) for n in ("hi", "lo")]
        nmax = m.sb("nmax", [S, 2, H])
        sums = m.sb("sums", [S, 2, H])
        rsum = m.sb("rsum", [S, 2, H])
        score = [m.ps(f"score{n}", [P, 512]) for n in range(AHEAD)]
        turned = [m.ps(f"turned{n}", [P, 512]) for n in range(2)]
        outp = m.ps("outp", [P, 512])
        y = m.ps("y", [P, 512])
        q_loaded, k_loaded, v_loaded = m.sem("q_loaded"), m.sem("k_loaded"), m.sem("v_loaded")
        x_loaded = [m.sem(f"x_loaded{n}") for n in range(2)]
        x_stored = [m.sem(f"x_stored{n}") for n in range(2)]
        q_hi, q_split, k_hi, k_split, v_hi, v_split = (m.sem(n) for n in ("q_hi", "q_split", "k_hi", "k_split", "v_hi", "v_split"))
        scores_ready, max_done, probs_ready, rsum_done, scaled = (m.sem(n) for n in ("scores_ready", "max_done", "probs_ready", "rsum_done", "scaled"))
        turned_ready, pT_hi, pT_split = m.sem("turned_ready"), m.sem("pT_hi"), m.sem("pT_split")
        out_ready, o_hi, o_split, y_ready, x_done = (m.sem(n) for n in ("out_ready", "o_hi", "o_split", "y_ready", "x_done"))
        norm = norm_semaphores(m)
        block = m.block()

        def group(slots, h, before, cur):
            if h not in slots:
                return None
            which = before if slots[h] < 0 else cur
            return which and (*which, slots[h] % G)

        @block.sync
        def _(sp):
            def load(b, p, half):
                sp.dma_start(q_raw[:, :, :], io["q1"][:, :, bass.ds(b * S, S)]).then_inc(q_loaded, 16)
                sp.dma_start(k_raw[:, :, :], io["k1"][b, :, :, :]).then_inc(k_loaded, 16)

                sp.dma_start(v_raw[:, :, :], io["v1"][b, :, :, :]).then_inc(v_loaded, 16)

            def load_x(b, p, half):
                sp.dma_start(xin[:, p, :], io["x2"][b, :, :]).then_inc(x_loaded[p], 16)

            def head(cur):
                load(*cur)
                load_x(*cur)

            def body(before, cur, after):
                if after:
                    sp.wait_ge(q_split, G * cur[0] + G)
                    sp.wait_ge(k_split, G * cur[0] + G)
                    sp.wait_ge(v_split, KC * cur[0] + KC)
                    load(*after)
                if before:
                    b, p, half = before
                    sp.wait_ge(x_done, b + 1 + 1)
                    sp.dma_start(io["x3"][b, :, :], xout[:, p, :]).then_inc(x_stored[p], 16)
                if after:
                    load_x(*after)

            batches(sp, head, body)
            for p in range(2):
                sp.wait_ge(x_stored[p], 16 * (B // 2) + 16)

        @block.gpsimd
        def _(pool):
            def scale(b, p, h):
                pool.wait_ge(rsum_done, H * b + h + 1)
                pool.tensor_tensor(probs[:, h % AHEAD, :], probs[:, h % AHEAD, :], rsum[:, p, h:h + 1].broadcast_to([S, T]),
                                   ALU.mult).then_inc(scaled, 1)

            def values_lo(b, p, c):
                pool.wait_ge(v_hi, KC * b + c + 1)
                pool.tensor_tensor(v[1][:, p, c, :], v_raw[:, c, :], f32(v[0][:, p, c, :]), ALU.subtract).then_inc(v_split, 1)

            def head(cur):
                for c in range(KC):
                    values_lo(cur[0], cur[1], c)

            def body(before, cur, after):
                for h in range(H if cur else 0):
                    scale(cur[0], cur[1], h)
                    if h in SPLIT_V_LOW and after:
                        values_lo(after[0], after[1], SPLIT_V_LOW[h])
                norm_early(norm_rstd, pool, keep, norm, cur)

            batches(pool, head, body)
            norm_rstd(pool, keep, norm, NORM_EARLY, B)

        @block.scalar
        def _(act):
            act.sem_inc(probs_ready, AHEAD)

            def queries_hi(b, p, g):
                act.wait_ge(q_loaded, 16 * b + 16)
                act.activation(q[0][:, p, HPG * g:HPG * g + HPG, :], q_raw[:, HPG * g:HPG * g + HPG, :], ACT.Copy).then_inc(q_hi, 1)

            def keys_hi(b, p, g):
                act.wait_ge(k_loaded, 16 * b + 16)
                act.activation(k[0][:, p, g, :], k_raw[:, g, :], ACT.Copy).then_inc(k_hi, 1)

            def values_hi(b, p, c):
                act.wait_ge(v_loaded, 16 * b + 16)
                act.activation(v[0][:, p, c, :], v_raw[:, c, :], ACT.Copy).then_inc(v_hi, 1)

            def head(cur):
                for g in range(G):
                    keys_hi(cur[0], cur[1], g)
                    queries_hi(cur[0], cur[1], g)
                for c in range(KC):
                    values_hi(cur[0], cur[1], c)

            def exps(b, p, h):
                act.wait_ge(max_done, H * b + h + 1)
                act.wait_ge(turned_ready, H * b + h + 1)
                act.activation(probs[:, h % AHEAD, :], score[h % AHEAD][0:S, 0:T], ACT.Exp, bias=nmax[:, p, h:h + 1],
                               accum_out=sums[:, p, h:h + 1]).then_inc(probs_ready, 1)

            def probs_hi(b, h):
                g, j = divmod(h, HPG)
                act.wait_ge(turned_ready, H * b + h + 1 + AHEAD)
                src = turned[h % 2][0:KP, 0:KC * S].rearrange("p (c s) -> p c s", c=KC)
                act.activation(pT[0][:, g % 2, :, j, :], src, ACT.Copy).then_inc(pT_hi, 1)

            def out_hi(b, p, half, g):
                act.wait_ge(out_ready, G * b + g + 1)
                act.activation(oT[0][:, g % 2, :, :], outp[:, 0:HPG * S].rearrange("p (j s) -> p j s", j=HPG), ACT.Copy).then_inc(o_hi, 1)

            def body(before, cur, after):
                if cur and not before:
                    for h in range(EXPS):
                        exps(cur[0], cur[1], h)
                for h in range(H):
                    if h in SPLIT_V and after:
                        values_hi(after[0], after[1], SPLIT_V[h])
                    if h in SPLIT_Q and after:
                        queries_hi(after[0], after[1], SPLIT_Q[h])
                    done = group(SPLIT_OUT, h, before, cur)
                    if done:
                        out_hi(*done)
                    if cur:
                        probs_hi(cur[0], h)
                    if cur and h + EXPS < H:
                        exps(cur[0], cur[1], h + EXPS)
                    elif after and h + EXPS >= H:
                        exps(after[0], after[1], h + EXPS - H)
                    if h in SPLIT_K and after:
                        keys_hi(after[0], after[1], SPLIT_K[h])

            batches(act, head, body)

        @block.vector
        def _(dve):
            for signal, credit in ((pT_split, 2), (o_split, 1), (x_done, 1)):
                dve.sem_inc(signal, credit)
            for n in range(2):
                dve.sem_inc(x_stored[n], 16)

            def queries_lo(b, p, g):
                dve.wait_ge(q_hi, G * b + g + 1)
                heads = slice(HPG * g, HPG * g + HPG)
                dve.tensor_tensor(q[1][:, p, heads, :], q_raw[:, heads, :], f32(q[0][:, p, heads, :]), ALU.subtract).then_inc(q_split, 1)

            def keys_lo(b, p, g):
                dve.wait_ge(k_hi, G * b + g + 1)
                dve.tensor_tensor(k[1][:, p, g, :], k_raw[:, g, :], f32(k[0][:, p, g, :]), ALU.subtract).then_inc(k_split, 1)

            def head(cur):
                for g in range(G):
                    keys_lo(cur[0], cur[1], g)
                    queries_lo(cur[0], cur[1], g)

            def maximum(b, p, h):
                dve.wait_ge(scores_ready, H * b + h + 1)
                dve.tensor_reduce(nmax[:, p, h:h + 1], score[h % AHEAD][0:S, 0:T], axis=AX.X, op=ALU.max, negate=True).then_inc(max_done, 1)

            def reciprocal(b, p, h):
                dve.wait_ge(probs_ready, H * b + h + 1 + AHEAD)
                dve.reciprocal(rsum[:, p, h:h + 1], sums[:, p, h:h + 1]).then_inc(rsum_done, 1)

            def probs_lo(b, h):
                g, j = divmod(h, HPG)
                dve.wait_ge(pT_hi, H * b + h + 1)
                src = turned[h % 2][0:KP, 0:KC * S].rearrange("p (c s) -> p c s", c=KC)
                dve.tensor_tensor(pT[1][:, g % 2, :, j, :], src, f32(pT[0][:, g % 2, :, j, :]), ALU.subtract).then_inc(pT_split, 1)

            def out_lo(b, p, half, g):
                dve.wait_ge(o_hi, G * b + g + 1)
                dve.tensor_tensor(oT[1][:, g % 2, :, :], outp[:, 0:HPG * S].rearrange("p (j s) -> p j s", j=HPG),
                                  f32(oT[0][:, g % 2, :, :]), ALU.subtract).then_inc(o_split, 1)

            def finish(b, p, half):
                dve.wait_ge(y_ready, b + 1)
                dve.wait_ge(x_loaded[p], 16 * half + 16)
                dve.wait_ge(x_stored[p], 16 * half + 16)
                dve.scalar_tensor_tensor(out=xout[:, p, :], in0=y[0:S, :], scalar=keep["gates"][0:S, 1:2], in1=xin[:, p, :],
                                         op0=ALU.mult, op1=ALU.add).then_inc(x_done, 1)
                dve.wait_ge(x_done, b + 1 + 1)
                dve.bn_stats(keep["bn"][:, b, :], xout[:, p, :]).then_inc(norm["counted"], 1)

            def body(before, cur, after):
                norm_early(norm_moments, dve, keep, norm, cur)

                def ahead(what, n):
                    if n < H:
                        what(cur[0], cur[1], n)
                    elif after:
                        what(after[0], after[1], n - H)

                if cur and not before:
                    for h in range(AHEAD):
                        maximum(cur[0], cur[1], h)
                    for h in range(RECIPROCAL):
                        reciprocal(cur[0], cur[1], h)
                for h in range(H):
                    done = group(SPLIT_OUT, h, before, cur)
                    if done:
                        out_lo(*done)
                    if cur:
                        ahead(reciprocal, h + RECIPROCAL)
                        ahead(maximum, h + AHEAD)
                        probs_lo(cur[0], h)
                    if h == FINISH and before:
                        finish(*before)
                    if h in SPLIT_K and after:
                        keys_lo(after[0], after[1], SPLIT_K[h])
                    if h in SPLIT_Q and after:
                        queries_lo(after[0], after[1], SPLIT_Q[h])

            batches(dve, head, body)
            norm_moments(dve, keep, norm, NORM_EARLY, B)

        @block.tensor
        def _(pe):
            pe.sem_inc(turned_ready, AHEAD)
            ident = keep["ident"]

            def scores(b, p, h):
                if h % HPG == 0:
                    pe.wait_ge(q_split, G * b + h // HPG + 1)
                    pe.wait_ge(k_split, G * b + h // HPG + 1)
                pe.wait_ge(probs_ready, H * b + h + 1)
                for n, (s, r) in enumerate(PASSES):
                    last = pe.matmul(score[h % AHEAD][0:S, 0:TE], q[s][:, p, h, :], k[r][:, p, h // HPG, :],
                                     start=n == 0, stop=n == len(PASSES) - 1)
                last.then_inc(scores_ready, 1)

            def turn(b, h):
                pe.wait_ge(scaled, H * b + h + 1)
                pe.wait_ge(pT_split, H * b + h + 1)
                for c in range(KC):
                    last = pe.transpose(turned[h % 2][0:KP, c * S:(c + 1) * S], probs[:, h % AHEAD, c * KP:(c + 1) * KP], ident[0:S, 0:S])
                last.then_inc(turned_ready, 1)

            def weigh(b, p, half, g):
                pe.wait_ge(pT_split, H * b + HPG * (g + 1) + 2)
                pe.wait_ge(o_split, G * b + g + 1)
                if g == 0:
                    pe.wait_ge(v_split, KC * b + KC)
                for n, (s, r) in enumerate(PASSES):
                    for c in range(KC):
                        last = pe.matmul(outp[:, 0:HPG * S], v[s][:, p, c, g * P:(g + 1) * P],
                                         pT[r][:, g % 2, c, :, :].rearrange("p j s -> p (j s)"),
                                         start=n == 0 and c == 0, stop=n == len(PASSES) - 1 and c == KC - 1)
                last.then_inc(out_ready, 1)

            def project(b, p, half, g):
                pe.wait_ge(o_split, G * b + g + 1 + 1)
                if g == 0:
                    pe.wait_ge(x_done, b + 1)
                for n, (s, r) in enumerate(PASSES):
                    for j in range(HPG):
                        last = pe.matmul(y[0:S, :], oT[s][:, g % 2, j, :], wo[r][:, HPG * g + j, :],
                                         start=g == 0 and n == 0 and j == 0, stop=g == G - 1 and n == len(PASSES) - 1 and j == HPG - 1)
                if g == G - 1:
                    last.then_inc(y_ready, 1)

            def body(before, cur, after):
                if cur and not before:
                    for h in range(AHEAD):
                        scores(cur[0], cur[1], h)
                for h in range(H):
                    if cur:
                        turn(cur[0], h)
                    if cur and h + AHEAD < H:
                        scores(cur[0], cur[1], h + AHEAD)
                    elif after and h + AHEAD >= H:
                        scores(after[0], after[1], h + AHEAD - H)
                    done = group(WEIGH, h, before, cur)
                    if done:
                        weigh(*done)
                    done = group(PROJECT, h, before, cur)
                    if done:
                        project(*done)

            batches(pe, lambda cur: None, body)


def phase_d(nc, keep, io):
    with Memory(nc, "e") as outer:
        qkv = {
            "q": outer.sb("q", [P, G, B * S]),
            "k": outer.sb("k", [P, G, B * S]),
            "v": outer.sb("v", [S, B, D]),
        }
        phase_d_project(nc, keep, io, qkv)
        phase_d_attention(nc, keep, io, qkv)


def phase_d_project(nc, keep, io, qkv):
    THRESHOLD = 0.1
    CLIP = 1e-8
    QS, KS, V0, QL, KL = 0, H * DS, 2 * H * DS, 2 * H * DS + D, 2 * H * DS + D + H * R
    WIDTH = KL + H * R
    BLOCKS = 2 * G + BPG
    RAW = 3
    NEXT = 2
    with Memory(nc, "g") as m:
        raw = m.sb("raw", [P, RAW, WIDTH])
        wf = m.sb("wf", [P, 2, 2 * D])
        low = m.sb("low", [P, 2, 2, H, R])
        w = [m.sb(f"w_{n}", [P, DC, 3 * D], F32R) for n in ("hi", "lo")]
        head_raw = m.sb("head_raw", [P, 2, H])
        head_clip = m.sb("head_clip", [P, 2, H])
        head_scale = m.sb("head_scale", [P, 2, H])
        half = m.sb("half", [P, 2, H])
        swap = m.sb("swap", [P, H, R], U8)
        xn = m.sb("xn", [S, BPG, D])
        xT = [m.sb(f"xT_{n}", [P, 2, DC, GS], F32R) for n in ("hi", "lo")]
        x_bank = [m.ps(f"x_bank{n}", [P, 512]) for n in range(2)]
        out_bank = [m.ps(f"out_bank{n}", [P, 512]) for n in range(4)]
        head_loaded, clipped, scaled, swapped = (m.sem(n) for n in ("head_loaded", "clipped", "scaled", "swapped"))
        w_loaded = [m.sem(f"w_loaded{n}") for n in range(DC)]
        low_done, w_done, w_chosen, w_hi, w_split = (m.sem(n) for n in ("low_done", "w_done", "w_chosen", "w_hi", "w_split"))
        x_loaded, xn_done, x_turned, x_hi, x_split = (m.sem(n) for n in ("x_loaded", "xn_done", "x_turned", "x_hi", "x_split"))
        ready, copied = m.sem("ready"), [m.sem(f"copied{n}") for n in range(2)]
        block = m.block()

        def groups(eng, head, body):
            head((0, 0))
            body((0, 0), (1, 1))
            with eng.Fori(0, NG // 2 - 1) as i:
                body((2 * i + 1, 1), (2 * i + 2, 0))
                body((2 * i + 2, 0), (2 * i + 3, 1))
            body((NG - 1, 1), None)

        @block.sync
        def _(sp):
            for n, name in enumerate(("w_std", "w_rec")):
                with nc.allow_non_contiguous_dma(reason="a few words"):
                    sp.dma_start(head_raw[:, n, :], io[name].rearrange("(a n) -> a n", a=1).broadcast_to([P, H])).then_inc(head_loaded, 16)

            def head(cur):
                sp.wait_ge(x_turned, DC * cur[0] + 1)
                first = BPG * cur[0]
                sp.dma_start(xn[:, :, :], io["x3"][bass.ds(first, BPG), :, :].rearrange("b s d -> s b d")).then_inc(x_loaded, 16)
                if isinstance(cur[0], int) and cur[0] == 0:
                    for c in range(DC):
                        if c >= RAW:
                            sp.wait_ge(w_split, c - RAW + 1)
                        sp.dma_start(raw[:, c % RAW, :], io["Wa"].rearrange("(c p) n -> c p n", p=P)[c, :, :]).then_inc(w_loaded[c], 16)

            groups(sp, head, lambda cur, after: after and head(after))

        @block.gpsimd
        def _(pool):
            pool.memset(half[:, :, :], 0.5).then_inc(clipped, 1)
            pool.wait_ge(clipped, 2)
            pool.tensor_tensor(head_scale[:, :, :], head_clip[:, :, :], half[:, :, :], ALU.pow).then_inc(scaled, 1)

        def columns(c, n, width):
            return wf[:, c % 2, n * D:(n + 1) * D].rearrange("p (h d) -> p h d", h=H)[:, :, width]

        @block.scalar
        def _(act):
            act.sem_inc(copied[0], 2)

            def x_hi_chunk(cur, c):
                act.wait_ge(x_turned, DC * cur[0] + c + 1 + 1)
                act.activation(xT[0][:, cur[1], c, :], x_bank[c % 2][:, 0:GS], ACT.Copy).then_inc(x_hi, 1)

            for c in range(DC):
                act.wait_ge(w_loaded[c], 16)
                act.activation(w[0][:, c, 2 * D:], raw[:, c % RAW, V0:V0 + D], ACT.Copy).then_inc(w_hi, 1)
                act.wait_ge(w_chosen, 2 * c + 2)
                act.activation(w[0][:, c, 0:2 * D], wf[:, c % 2, :], ACT.Copy).then_inc(w_hi, 1)
                x_hi_chunk((0, 0), c)

            def head(cur):
                for c in range(DC):
                    x_hi_chunk(cur, c)

            def body(cur, after):
                g = cur[0]
                for n in range(0, BLOCKS, 2):
                    act.wait_ge(ready, BLOCKS * g + n + 1)
                    if n < G:
                        act.activation(qkv["q"][:, n, bass.ds(g * GS, GS)], out_bank[n % 4][:, 0:GS], ACT.Copy,
                                       scale=float(HD) ** -0.5).then_inc(copied[0], 1)
                    elif n < 2 * G:
                        act.activation(qkv["k"][:, n - G, bass.ds(g * GS, GS)], out_bank[n % 4][:, 0:GS], ACT.Copy).then_inc(copied[0], 1)
                    else:
                        act.activation(qkv["v"][:, BPG * g + n - 2 * G, :], out_bank[n % 4][0:S, :], ACT.Copy).then_inc(copied[0], 1)
                    if n == NEXT and after:
                        head(after)

            groups(act, lambda cur: None, body)

        @block.vector
        def _(dve):
            dve.sem_inc(copied[1], 2)
            dve.sem_inc(x_split, 2)
            dve.wait_ge(head_loaded, 32)
            dve.tensor_scalar(head_clip[:, :, :], head_raw[:, :, :], CLIP, None, ALU.max).then_inc(clipped, 1)
            dve.tensor_scalar(swap[:, :, :], head_raw[:, 1, :].unsqueeze(2).broadcast_to([P, H, R]), THRESHOLD, None, ALU.is_gt).then_inc(swapped, 1)

            def normalize(cur):
                g = cur[0]
                dve.wait_ge(x_loaded, 16 * g + 16)
                for n in range(BPG):
                    b = BPG * g + n
                    last = dve.tensor_scalar(xn[:, n, :], xn[:, n, :], keep["mv"][:, b, 0:1], keep["rstd"][:, b, :],
                                             ALU.subtract, ALU.mult)
                last.then_inc(xn_done, 1)

            def x_lo(cur, c):
                dve.wait_ge(x_hi, DC * cur[0] + c + 1)
                dve.tensor_tensor(xT[1][:, cur[1], c, :], x_bank[c % 2][:, 0:GS], f32(xT[0][:, cur[1], c, :]), ALU.subtract).then_inc(x_split, 1)

            def head(cur):
                normalize(cur)
                for c in range(DC):
                    x_lo(cur, c)

            def order_weights(c):
                dve.wait_ge(scaled, 1)
                dve.wait_ge(w_loaded[c], 16)
                for n, first in enumerate((QL, KL)):
                    dve.tensor_tensor(low[:, c % 2, n, :, :], raw[:, c % RAW, first:first + H * R].rearrange("p (h r) -> p h r", h=H),
                                      head_scale[:, 1, :].unsqueeze(2).broadcast_to([P, H, R]), ALU.mult).then_inc(low_done, 1)
                if c > 1:
                    dve.wait_ge(w_split, c - 1)
                for n, first in enumerate((QS, KS)):
                    dve.tensor_tensor(columns(c, n, slice(0, DS)), raw[:, c % RAW, first:first + H * DS].rearrange("p (h d) -> p h d", h=H),
                                      head_scale[:, 0, :].unsqueeze(2).broadcast_to([P, H, DS]), ALU.mult)
                dve.wait_ge(low_done, 2 * c + 2)
                for n in range(2):
                    dve.tensor_copy(columns(c, n, slice(DS, HD)), low[:, c % 2, n, :, :]).then_inc(w_done, 1)
                dve.wait_ge(w_done, 2 * c + 2)
                dve.wait_ge(swapped, 1)
                for n in range(2):
                    dve.copy_predicated(columns(c, n, slice(DS, HD)), swap[:, :, :], low[:, c % 2, 1 - n, :, :]).then_inc(w_chosen, 1)

            def weights_lo(c):
                dve.wait_ge(w_hi, 2 * c + 2)
                dve.tensor_tensor(w[1][:, c, 0:2 * D], wf[:, c % 2, :], f32(w[0][:, c, 0:2 * D]), ALU.subtract)
                dve.tensor_tensor(w[1][:, c, 2 * D:], raw[:, c % RAW, V0:V0 + D], f32(w[0][:, c, 2 * D:]), ALU.subtract).then_inc(w_split, 1)

            def weights():
                normalize((0, 0))
                order_weights(0)
                for c in range(DC):
                    if c + 1 < DC:
                        order_weights(c + 1)
                    weights_lo(c)
                    x_lo((0, 0), c)

            def body(cur, after):
                g = cur[0]
                for n in range(1, BLOCKS, 2):
                    dve.wait_ge(ready, BLOCKS * g + n + 1)
                    if n < G:
                        dve.tensor_scalar(qkv["q"][:, n, bass.ds(g * GS, GS)], out_bank[n % 4][:, 0:GS], float(HD) ** -0.5, None,
                                          ALU.mult).then_inc(copied[1], 1)
                    elif n < 2 * G:
                        dve.tensor_copy(qkv["k"][:, n - G, bass.ds(g * GS, GS)], out_bank[n % 4][:, 0:GS]).then_inc(copied[1], 1)
                    else:
                        dve.tensor_copy(qkv["v"][:, BPG * g + n - 2 * G, :], out_bank[n % 4][0:S, :]).then_inc(copied[1], 1)
                    if n == NEXT - 1 and after:
                        head(after)

            weights()
            groups(dve, lambda cur: None, body)

        @block.tensor
        def _(pe):
            pe.sem_inc(x_turned, 1)
            ident = keep["ident"]

            def head(cur):
                g = cur[0]
                pe.wait_ge(xn_done, g + 1)
                for c in range(DC):
                    pe.wait_ge(x_split, DC * g + c + 1)
                    for n in range(BPG):
                        last = pe.transpose(x_bank[c % 2][:, n * S:(n + 1) * S], xn[:, n, c * P:(c + 1) * P], ident[0:S, 0:S])
                    last.then_inc(x_turned, 1)

            def body(cur, after):
                g, p = cur
                if isinstance(g, int) and g == 0:
                    pe.wait_ge(w_split, DC)
                pe.wait_ge(x_split, DC * g + DC + 2)
                for n in range(BLOCKS):
                    pe.wait_ge(copied[n % 2], BLOCKS // 2 * g + n // 2 + 1)
                    for k, (s, r) in enumerate(PASSES):
                        for c in range(DC):
                            flags = dict(start=k == 0 and c == 0, stop=k == len(PASSES) - 1 and c == DC - 1)
                            if n < 2 * G:
                                last = pe.matmul(out_bank[n % 4][:, 0:GS], w[s][:, c, n * P:(n + 1) * P], xT[r][:, p, c, :], **flags)
                            else:
                                b = n - 2 * G
                                last = pe.matmul(out_bank[n % 4][0:S, :], xT[s][:, p, c, b * S:(b + 1) * S], w[r][:, c, 2 * D:], **flags)
                    last.then_inc(ready, 1)
                    if n == NEXT and after:
                        head(after)

            groups(pe, head, body)


def phase_d_attention(nc, keep, io, qkv):
    AHEAD = 4
    EXPS = 2
    RECIPROCAL = 3
    NORMALIZE, TURN_OUT, SPLIT_OUT, PROJECT, FINISH = 1, 2, 2, 3, 3
    LOWEST = -3.4028234663852886e38
    SPLIT_Q, SPLIT_K = 2, {1: (0,), 2: (1, 2), 3: (3,)}
    with Memory(nc, "d") as m:
        wp_raw = m.sb("wp_raw", [P, DC, D])
        wp = [m.sb(f"wp_{n}", [P, DC, D], F32R) for n in ("hi", "lo")]
        lowest = m.sb("lowest", [S, S])
        q = [m.sb(f"q_{n}", [P, 2, G, S], F32R) for n in ("hi", "lo")]
        k = [m.sb(f"k_{n}", [P, 2, G, HPG, S], F32R) for n in ("hi", "lo")]
        probs = m.sb("probs", [S, G, HPG, S])
        pT = m.sb("pT", [S, 2, HPG, S])
        nmax = m.sb("nmax", [S, 2, H])
        sums = m.sb("sums", [S, 2, H])
        rsum = m.sb("rsum", [S, H])
        on = m.sb("on", [S, D])
        oT = [m.sb(f"oT_{n}", [P, DC, S], F32R) for n in ("hi", "lo")]
        xin = m.sb("xin", [S, 2, D])
        xout = m.sb("xout", [S, 2, D])
        score = [m.ps(f"score{n}", [P, 512]) for n in range(G)]
        turned = m.ps("turned", [P, 512])
        outp = [m.ps(f"outp{n}", [P, 512]) for n in range(2)]
        tail = m.ps("tail", [P, 512])
        wp_loaded, wp_hi, wp_split, cleared, cleared_hi = (m.sem(n) for n in ("wp_loaded", "wp_hi", "wp_split", "cleared", "cleared_hi"))
        x_loaded = [m.sem(f"x_loaded{n}") for n in range(2)]
        x_stored = [m.sem(f"x_stored{n}") for n in range(2)]
        q_hi, q_split, k_hi, k_split, k_first_split = (m.sem(n) for n in ("q_hi", "q_split", "k_hi", "k_split", "k_first_split"))
        scores_ready, masked, max_done, probs_ready = (m.sem(n) for n in ("scores_ready", "masked", "max_done", "probs_ready"))
        turned_ready, pT_copied, out_ready, rsum_done, on_done = (m.sem(n) for n in ("turned_ready", "pT_copied", "out_ready", "rsum_done", "on_done"))
        o_turned, o_hi, o_split, y_ready, x_done = (m.sem(n) for n in ("o_turned", "o_hi", "o_split", "y_ready", "x_done"))
        block = m.block()

        def rounds(eng, head, body):
            head((0, 0, 0))
            head((1, 1, 0))
            body(None, (0, 0, 0), (1, 1, 0), (2, 0, 1))
            with eng.Fori(0, B // 2 - 2) as i:
                body((2 * i, 0, i), (2 * i + 1, 1, i), (2 * i + 2, 0, i + 1), (2 * i + 3, 1, i + 1))
                body((2 * i + 1, 1, i), (2 * i + 2, 0, i + 1), (2 * i + 3, 1, i + 1), (2 * i + 4, 0, i + 2))
            last = B // 2 - 1
            body((B - 4, 0, last - 1), (B - 3, 1, last - 1), (B - 2, 0, last), (B - 1, 1, last))
            body((B - 3, 1, last - 1), (B - 2, 0, last), (B - 1, 1, last), None)
            body((B - 2, 0, last), (B - 1, 1, last), None, None)
            body((B - 1, 1, last), None, None, None)

        def keys_lo(eng, signal, b, p, j):
            eng.wait_ge(k_hi, HPG * b + j + 1)
            r = slice(HD * j, HD * j + HD)
            eng.tensor_tensor(k[1][r, p, :, j, :], qkv["k"][r, :, bass.ds(b * S, S)], f32(k[0][r, p, :, j, :]), ALU.subtract).then_inc(signal, 1)

        @block.sync
        def _(sp):
            sp.dma_start(wp_raw[:, :, :], io["Wp"].rearrange("(c p) n -> p c n", p=P)).then_inc(wp_loaded, 16)

            def load(b, p, half):
                sp.dma_start(xin[:, p, :], io["x3"][b, :, :]).then_inc(x_loaded[p], 16)

            def body(before, cur, after, further):
                if before:
                    b, p, half = before
                    sp.wait_ge(x_done, b + 1 + 1)
                    sp.dma_start(io["out"][b, :, :], xout[:, p, :]).then_inc(x_stored[p], 16)
                if after and before:
                    load(*after)

            rounds(sp, lambda cur: load(*cur), body)
            for p in range(2):
                sp.wait_ge(x_stored[p], 16 * (B // 2) + 16)

        @block.gpsimd
        def _(pool):
            pool.memset(f32(k[1][:, :, :, :, :]), 0.0).then_inc(cleared, 1)
            pool.memset(lowest[:, :], LOWEST).then_inc(cleared, 1)
            pool.wait_ge(cleared, 2)

            def head(cur):
                for j in range(HPG if not isinstance(cur[0], int) or cur[0] > 0 else 0):
                    keys_lo(pool, k_split, cur[0], cur[1], j)

            rounds(pool, head, lambda before, cur, after, further: further and head(further))

        @block.scalar
        def _(act):
            act.sem_inc(probs_ready, G)

            def keys_hi(b, p, j):
                r = slice(HD * j, HD * j + HD)
                act.activation(k[0][r, p, :, j, :], qkv["k"][r, :, bass.ds(b * S, S)], ACT.Copy).then_inc(k_hi, 1)

            def queries_hi(b, p):
                act.activation(q[0][:, p, :, :], qkv["q"][:, :, bass.ds(b * S, S)], ACT.Copy).then_inc(q_hi, 1)

            def head(cur):
                queries_hi(cur[0], cur[1])
                act.wait_ge(cleared_hi, cur[0] + 1)
                for j in range(HPG):
                    keys_hi(cur[0], cur[1], j)

            def exps(b, p, g):
                t = G * b + g + 1
                act.wait_ge(max_done, t)
                act.wait_ge(turned_ready, t)
                for j in range(HPG):
                    h = HPG * g + j
                    last = act.activation(probs[:, g, j, :], score[g][0:S, j * S:(j + 1) * S], ACT.Exp,
                                          bias=nmax[:, p, h:h + 1], accum_out=sums[:, p, h:h + 1])
                last.then_inc(probs_ready, 1)

            def out_hi(b, p, half):
                act.wait_ge(o_turned, b + 1)
                act.activation(oT[0][:, :, :], tail[:, 0:DC * S].rearrange("p (c s) -> p c s", c=DC), ACT.Copy).then_inc(o_hi, 1)

            def body(before, cur, after, further):
                if cur and not before:
                    for g in range(EXPS):
                        exps(cur[0], cur[1], g)
                for g in range(G):
                    if cur and g + EXPS < G:
                        exps(cur[0], cur[1], g + EXPS)
                    elif after and g + EXPS >= G:
                        exps(after[0], after[1], g + EXPS - G)
                    if g == SPLIT_OUT and before:
                        out_hi(*before)
                    if g == SPLIT_Q and further:
                        queries_hi(further[0], further[1])
                    for j in SPLIT_K.get(g, ()) if further else ():
                        keys_hi(further[0], further[1], j)
                if cur and not before:
                    act.wait_ge(wp_loaded, 16)
                    act.activation(wp[0][:, :, :], wp_raw[:, :, :], ACT.Copy).then_inc(wp_hi, 1)

            rounds(act, head, body)

        @block.vector
        def _(dve):
            for signal, credit in ((on_done, 2), (x_done, 1), (pT_copied, 1)):
                dve.sem_inc(signal, credit)
            for p in range(2):
                dve.memset(f32(k[0][:, p, :, :, :]), 0.0).then_inc(cleared_hi, 1)
            for n in range(2):
                dve.sem_inc(x_stored[n], 16)

            def queries_lo(b, p):
                dve.wait_ge(q_hi, b + 1)
                dve.tensor_tensor(q[1][:, p, :, :], qkv["q"][:, :, bass.ds(b * S, S)], f32(q[0][:, p, :, :]), ALU.subtract).then_inc(q_split, 1)

            def maximum(b, p, g):
                t = G * b + g + 1
                four = score[g][0:S, 0:HPG * S].rearrange("p (j s) -> p j s", j=HPG)
                t = t if isinstance(t, int) else dve.to_reg(t)
                dve.wait_ge(cleared, 2)
                dve.wait_ge(scores_ready, t)
                dve.copy_predicated(four, keep["later"][:, :].unsqueeze(1).broadcast_to([S, HPG, S]),
                                    lowest[:, :].unsqueeze(1).broadcast_to([S, HPG, S])).then_inc(masked, 1)
                dve.wait_ge(masked, G * b + g + 1)
                dve.tensor_reduce(nmax[:, p, HPG * g:HPG * g + HPG], four, axis=AX.X, op=ALU.max, negate=True).then_inc(max_done, 1)

            def probs_copy(b, g):
                t = G * b + g + 1
                dve.wait_ge(turned_ready, t + G)
                dve.tensor_copy(pT[:, g % 2, :, :], turned[0:S, 0:HPG * S].rearrange("p (j s) -> p j s", j=HPG)).then_inc(pT_copied, 1)

            def reciprocals(b, p):
                dve.wait_ge(probs_ready, G * b + G + G)
                dve.reciprocal(rsum[:, :], sums[:, p, :]).then_inc(rsum_done, 1)

            def normalize_out(b, p, half):
                dve.wait_ge(out_ready, b + 1)
                dve.wait_ge(rsum_done, b + 1)
                dve.tensor_tensor(on[:, :].rearrange("p (h d) -> p h d", h=H), outp[p][0:S, :].rearrange("p (h d) -> p h d", h=H),
                                  rsum[:, :].unsqueeze(2).broadcast_to([S, H, HD]), ALU.mult).then_inc(on_done, 1)

            def out_lo(b, p, half):
                dve.wait_ge(o_hi, b + 1)
                dve.tensor_tensor(oT[1][:, :, :], tail[:, 0:DC * S].rearrange("p (c s) -> p c s", c=DC), f32(oT[0][:, :, :]),
                                  ALU.subtract).then_inc(o_split, 1)

            def finish(b, p, half):
                dve.wait_ge(y_ready, b + 1)
                dve.wait_ge(x_loaded[p], 16 * half + 16)
                dve.wait_ge(x_stored[p], 16 * half + 16)
                dve.scalar_tensor_tensor(out=xout[:, p, :], in0=tail[0:S, :], scalar=keep["gates"][0:S, 3:4], in1=xin[:, p, :],
                                         op0=ALU.mult, op1=ALU.add).then_inc(x_done, 1)

            def body(before, cur, after, further):
                if cur and not before:
                    for g in range(AHEAD):
                        maximum(cur[0], cur[1], g)
                for g in range(G):
                    if cur:
                        probs_copy(cur[0], g)
                    if g == NORMALIZE and before:
                        normalize_out(*before)
                    if cur and g + AHEAD < G:
                        maximum(cur[0], cur[1], g + AHEAD)
                    elif after and g + AHEAD >= G:
                        maximum(after[0], after[1], g + AHEAD - G)
                    if g == SPLIT_OUT and before:
                        out_lo(*before)
                    if g == RECIPROCAL and cur:
                        reciprocals(cur[0], cur[1])
                    if g == FINISH and before:
                        finish(*before)
                    if g == SPLIT_Q and further:
                        queries_lo(further[0], further[1])
                if cur and not before:
                    dve.wait_ge(wp_hi, 1)
                    dve.tensor_tensor(wp[1][:, :, :], wp_raw[:, :, :], f32(wp[0][:, :, :]), ALU.subtract).then_inc(wp_split, 1)

            def head(cur):
                queries_lo(cur[0], cur[1])
                if cur[0] == 0:
                    dve.wait_ge(cleared, 2)
                    for j in range(HPG):
                        keys_lo(dve, k_first_split, cur[0], cur[1], j)

            rounds(dve, head, body)

        @block.tensor
        def _(pe):
            pe.sem_inc(turned_ready, G)
            ident = keep["ident"]

            def scores(b, p, g):
                if g == 0:
                    pe.wait_ge(q_split, b + 1)
                    if isinstance(b, int) and b == 0:
                        pe.wait_ge(k_first_split, HPG)
                    else:
                        pe.wait_ge(k_split, HPG * b)
                pe.wait_ge(probs_ready, G * b + g + 1)
                for n, (s, r) in enumerate(PASSES):
                    last = pe.matmul(score[g][0:S, 0:HPG * S], q[s][:, p, g, :], k[r][:, p, g, :, :].rearrange("p j s -> p (j s)"),
                                     start=n == 0, stop=n == len(PASSES) - 1)
                last.then_inc(scores_ready, 1)

            def turn(b, g):
                t = G * b + g + 1
                pe.wait_ge(probs_ready, t + G)
                pe.wait_ge(pT_copied, t)
                for j in range(HPG):
                    last = pe.transpose(turned[0:S, j * S:(j + 1) * S], probs[:, g, j, :], ident[0:S, 0:S])
                last.then_inc(turned_ready, 1)

            def weigh(b, p, g):
                pe.wait_ge(pT_copied, G * b + g + 1 + 1)
                if g == 0:
                    pe.wait_ge(on_done, b + 1)
                for j in range(HPG):
                    h = HPG * g + j
                    last = pe.matmul(outp[p][0:S, h * HD:(h + 1) * HD], pT[:, g % 2, j, :], qkv["v"][:, b, h * HD:(h + 1) * HD],
                                     start=True, stop=True)
                if g == G - 1:
                    last.then_inc(out_ready, 1)

            def turn_out(b):
                pe.wait_ge(on_done, b + 1 + 2)
                pe.wait_ge(x_done, b + 1)
                for c in range(DC):
                    last = pe.transpose(tail[:, c * S:(c + 1) * S], on[:, c * P:(c + 1) * P], ident[0:S, 0:S])
                last.then_inc(o_turned, 1)

            def project(b):
                pe.wait_ge(wp_split, 1)
                pe.wait_ge(o_split, b + 1)
                for n, (s, r) in enumerate(PASSES):
                    for c in range(DC):
                        last = pe.matmul(tail[0:S, :], oT[s][:, c, :], wp[r][:, c, :], start=n == 0 and c == 0,
                                         stop=n == len(PASSES) - 1 and c == DC - 1)
                last.then_inc(y_ready, 1)

            def body(before, cur, after, further):
                if cur and not before:
                    for g in range(AHEAD):
                        scores(cur[0], cur[1], g)
                for g in range(G):
                    if cur:
                        turn(cur[0], g)
                    if g == TURN_OUT and before:
                        turn_out(before[0])
                    if cur and g + AHEAD < G:
                        scores(cur[0], cur[1], g + AHEAD)
                    elif after and g + AHEAD >= G:
                        scores(after[0], after[1], g + AHEAD - G)
                    if g == 0 and before:
                        weigh(before[0], before[1], G - 1)
                    elif g > 0 and cur:
                        weigh(cur[0], cur[1], g - 1)
                    if g == PROJECT and before:
                        project(before[0])

            rounds(pe, lambda cur: None, body)


def flamingo_layers(nc, ins, out):
    io = dict(ins, out=out)
    for name in ("x1", "x2", "x3"):
        io[name] = nc.dram_tensor(name, [B, S, D], F32).ap()
    io["k1"] = nc.dram_tensor("k1", [B, P, G, TE], F32).ap()
    io["v1"] = nc.dram_tensor("v1", [B, KP, KC, D], F32).ap()
    io["q1"] = nc.dram_tensor("q1", [P, H, B * S], F32).ap()
    with Memory(nc, "keep") as m:
        keep = constants(m)
        setup_phase(nc, keep, io)
        phase_a(nc, keep, io)
        phase_b(nc, keep, io)
        phase_c(nc, keep, io)
        phase_d(nc, keep, io)


_INS = {"x": "x", "ctx": "ctx_2048", "g_xattn": "g_xattn", "g_ffn": "g_ffn"}
for _layer, _names in (("L0_ffn", ("SU_ug", "SU_dp", "Wscale_ug", "Wscale_dp", "W_up", "W_gate", "W_down")),
                       ("L1_xattn", ("Wq", "Wk", "Wv", "Wo", "q_norm_w", "k_norm_w")),
                       ("L1_ffn", ("Wa", "Wp", "w_std", "w_rec"))):
    for _name in _names:
        _INS[_name] = f"{_layer}_{_name}"


def kernel(**inputs):
    import numpy as _np
    import concourse.bacc as _bacc
    from concourse import mybir as _mybir
    from concourse.bass_utils import run_bass_kernel_spmd as _run

    nc = _bacc.Bacc("TRN2", target_bir_lowering=False, num_devices=1)
    arrays, ins = {}, {}
    for short, name in _INS.items():
        a = _np.ascontiguousarray(inputs[name])
        arrays[f"in_{name}_dram"] = a
        ins[short] = nc.dram_tensor(f"in_{name}_dram", a.shape, _mybir.dt.from_np(a.dtype), kind="ExternalInput").ap()
    out = nc.dram_tensor("out_0_dram", (B, S, D), F32, kind="ExternalOutput").ap()
    flamingo_layers(nc, ins, out)
    r = _run(nc, [arrays], core_ids=[0])
    return r.results[0]["out_0_dram"]
```
